# Optimizing a Trainium2 kernel written in Bass

```python
import numpy as np
import jax
import jax.numpy as jnp

def _softmax(x, axis=-1):
    return jax.nn.softmax(x, axis=axis)

def _gelu(x):
    return jax.nn.gelu(x, approximate=True)

def _silu(x):
    return jax.nn.silu(x)

def _sigmoid(x):
    return jax.nn.sigmoid(x)

def _layernorm(x, axis=-1, eps=1e-05):
    m = jnp.mean(x, axis=axis, keepdims=True)
    v = jnp.var(x, axis=axis, keepdims=True)
    return (x - m) / jnp.sqrt(v + eps)

def _scatter_add(tgt, idx, src, axis=0):
    return tgt.at[idx].add(src)

def _segment_sum(src, seg, n):
    return jax.ops.segment_sum(src, seg, n)
kernel_name = 'mk_xattn_ffn_d2_seqx_r8_9faff1'

def setup_inputs(seed: int=0):
    np.random.seed(seed)
    _w = jnp.asarray

    def _rec_inputs():
        import jax
        import jax.numpy as jnp
        _rk = jax.random.key(seed)
        x = 0.5 + 0.2887 * jax.random.normal(jax.random.fold_in(_rk, 1), (4, 256, 256), jnp.float32)
        _lenS = 256 - jax.random.randint(jax.random.fold_in(_rk, 7), (4,), 0, max(1, 256 // 4) + 1, jnp.int32)
        _lenS2 = 256 - jax.random.randint(jax.random.fold_in(_rk, 8), (4,), 0, max(1, 256 // 4) + 1, jnp.int32)
        _ctx_512P = jax.random.normal(jax.random.fold_in(_rk, 11), (4, 16, 64), jnp.float32)
        _ctx_512c = jax.random.dirichlet(jax.random.fold_in(_rk, 511), 0.3 * jnp.ones((16,), jnp.float32), (4, 256))
        _ctx_512t = jnp.einsum('bsk,bkd->bsd', _ctx_512c, _ctx_512P)
        _ctx_512t = _ctx_512t * jax.lax.rsqrt(jnp.mean(jnp.square(_ctx_512t)) + 1e-12) * 0.953939
        ctx_512 = -0.000392918 + 0.999932 * (_ctx_512t + 0.3 * jax.random.normal(jax.random.fold_in(_rk, 611), (4, 256, 64), jnp.float32))
        return (x, ctx_512)
    x, ctx_512 = _rec_inputs()

    def _L0_xattn_setup():
        import jax, jax.numpy as jnp
        import numpy as np
        B, N, D = (16, 256, 64)
        H = 4
        TOP_K_RATIO = 0.3
        key = jax.random.key(seed)
        k1, k2, k3, k4 = jax.random.split(key, 4)
        h = jax.random.normal(k1, (B, N, D), dtype=jnp.float32)
        adj_raw = jax.random.uniform(k2, (B, N, N), dtype=jnp.float32)
        lim = 1.0 / np.sqrt(D)
        Wq = jax.random.uniform(k3, (D, D), minval=-lim, maxval=lim, dtype=jnp.float32)
        Wk = jax.random.uniform(k4, (D, D), minval=-lim, maxval=lim, dtype=jnp.float32)
        gamma_raw = jnp.float32(-0.85)
        return {'h': h, 'adj_raw': adj_raw, 'Wq': Wq, 'Wk': Wk, 'gamma_raw': gamma_raw}
    _L0_xattn_all = _L0_xattn_setup()
    _L0_xattn_in = {k: v for k, v in _L0_xattn_all.items() if k in ('Wq', 'Wk', 'gamma_raw')}
    del _L0_xattn_all

    def _L0_ffn_setup():
        import jax, jax.numpy as jnp
        import numpy as np
        _FP8_MAX = 448.0
        _BLOCK = 32
        _EPS = 1e-30

        def _mx_dequant(t):
            rows, feat = t.shape
            blocks = t.reshape(rows, feat // _BLOCK, _BLOCK)
            max_abs = jnp.max(jnp.abs(blocks), axis=-1)
            scales = jnp.maximum(max_abs / _FP8_MAX, _EPS)
            q = (blocks / scales[..., None]).astype(jnp.float8_e4m3fn).astype(jnp.float32)
            return (q * scales[..., None]).reshape(rows, feat)

        def _mx_linear(x2d, w):
            return _mx_dequant(x2d) @ _mx_dequant(w).T
        key = jax.random.key(seed)
        k1, k2, k3, k4 = jax.random.split(key, 4)
        B, S, H, I = (2, 128, 256, 1024)
        return {'x': jax.random.normal(k1, (B, S, H), dtype=jnp.float32), 'gate_w': jax.random.normal(k2, (I, H), dtype=jnp.float32) * 0.02, 'up_w': jax.random.normal(k3, (I, H), dtype=jnp.float32) * 0.02, 'down_w': jax.random.normal(k4, (H, I), dtype=jnp.float32) * 0.02}
    _L0_ffn_all = _L0_ffn_setup()
    _L0_ffn_in = {k: v for k, v in _L0_ffn_all.items() if k in ('gate_w', 'up_w', 'down_w')}
    del _L0_ffn_all

    def _L1_xattn_setup():
        import jax, jax.numpy as jnp
        import numpy as np
        B, S, L = (2, 128, 128)
        DIM_Q, H, K, D_C, D_CQ, R = (256, 16, 128, 64, 192, 64)

        def _rope_tables(length, dim):
            inv = 1.0 / 10000.0 ** (jnp.arange(0, dim, 2, dtype=jnp.float32) / dim)
            f = jnp.arange(length, dtype=jnp.float32)[:, None] * inv[None, :]
            sin = jnp.repeat(jnp.sin(f), 2, axis=-1)
            cos = jnp.repeat(jnp.cos(f), 2, axis=-1)
            return (sin, cos)

        def _rotate_half(x):
            half = x.shape[-1] // 2
            return jnp.concatenate([-x[..., half:], x[..., :half]], axis=-1)

        def _apply_rope(x, sin, cos):
            return x * cos + _rotate_half(x) * sin
        key = jax.random.key(seed)
        ks = jax.random.split(key, 8)
        return {'hidden_q': jax.random.normal(ks[0], (B, S, DIM_Q), jnp.float32), 'kv_c': jax.random.normal(ks[1], (B, L, D_C), jnp.float32), 'Wq': jax.random.normal(ks[2], (H * K, DIM_Q), jnp.float32) / np.sqrt(DIM_Q).astype(np.float32), 'w_kc_q': jax.random.normal(ks[3], (H, K, D_CQ), jnp.float32) / np.sqrt(K).astype(np.float32), 'w_kc_kv': jax.random.normal(ks[4], (H, K, D_C), jnp.float32) / np.sqrt(K).astype(np.float32), 'W_qr': jax.random.normal(ks[5], (H, D_CQ, R), jnp.float32) / np.float32(np.sqrt(D_CQ) * np.sqrt(R)), 'W_kr': jax.random.normal(ks[6], (H, D_C, R), jnp.float32) / np.sqrt(D_C).astype(np.float32), 'Wo': jax.random.normal(ks[7], (DIM_Q, H * K), jnp.float32) / np.sqrt(H * K).astype(np.float32)}
    _L1_xattn_all = _L1_xattn_setup()
    _L1_xattn_in = {k: v for k, v in _L1_xattn_all.items() if k in ('Wq', 'w_kc_q', 'w_kc_kv', 'W_qr', 'W_kr', 'Wo')}
    del _L1_xattn_all

    def _L1_ffn_setup():
        import jax, jax.numpy as jnp
        import numpy as np
        B, S, D_IN, D_OUT, E = (4, 128, 256, 256, 32)
        MASK_DENSITY = 0.3
        THRESH = 0.5
        key = jax.random.key(seed)
        k_x, k_w, k_m, k_r = jax.random.split(key, 4)
        x = jax.random.normal(k_x, (B, S, D_IN), dtype=jnp.float32)
        bound = np.sqrt(1.0 / D_IN) * np.sqrt(3.0)
        weight = jax.random.uniform(k_w, (D_OUT, D_IN), minval=-bound, maxval=bound, dtype=jnp.float32)
        scale = jnp.ones((D_OUT,), dtype=jnp.float32)
        expert_masks = (jax.random.uniform(k_m, (E, D_OUT, D_IN)) < MASK_DENSITY).astype(jnp.float32)
        router_w = 0.01 * jax.random.normal(k_r, (E, D_IN), dtype=jnp.float32)
        return {'x': x, 'weight': weight, 'scale': scale, 'expert_masks': expert_masks, 'router_w': router_w}
    _L1_ffn_all = _L1_ffn_setup()
    _L1_ffn_in = {k: v for k, v in _L1_ffn_all.items() if k in ('weight', 'scale', 'expert_masks', 'router_w')}
    del _L1_ffn_all
    return {'x': x, 'ctx_512': ctx_512, 'L0_xattn_Wq': _L0_xattn_in['Wq'], 'L0_xattn_Wk': _L0_xattn_in['Wk'], 'L0_xattn_gamma_raw': _L0_xattn_in['gamma_raw'], 'L0_ffn_gate_w': _L0_ffn_in['gate_w'], 'L0_ffn_up_w': _L0_ffn_in['up_w'], 'L0_ffn_down_w': _L0_ffn_in['down_w'], 'L1_xattn_Wq': _L1_xattn_in['Wq'], 'L1_xattn_w_kc_q': _L1_xattn_in['w_kc_q'], 'L1_xattn_w_kc_kv': _L1_xattn_in['w_kc_kv'], 'L1_xattn_W_qr': _L1_xattn_in['W_qr'], 'L1_xattn_W_kr': _L1_xattn_in['W_kr'], 'L1_xattn_Wo': _L1_xattn_in['Wo'], 'L1_ffn_weight': _L1_ffn_in['weight'], 'L1_ffn_scale': _L1_ffn_in['scale'], 'L1_ffn_expert_masks': _L1_ffn_in['expert_masks'], 'L1_ffn_router_w': _L1_ffn_in['router_w']}

def reference(x, ctx_512, L0_xattn_Wq, L0_xattn_Wk, L0_xattn_gamma_raw, L0_ffn_gate_w, L0_ffn_up_w, L0_ffn_down_w, L1_xattn_Wq, L1_xattn_w_kc_q, L1_xattn_w_kc_kv, L1_xattn_W_qr, L1_xattn_W_kr, L1_xattn_Wo, L1_ffn_weight, L1_ffn_scale, L1_ffn_expert_masks, L1_ffn_router_w):
    import jax
    import jax.numpy as jnp

    def _L0_xattn_ref(h, adj_raw, Wq, Wk, gamma_raw):
        import jax, jax.numpy as jnp
        import numpy as np
        B, N, D = (16, 256, 64)
        H = 4
        TOP_K_RATIO = 0.3
        b, n, dm = h.shape
        d = dm // H
        Q = (h @ Wq.T).reshape(b, n, H, d).transpose(0, 2, 1, 3)
        K = (h @ Wk.T).reshape(b, n, H, d).transpose(0, 2, 1, 3)
        sim = jnp.einsum('bhnd,bhmd->bnm', Q, K) / (jnp.sqrt(jnp.float32(d)) * H)
        k = max(1, int(n * TOP_K_RATIO))
        topk_vals = jax.lax.top_k(sim, k)[0]
        threshold = topk_vals[:, :, -1:]
        sparse_mask = (sim >= threshold).astype(sim.dtype)
        A_learned = jax.nn.sigmoid(sim) * sparse_mask
        A_learned = (A_learned + jnp.swapaxes(A_learned, -1, -2)) * 0.5
        gamma = jax.nn.sigmoid(gamma_raw)
        return (1.0 - gamma) * adj_raw + gamma * A_learned

    def _L0_ffn_ref(x, gate_w, up_w, down_w):
        import jax, jax.numpy as jnp
        import numpy as np
        _FP8_MAX = 448.0
        _BLOCK = 32
        _EPS = 1e-30

        def _mx_dequant(t):
            rows, feat = t.shape
            blocks = t.reshape(rows, feat // _BLOCK, _BLOCK)
            max_abs = jnp.max(jnp.abs(blocks), axis=-1)
            scales = jnp.maximum(max_abs / _FP8_MAX, _EPS)
            q = (blocks / scales[..., None]).astype(jnp.float8_e4m3fn).astype(jnp.float32)
            return (q * scales[..., None]).reshape(rows, feat)

        def _mx_linear(x2d, w):
            return _mx_dequant(x2d) @ _mx_dequant(w).T
        B, S, H = x.shape
        x2d = x.reshape(B * S, H)
        gate = _mx_linear(x2d, gate_w)
        up = _mx_linear(x2d, up_w)
        h = jax.nn.silu(gate) * up
        out = _mx_linear(h, down_w)
        return out.reshape(B, S, H)

    def _L1_xattn_ref(hidden_q, kv_c, Wq, w_kc_q, w_kc_kv, W_qr, W_kr, Wo):
        import jax, jax.numpy as jnp
        import numpy as np
        B, S, L = (2, 128, 128)
        DIM_Q, H, K, D_C, D_CQ, R = (256, 16, 128, 64, 192, 64)

        def _rope_tables(length, dim):
            inv = 1.0 / 10000.0 ** (jnp.arange(0, dim, 2, dtype=jnp.float32) / dim)
            f = jnp.arange(length, dtype=jnp.float32)[:, None] * inv[None, :]
            sin = jnp.repeat(jnp.sin(f), 2, axis=-1)
            cos = jnp.repeat(jnp.cos(f), 2, axis=-1)
            return (sin, cos)

        def _rotate_half(x):
            half = x.shape[-1] // 2
            return jnp.concatenate([-x[..., half:], x[..., :half]], axis=-1)

        def _apply_rope(x, sin, cos):
            return x * cos + _rotate_half(x) * sin
        Bv, Sv, _ = hidden_q.shape
        _, Lv, _ = kv_c.shape
        q_hk = (hidden_q @ Wq.T).reshape(Bv, Sv, H, K)
        q_big = jnp.einsum('bshk,hkq->bshq', q_hk, w_kc_q)
        sin_q, cos_q = _rope_tables(Sv, D_CQ)
        q_big = _apply_rope(q_big, sin_q[None, :, None, :], cos_q[None, :, None, :])
        sin_k, cos_k = _rope_tables(Lv, D_C)
        kv_r = _apply_rope(kv_c, sin_k[None], cos_k[None])
        q_r = jnp.einsum('bshq,hqr->bhsr', q_big, W_qr)
        k_r = jnp.einsum('bld,hdr->bhlr', kv_r, W_kr)
        scores = jnp.einsum('bhsr,bhlr->bhsl', q_r, k_r)
        attn = jax.nn.softmax(scores, axis=-1)
        ctx_c = jnp.einsum('bhsl,bld->bhsd', attn, kv_r)
        ctx_lat = jnp.einsum('bhsd,hkd->bhsk', ctx_c, w_kc_kv)
        ctx = ctx_lat.transpose(0, 2, 1, 3).reshape(Bv, Sv, H * K)
        return ctx @ Wo.T

    def _L1_ffn_ref(x, weight, scale, expert_masks, router_w):
        import jax, jax.numpy as jnp
        import numpy as np
        B, S, D_IN, D_OUT, E = (4, 128, 256, 256, 32)
        MASK_DENSITY = 0.3
        THRESH = 0.5
        logits = jnp.einsum('bsd,ed->bse', x, router_w)
        probs = jax.nn.softmax(logits, axis=-1)
        top1_w = jnp.max(probs, axis=-1)
        top1_idx = jnp.argmax(probs, axis=-1)
        w_q = jnp.clip(jnp.round(weight / THRESH), -1.0, 1.0)
        w_scaled = w_q * scale[:, None]
        out0 = jnp.zeros((x.shape[0], x.shape[1], weight.shape[0]), dtype=x.dtype)

        def body(out, inputs):
            e_idx, mask_e = inputs
            y = jnp.einsum('bsi,oi->bso', x, w_scaled * mask_e)
            sel = (top1_idx == e_idx)[..., None]
            out = jnp.where(sel, y * top1_w[..., None], out)
            return (out, None)
        out, _ = jax.lax.scan(body, out0, (jnp.arange(E), expert_masks))
        return out
    x = x + _L0_xattn_ref(ctx_512, _layernorm(x, axis=-1), L0_xattn_Wq, L0_xattn_Wk, L0_xattn_gamma_raw)
    x = x + _L0_ffn_ref(_layernorm(x, axis=-1), L0_ffn_gate_w, L0_ffn_up_w, L0_ffn_down_w)
    x = x + _L1_xattn_ref(_layernorm(x, axis=-1), ctx_512, L1_xattn_Wq, L1_xattn_w_kc_q, L1_xattn_w_kc_kv, L1_xattn_W_qr, L1_xattn_W_kr, L1_xattn_Wo)
    x = x + _L1_ffn_ref(_layernorm(x, axis=-1), L1_ffn_weight, L1_ffn_scale, L1_ffn_expert_masks, L1_ffn_router_w)
    return x

_drawn_inputs = setup_inputs


def setup_inputs(seed=0):
    import zlib

    import numpy as np

    out = dict(_drawn_inputs(seed))
    spreads = {'L1_ffn_scale': (1.0, 0.2)}
    factors = {}
    for name, (base, spread) in spreads.items():
        noise = np.random.default_rng([zlib.crc32(name.encode()), seed]).standard_normal(out[name].shape)
        drawn = base * np.exp(spread * noise) if base else spread * noise
        out[name] = jnp.asarray(drawn.astype(out[name].dtype))
    for name, factor in factors.items():
        out[name] = (out[name] * factor).astype(out[name].dtype)
    return out
```

```python
from contextlib import ExitStack

import numpy as np

import concourse.bass as bass
from concourse import mybir

P = 128
F32 = mybir.dt.float32
F16 = mybir.dt.float16
F8 = mybir.dt.float8e4
U32 = mybir.dt.uint32
ALU = mybir.AluOpType
ACT = mybir.ActivationFunctionType
AX_X = mybir.AxisListType.X

B, S, D = 4, 256, 256
T = S // P
C = D // P
DC = 64
TOPK = int(S * 0.3)
ROUNDS = (TOPK + 7) // 8
I = 1024
BLK = 32
H, HK, DQ, R = 16, 128, 192, 64
PAIRS = H // 2
J = 2 * DQ // P
E = 32
EC = 2
NEC = E // EC
EF = 4
EPS = 1e-5
FP8_MAX = 448.0
EXP_BITS = 0x7F800000
ROUND4 = 1.5 * 2.0 ** 20
MIN_NORMAL = 2.0 ** -6
ROUND_INT = 1.5 * 2.0 ** 23


class Count:

    made = []

    def __init__(self, sem, per_batch, setup=0):
        self.sem, self.per_batch, self.setup = sem, per_batch, setup

    def at(self, b, k):
        return b * self.per_batch + (self.setup + k)


def build(nc, x, ctx_nat, ctx_t, adj_wq, adj_wk, gamma, gate_w, up_w, down_w, att_wq, kc_q, kc_kv,
          qr_t, kr_t, wo_t, moe_w, moe_scale, moe_masks, router, cos_q, sin_q, cos_k, sin_k, ident,
          rank, out):
    ctx = ExitStack()
    with ctx:
        def sb(name, cols, dt=F32, parts=P):
            return ctx.enter_context(nc.sbuf_tensor(name, [parts, cols], dt))

        def psum(name, cols):
            return ctx.enter_context(nc.psum_tensor(name, [P, cols], F32))

        def count(name, per_batch, setup=0):
            return Count(ctx.enter_context(nc.semaphore(name)), per_batch, setup)

        wA = sb("wA", C * H * DQ)
        wM = sb("wM", 2 * PAIRS * J * P)
        wF = sb("wF", PAIRS * D)
        wG = sb("wG", C * I)
        wU = sb("wU", C * I)
        wD = sb("wD", (I // P) * D)
        wE = sb("wE", C * E * D, F8)
        cosq = sb("cosq", J * S)
        sinq = sb("sinq", J * S)
        cosk = sb("cosk", T * DC)
        sink = sb("sink", T * DC)
        idn = sb("idn", P)
        scl = sb("scl", D)
        tern = sb("tern", C * D)
        rtr = sb("rtr", C * E)
        rnk = sb("rnk", T * E)
        awq = sb("awq", DC, parts=DC)
        awk = sb("awk", DC, parts=DC)
        gam = sb("gam", 4)
        halfneg = sb("halfneg", T)
        masks = sb("masks", 2 * C * EC * D)

        xb = sb("xb", T * D)
        cxt = sb("cxt", S, parts=DC)
        qk0 = sb("qk0", 2 * S, parts=DC)
        sim = sb("sim", T * S)
        wk = sb("wk", T * S)
        th = sb("th", T * S)
        am = wk
        y2 = sb("y2", T * D)
        x1 = y2
        x2 = sb("x2", T * D)
        top = sb("top", T * 8)
        ffn = sb("ffn", 6144)
        hid, qy, qm, hq = (ffn[:, i * I:(i + 1) * I] for i in range(4))
        hqT = ffn[:, 4096:5120]
        xn = ffn[:, 5120:5632]
        xqT = ffn[:, 5632:6144]
        sg = sb("sg", 512)
        small = sb("small", 128)
        amax, qsc, qrs = (sb(n, 64) for n in ("amax", "qsc", "qrs"))

        reg = sb("reg", 11392)
        at = [0]
        v3 = lambda ap, n: ap.rearrange("p (a b) -> p a b", a=n)

        def part(cols):
            at[0] += cols
            return reg[:, at[0] - cols:at[0]]
        cxn = part(T * DC)
        kvn = part(T * 2 * DC)
        kvt = part(S)
        xT = part(C * S)
        qcs = [part(2 * J * S) for _ in range(2)]
        qkT = part(S)
        at_attn = [at[0]]
        attn = [part(4 * S) for _ in range(2)]
        attT = part(4 * S)
        cT = part(PAIRS * S)
        xr = part(T * D)
        x3 = part(T * D)
        xT4 = part(C * S)
        outb = xr
        kvtmp = part(T * DC * 2)
        xhi = sb("xhi", C * S, F16)
        xlo = sb("xlo", C * S, F16)
        acc = [[attn[t][:, k * D:(k + 1) * D] for k in range(4)] for t in range(T)]
        a0 = at_attn[0]
        reg_acc = v3(reg[:, a0:a0 + 8 * S], T)
        nmax = sb("nmax", 8)
        ssum = sb("ssum", 8)
        rsum = sb("rsum", 8)
        route = sb("route", 8 * T * E)

        raw_q = reg[:, 0:H * DQ]
        raw_qr = reg[0:R, 3072:3072 + 2 * H * DQ]
        raw_kv = reg[:, 9216:9216 + H * DC]
        raw_kr = reg[0:R, 10240:10240 + H * DC]
        raw_wq = wM[:, 0:H * D]
        raw_wo = wE[:, :].bitcast(F32)
        nat = [wU[:, :], wD[:, :], ffn[:, 4096:6144]]
        wqy, wqm = ffn[:, 0:2048], ffn[:, 2048:4096]

        pQB = psum("pQB", 1024)
        pSC = psum("pSC", 1024)
        pQC = psum("pQC", 512)
        pTP = psum("pTP", 512)
        pGA = psum("pGA", 512)
        pUA = psum("pUA", 512)

        QBf, QBd = count("qb_filled", 16, 6), count("qb_drained", 16, 6)
        SCf, SCd = count("sc_filled", 16, 6), count("sc_drained", 16, 6)
        QCf, QCd = count("qc_filled", 10, 3), count("qc_drained", 10, 3)
        TPf, TPd = count("tp_filled", 19, 3), count("tp_drained", 19, 3)
        GAf, GAd = count("ga_filled", 10, 6), count("ga_drained", 10, 6)
        UAf, UAd = count("ua_filled", 8, 6), count("ua_drained", 8, 6)
        CXf, CXd = count("cx_filled", 8), count("cx_drained", 8)
        ld_x, ld_cxt, ld_cxn = (count(n, 16) for n in ("ld_x", "ld_cxt", "ld_cxn"))
        ld_adj = count("ld_adj", 0, 16 * 4)
        ld_nat = [count(f"ld_nat{i}", 0, 16) for i in range(3)]
        ld_fold = count("ld_fold", 0, 16 * 2)
        ld_fold2 = count("ld_fold2", 0, 16 * 4)
        ld_tab = count("ld_tab", 0, 16 * 7)
        ld_moe = count("ld_moe", 0, 16)
        ld_mask = [count(f"ld_mask{i}", 0) for i in range(2)]
        stored = count("stored", 16)
        half_ready = count("half_ready", 0, 1)
        m_zero = count("m_zero", 0, 1)
        gam_t = count("gam_t", 0, 1)
        gam_ready = count("gam_ready", 0, 2)
        tern_step = count("tern_step", 0, 3)
        mask_used = count("mask_used", 0, NEC)
        ln_stats = [count(f"ln{i}_stats", 2) for i in range(4)]
        ln_mv = [count(f"ln{i}_mv", 2) for i in range(4)]
        ln_step = [count(f"ln{i}_step", 4 if i == 0 else 3) for i in range(4)]
        ln_ready = [count(f"ln{i}_ready", 2 if i == 0 else 1) for i in range(4)]
        th_ready = count("th_ready", 1)
        th1_ready = count("th1_ready", 1)
        topk_step = count("topk_step", T * (2 * ROUNDS - 1))
        am_ready = count("am_ready", T)
        y2_ready = count("y2_ready", T)
        x1_ready = count("x1_ready", 1)
        xn_ready = count("xn_ready", T)
        q_step = count("q_step", 8 * 3, 8 * 3)
        hq_ready = count("hq_ready", 3, 3)
        thg_ready = count("thg_ready", 4)
        xr_ready = count("xr_ready", 1)
        xn3_ready = count("xn3_ready", T)
        kv_step = count("kv_step", 4)
        kv_ready = count("kv_ready", 1)
        qc_ready = count("qc_ready", PAIRS)
        nmax_ready = count("nmax_ready", PAIRS)
        exp_done = count("exp_done", 4 * PAIRS)
        rsum_ready = count("rsum_ready", PAIRS)
        attn_ready = count("attn_ready", PAIRS)
        xn4_ready = count("xn4_ready", T)
        xhi_ready = count("xhi_ready", 1)
        xlo_ready = count("xlo_ready", 1)
        rt_step = count("rt_step", 7)
        ex_done = count("ex_done", 1)
        sel_ready = count("sel_ready", 1)
        acc_step = count("acc_step", 3 * 16)
        osum = count("osum", 3)
        o_step = count("o_step", 1)
        o_ready = count("o_ready", 1)

        block = ctx.enter_context(nc.Block())

        def ln_small(i):
            o = 24 * i
            st = small[:, o:o + 12].rearrange("p (t s) -> p t s", t=T)
            mv = small[:, o + 12:o + 16].rearrange("p (t s) -> p t s", t=T)
            return st, mv, small[:, o + 16:o + 18], small[:, o + 18:o + 20], small[:, o + 20:o + 22], small[:, o + 22:o + 24]

        selw = v3(route[:, 0:T * E], T)

        def qb_fill(f):
            return (pQB, QBf, QBd) if f % 2 == 0 else (pSC, SCf, SCd)

        def fold_fill(i):
            return (pQB, QBf, QBd, i // 2) if i % 2 == 0 else (pSC, SCf, SCd, i // 2)

        @block.sync
        def _(sp):
            sp.dma_start(awq[:, :], adj_wq).then_inc(ld_adj.sem, 16)
            sp.dma_start(awk[:, :], adj_wk).then_inc(ld_adj.sem, 16)
            sp.dma_start(idn[:, :], ident).then_inc(ld_adj.sem, 16)
            sp.dma_start(gam[:, 0:1], gamma.partition_broadcast(P)).then_inc(ld_adj.sem, 16)
            sp.dma_start(nat[0], gate_w).then_inc(ld_nat[0].sem, 16)
            sp.dma_start(nat[1], up_w).then_inc(ld_nat[1].sem, 16)
            sp.dma_start(nat[2], down_w).then_inc(ld_nat[2].sem, 16)
            sp.dma_start(tern[:, :], moe_w).then_inc(ld_moe.sem, 16)
            for dst, src in ((cosq, cos_q), (sinq, sin_q), (cosk, cos_k), (sink, sin_k), (rtr, router), (rnk, rank)):
                sp.dma_start(dst[:, :], src).then_inc(ld_tab.sem, 16)
            sp.dma_start(scl[:, :], moe_scale.partition_broadcast(P)).then_inc(ld_tab.sem, 16)
            for n in range(NEC):
                if n >= 2:
                    sp.wait_ge(mask_used.sem, n - 1)
                sp.dma_start(masks[:, (n % 2) * 1024:(n % 2 + 1) * 1024], moe_masks[n]).then_inc(ld_mask[n % 2].sem, 16)
            for b in range(B):
                sp.wait_ge(y2_ready.sem, y2_ready.at(b, 0))
                sp.dma_start(v3(xb[:, :], T), x[b].rearrange("(t p) d -> p t d", p=P)).then_inc(ld_x.sem, 16)
                sp.wait_ge(GAf.sem, GAf.at(b, 0))
                sp.dma_start(cxt[:, :], ctx_t[b]).then_inc(ld_cxt.sem, 16)
                sp.wait_ge(kv_ready.sem, kv_ready.at(b, 0))
                sp.wait_ge(CXf.sem, CXf.at(b, 0))
                sp.wait_ge(QBd.sem, QBd.at(0, 0))
                sp.wait_ge(SCd.sem, SCd.at(0, 0))
                sp.wait_ge(QCd.sem, QCd.at(0, 0))
                sp.wait_ge(TPd.sem, TPd.at(0, 0))
                sp.dma_start(v3(cxn, T), ctx_nat[b].rearrange("(t p) d -> p t d", p=P)).then_inc(ld_cxn.sem, 16)

        @block.tensor
        def _(pe):
            def mm(dst, lhsT, rhs, start=True, stop=True):
                return nc.tensor.matmul(dst, lhsT, rhs, start=start, stop=stop)

            def turn(dst, src):
                return nc.tensor.transpose(dst, src, idn[:, :])

            def setup():
                pe.wait_ge(ld_fold.sem, 32)
                for n in range(H // 2):
                    bank, f, d, k = fold_fill(n)
                    if k >= 1:
                        pe.wait_ge(d.sem, k)
                    for c in range(C):
                        for hh in range(2):
                            h = 2 * n + hh
                            last = mm(bank[:, c * 512 + hh * DQ:c * 512 + (hh + 1) * DQ],
                                      raw_wq[:, h * D + c * P:h * D + (c + 1) * P],
                                      raw_q[:, h * DQ:(h + 1) * DQ])
                    last.then_inc(f.sem, 1)
                pe.wait_ge(ld_fold2.sem, 64)
                for n in range(2 * J):
                    g, j = divmod(n, J)
                    bank, f, d = ((pTP, TPf, TPd), (pQC, QCf, QCd))[n % 2]
                    if n >= 2:
                        pe.wait_ge(d.sem, n // 2)
                    for p in range(PAIRS):
                        o = bank[:, p * DC:(p + 1) * DC]
                        for hh, lo, q0, w in ((0, 0, 0, P),) if j == 0 else ((1, 0, DC, P),) if j == 2 else ((0, 0, P, 64), (1, 64, 0, 64)):
                            h = 2 * p + hh
                            base = (g * H + h) * DQ + q0
                            last = mm(o[lo:lo + w, :], raw_qr[:, base:base + w], raw_kr[:, h * DC:(h + 1) * DC])
                    last.then_inc(f.sem, 1)
                for n in range(4):
                    bank, f, d, k = fold_fill(n)
                    pe.wait_ge(d.sem, 4 + k)
                    for pp in range(2):
                        for hh in range(2):
                            h = 4 * n + 2 * pp + hh
                            last = mm(bank[hh * 64:(hh + 1) * 64, pp * D:(pp + 1) * D],
                                      raw_kv[:, h * DC:(h + 1) * DC], raw_wo[:, h * D:(h + 1) * D])
                    last.then_inc(f.sem, 1)
                pe.wait_ge(ld_adj.sem, 64)
                for m in range(3):
                    pe.wait_ge(hq_ready.sem, m + 1)
                    for n in range(4):
                        bank, f, d = ((pGA, GAf, GAd), (pUA, UAf, UAd))[n % 2]
                        if 4 * m + n >= 2:
                            pe.wait_ge(d.sem, 2 * m + n // 2)
                        for k in range(4):
                            if m < 2:
                                c, half = divmod(n, 2)
                                src = nat[m][:, (4 * half + k) * D + c * P:(4 * half + k) * D + (c + 1) * P]
                            else:
                                j, ot = 2 * n + k // 2, k % 2
                                src = nat[m][:, ot * I + j * P:ot * I + (j + 1) * P]
                            last = turn(bank[:, k * P:(k + 1) * P], src)
                        last.then_inc(f.sem, 1)

            def adjacency(b):
                pe.wait_ge(ld_cxt.sem, ld_cxt.at(b, 16))
                pe.wait_ge(GAd.sem, GAd.at(b, 0))
                mm(pGA[0:DC, 0:S], awq[:, :], cxt[:, :])
                mm(pGA[0:DC, S:2 * S], awk[:, :], cxt[:, :]).then_inc(GAf.sem, 1)
                pe.wait_ge(GAd.sem, GAd.at(b, 1))
                pe.wait_ge(UAd.sem, UAd.at(b, 0))
                for t in range(T):
                    last = mm(pUA[:, t * S:(t + 1) * S], qk0[:, t * P:(t + 1) * P], qk0[:, S:2 * S])
                last.then_inc(UAf.sem, 1)

            def adjacency_turn(b):
                pe.wait_ge(am_ready.sem, am_ready.at(b, T))
                for r in range(T):
                    for c in range(T):
                        last = turn(pGA[:, r * S + c * P:r * S + (c + 1) * P], am[:, c * S + r * P:c * S + (r + 1) * P])
                last.then_inc(GAf.sem, 1)

            def ffn_in(b):
                pe.wait_ge(hq_ready.sem, hq_ready.at(b, 1))
                pe.wait_ge(UAd.sem, UAd.at(b, 1))
                for c in range(C):
                    for t in range(T):
                        last = turn(pUA[:, c * S + t * P:c * S + (t + 1) * P], hq[:, t * D + c * P:t * D + (c + 1) * P])
                last.then_inc(UAf.sem, 1)

            def ffn_up(b, t):
                for half in range(2):
                    u = 2 * t + half
                    pe.wait_ge(GAd.sem, GAd.at(b, 2 + u))
                    if u == 0:
                        pe.wait_ge(UAd.sem, UAd.at(b, 2))
                    for bank, w, f, d, k in ((pGA, wG, GAf, GAd, 2 + u), (pUA, wU, UAf, UAd, 2 + u)):
                        pe.wait_ge(d.sem, d.at(b, k))
                        for c in range(C):
                            last = mm(bank[:, :], xqT[:, c * S + t * P:c * S + (t + 1) * P],
                                      w[:, c * I + half * 512:c * I + (half + 1) * 512], c == 0, c == C - 1)
                        last.then_inc(f.sem, 1)

            def ffn_down(b, t):
                pe.wait_ge(hq_ready.sem, hq_ready.at(b, 2 + t))
                for bank, f, d, k, j0 in ((pGA, GAf, GAd, 6 + 2 * t, 0), (pUA, UAf, UAd, 6 + t, 4)):
                    pe.wait_ge(d.sem, d.at(b, k))
                    for j in range(4):
                        last = turn(bank[:, j * P:(j + 1) * P], hq[:, (j0 + j) * P:(j0 + j + 1) * P])
                    last.then_inc(f.sem, 1)
                pe.wait_ge(GAd.sem, GAd.at(b, 7 + 2 * t))
                pe.wait_ge(UAd.sem, UAd.at(b, 7 + t))
                for j in range(I // P):
                    last = mm(pGA[:, 0:D], hqT[:, j * P:(j + 1) * P], wD[:, j * D:(j + 1) * D], j == 0, j == I // P - 1)
                last.then_inc(GAf.sem, 1)

            def attention_in(b):
                pe.wait_ge(kv_ready.sem, kv_ready.at(b, 1))
                pe.wait_ge(TPd.sem, TPd.at(b, 0))
                for t in range(T):
                    last = turn(pTP[:, t * P:(t + 1) * P], kvn[:, t * P:(t + 1) * P])
                last.then_inc(TPf.sem, 1)
                pe.wait_ge(xn3_ready.sem, xn3_ready.at(b, T))
                pe.wait_ge(TPd.sem, TPd.at(b, 1))
                for c in range(C):
                    for t in range(T):
                        last = turn(pTP[:, c * S + t * P:c * S + (t + 1) * P], xT4[:, t * D + c * P:t * D + (c + 1) * P])
                last.then_inc(TPf.sem, 1)

            def project(b, p):
                if p == 0:
                    pe.wait_ge(TPd.sem, TPd.at(b, 2))
                pe.wait_ge(QBd.sem, QBd.at(b, p))
                pe.wait_ge(CXd.sem, CXd.at(b, max(p - 2, 0)))
                for j in range(J):
                    for c in range(C):
                        last = mm(pQB[:, j * S:(j + 1) * S], wA[:, c * H * DQ + (J * p + j) * P:c * H * DQ + (J * p + j + 1) * P],
                                  xT[:, c * S:(c + 1) * S], c == 0, c == C - 1)
                last.then_inc(QBf.sem, 1)

            def to_keys(b, p):
                pe.wait_ge(qc_ready.sem, qc_ready.at(b, p + 1))
                pe.wait_ge(QBd.sem, QBd.at(b, p + 1))
                pe.wait_ge(QCd.sem, QCd.at(b, p))
                for g in range(2):
                    for j in range(J):
                        m0 = ((g * PAIRS + p) * J + j) * P
                        last = mm(pQC[:, 0:S], wM[:, m0:m0 + P], qcs[p % 2][:, (g * J + j) * S:(g * J + j + 1) * S],
                                  g == 0 and j == 0, g == 1 and j == J - 1)
                last.then_inc(QCf.sem, 1)

            def scores(b, p, hh):
                if hh == 0:
                    pe.wait_ge(QCd.sem, QCd.at(b, p + 1))
                    pe.wait_ge(SCd.sem, SCd.at(b, p))
                for t in range(T):
                    o = (2 * hh + t) * S
                    last = mm(pSC[:, o:o + S], qkT[64 * hh:64 * hh + 64, t * P:(t + 1) * P], kvt[64 * hh:64 * hh + 64, :])
                if hh == 1:
                    last.then_inc(SCf.sem, 1)

            def attn_turn(b, p, hh):
                if hh == 0:
                    pe.wait_ge(attn_ready.sem, attn_ready.at(b, p + 1))
                pe.wait_ge(TPd.sem, TPd.at(b, 2 + 2 * p + hh))
                for c in range(T):
                    for t in range(T):
                        last = turn(pTP[:, c * S + t * P:c * S + (t + 1) * P],
                                    attn[p % 2][:, (2 * hh + t) * S + c * P:(2 * hh + t) * S + (c + 1) * P])
                last.then_inc(TPf.sem, 1)

            def context(b, p):
                pe.wait_ge(TPd.sem, TPd.at(b, 4 + 2 * p))
                pe.wait_ge(QBd.sem, QBd.at(b, min(p + 3, PAIRS)))
                pe.wait_ge(CXd.sem, CXd.at(b, p))
                for hh in range(2):
                    for c in range(T):
                        last = mm(pQB[64 * hh:64 * hh + 64, J * S:(J + 1) * S], kvn[:, c * P:c * P + DC],
                                  attT[:, (2 * hh + c) * S:(2 * hh + c + 1) * S], c == 0, c == T - 1)
                last.then_inc(CXf.sem, 1)

            def attention(b):
                project(b, 0)
                to_keys(b, 0)
                for p in range(PAIRS):
                    if p + 1 < PAIRS:
                        project(b, p + 1)
                    if p >= 1:
                        attn_turn(b, p - 1, 0)
                    scores(b, p, 0)
                    if p >= 1:
                        attn_turn(b, p - 1, 1)
                    scores(b, p, 1)
                    if p >= 1:
                        context(b, p - 1)
                    if p + 1 < PAIRS:
                        to_keys(b, p + 1)
                attn_turn(b, PAIRS - 1, 0)
                attn_turn(b, PAIRS - 1, 1)
                context(b, PAIRS - 1)
                pe.wait_ge(CXd.sem, CXd.at(b, PAIRS))
                for t in range(T):
                    for p in range(PAIRS):
                        last = mm(pQC[:, t * D:(t + 1) * D], cT[:, p * S + t * P:p * S + (t + 1) * P],
                                  wF[:, p * D:(p + 1) * D], p == 0, p == PAIRS - 1)
                last.then_inc(QCf.sem, 1)

            def experts(b):
                pe.wait_ge(xn4_ready.sem, xn4_ready.at(b, T))
                for c in range(C):
                    for t in range(T):
                        last = turn(pTP[:, c * S + t * P:c * S + (t + 1) * P], xT4[:, t * D + c * P:t * D + (c + 1) * P])
                last.then_inc(TPf.sem, 1)
                pe.wait_ge(TPd.sem, TPd.at(b, 19))
                pe.wait_ge(QCd.sem, QCd.at(b, 9))
                for t in range(T):
                    for c in range(C):
                        last = mm(pQC[:, t * E:(t + 1) * E], xT[:, c * S + t * P:c * S + (t + 1) * P],
                                  rtr[:, c * E:(c + 1) * E], c == 0, c == C - 1)
                last.then_inc(QCf.sem, 1)
                pe.wait_ge(xhi_ready.sem, xhi_ready.at(b, 1))
                pe.wait_ge(xlo_ready.sem, xlo_ready.at(b, 1))
                pe.wait_ge(mask_used.sem, NEC)
                for f in range(16):
                    t, q = divmod(f, E // EF)
                    bank, full, free = qb_fill(f)
                    pe.wait_ge(free.sem, free.at(b, 8 + f // 2))
                    for half in range(2):
                        e = EF * q + 2 * half
                        for c in range(C):
                            for k, src in enumerate((xhi, xlo)):
                                last = mm(bank[:, half * 512:(half + 1) * 512], src[:, c * S + t * P:c * S + (t + 1) * P],
                                          wE[:, (c * E + e) * D:(c * E + e + 2) * D], c == 0 and k == 0, c == C - 1 and k == 1)
                    last.then_inc(full.sem, 1)

            setup()
            for b in range(B):
                adjacency(b)
                adjacency_turn(b)
                ffn_in(b)
                ffn_up(b, 0)
                ffn_up(b, 1)
                ffn_down(b, 0)
                ffn_down(b, 1)
                attention_in(b)
                attention(b)
                experts(b)

        @block.scalar
        def _(act):
            def setup():
                act.dma_start(raw_wq, att_wq).then_inc(ld_fold.sem, 16)
                act.dma_start(raw_q, kc_q).then_inc(ld_fold.sem, 16)
                act.dma_start(raw_qr, qr_t).then_inc(ld_fold2.sem, 16)
                act.dma_start(raw_kr, kr_t).then_inc(ld_fold2.sem, 16)
                act.dma_start(raw_kv, kc_kv).then_inc(ld_fold2.sem, 16)
                act.dma_start(raw_wo, wo_t).then_inc(ld_fold2.sem, 16)
                act.wait_ge(ld_adj.sem, 64)
                nc.scalar.activation(gam[:, 1:2], gam[:, 0:1], ACT.Tanh, scale=0.5).then_inc(gam_t.sem, 1)
                for n in range(H // 2):
                    bank, f, d, k = fold_fill(n)
                    act.wait_ge(f.sem, k + 1)
                    nc.scalar.copy(v3(wA[:, :], C)[:, :, n * 384:(n + 1) * 384],
                                   v3(bank[:, :], 2)[:, :, 0:384]).then_inc(d.sem, 1)
                act.wait_ge(m_zero.sem, 1)
                for n in range(2 * J):
                    g, j = divmod(n, J)
                    bank, f, d = ((pTP, TPf, TPd), (pQC, QCf, QCd))[n % 2]
                    act.wait_ge(f.sem, n // 2 + 1)
                    dst = wM[:, :].rearrange("p (g a j m) -> p g a j m", g=2, a=PAIRS, j=J)[:, g, :, j, :]
                    src = v3(bank[:, :], PAIRS)
                    if j == 0:
                        last = nc.scalar.copy(dst[:, :, 0:DC], src)
                    elif j == 2:
                        last = nc.scalar.copy(dst[:, :, DC:P], src)
                    else:
                        nc.scalar.copy(dst[0:64, :, 0:DC], src[0:64])
                        last = nc.scalar.copy(dst[64:128, :, DC:P], src[64:128])
                    last.then_inc(d.sem, 1)
                for n in range(4):
                    bank, f, d, k = fold_fill(n)
                    act.wait_ge(f.sem, 5 + k)
                    nc.scalar.copy(wF[:, n * 512:(n + 1) * 512], bank[:, 0:512]).then_inc(d.sem, 1)
                for m in range(3):
                    for n in range(4):
                        bank, f, d = ((pGA, GAf, GAd), (pUA, UAf, UAd))[n % 2]
                        act.wait_ge(f.sem, 2 * m + n // 2 + 1)
                        nc.scalar.copy((wG, wU, wD)[m][:, n * 512:(n + 1) * 512], bank[:, :]).then_inc(d.sem, 1)

            def norm(b, i, dst, src, ready, r, nb):
                act.wait_ge(ln_ready[i].sem, ln_ready[i].at(b, ln_ready[i].per_batch))
                for t in range(T):
                    nc.scalar.activation(dst[:, t * D:(t + 1) * D], src[:, t * D:(t + 1) * D], ACT.Identity,
                                         bias=nb[:, t:t + 1], scale=r[:, t:t + 1]).then_inc(ready.sem, 1)

            def adjacency(b):
                act.wait_ge(GAf.sem, GAf.at(b, 1))
                nc.scalar.copy(qk0[:, :], pGA[0:DC, :]).then_inc(GAd.sem, 1)
                act.wait_ge(UAd.sem, UAd.at(b, 1))
                nc.scalar.activation(th[:, :], sim[:, :], ACT.Tanh, scale=1.0 / 32).then_inc(th_ready.sem, 1)
                _, _, r, nb, a1, b1 = ln_small(0)
                norm(b, 0, y2, xb, y2_ready, a1, b1)

            def ffn_in(b):
                _, _, r, nb, _, _ = ln_small(1)
                norm(b, 1, xn, x1, xn_ready, r, nb)
                act.wait_ge(UAf.sem, UAf.at(b, 2))
                nc.scalar.copy(xqT, pUA[:, :]).then_inc(UAd.sem, 1)

            def ffn_up(b, t):
                for half in range(2):
                    u = 2 * t + half
                    act.wait_ge(GAf.sem, GAf.at(b, 3 + u))
                    act.wait_ge(UAd.sem, UAd.at(b, 2 + u))
                    nc.scalar.activation(sg[:, :], pGA[:, :], ACT.Tanh, scale=0.5).then_inc(thg_ready.sem, 1)

            def ffn_down(b, t):
                act.wait_ge(GAf.sem, GAf.at(b, 7 + 2 * t))
                nc.scalar.copy(hqT[:, 0:512], pGA[:, :]).then_inc(GAd.sem, 1)
                act.wait_ge(UAf.sem, UAf.at(b, 7 + t))
                nc.scalar.copy(hqT[:, 512:1024], pUA[:, :]).then_inc(UAd.sem, 1)

            def attention_in(b):
                act.wait_ge(TPf.sem, TPf.at(b, 1))
                nc.scalar.copy(kvt, pTP[:, 0:S]).then_inc(TPd.sem, 1)
                _, _, r, nb, _, _ = ln_small(2)
                norm(b, 2, xT4, x2, xn3_ready, r, nb)
                act.wait_ge(TPf.sem, TPf.at(b, 2))
                nc.scalar.copy(xT, pTP[:, :]).then_inc(TPd.sem, 1)

            def keys_out(b, p):
                act.wait_ge(QCf.sem, QCf.at(b, p + 1))
                nc.scalar.copy(qkT, pQC[:, 0:S]).then_inc(QCd.sem, 1)

            def turned_out(b, p):
                for hh in range(2):
                    act.wait_ge(TPf.sem, TPf.at(b, 3 + 2 * p + hh))
                    nc.scalar.copy(attT[:, hh * 512:(hh + 1) * 512], pTP[:, :]).then_inc(TPd.sem, 1)

            def softmax(b, p):
                act.wait_ge(nmax_ready.sem, nmax_ready.at(b, p + 1))
                if p < 2:
                    act.wait_ge(o_step.sem, o_step.at(b, 0))
                for k in range(4):
                    o = 4 * (p % 2) + k
                    last = nc.scalar.activation(attn[p % 2][:, k * S:(k + 1) * S], pSC[:, k * S:(k + 1) * S], ACT.Exp,
                                                bias=nmax[:, o:o + 1], accum_out=ssum[:, o:o + 1])
                    last.then_inc((exp_done if k < 3 else SCd).sem, 1)

            def context_out(b, p):
                act.wait_ge(CXf.sem, CXf.at(b, p + 1))
                nc.scalar.copy(cT[:, p * S:(p + 1) * S], pQB[:, J * S:(J + 1) * S]).then_inc(CXd.sem, 1)

            def attention(b):
                keys_out(b, 0)
                for p in range(PAIRS):
                    if p >= 1:
                        turned_out(b, p - 1)
                    softmax(b, p)
                    if p >= 1:
                        context_out(b, p - 1)
                    if p + 1 < PAIRS:
                        keys_out(b, p + 1)
                turned_out(b, PAIRS - 1)
                context_out(b, PAIRS - 1)

            def experts(b):
                _, _, r, nb, _, _ = ln_small(3)
                norm(b, 3, xT4, x3, xn4_ready, r, nb)
                act.wait_ge(TPf.sem, TPf.at(b, 19))
                nc.scalar.copy(xT, pTP[:, :]).then_inc(TPd.sem, 1)
                act.wait_ge(TPd.sem, TPd.at(b, 19))
                nc.scalar.copy(xhi[:, :], xT).then_inc(xhi_ready.sem, 1)
                act.wait_ge(rt_step.sem, rt_step.at(b, 2))
                nc.scalar.activation(route[:, 64:128], route[:, 128:192], ACT.Exp).then_inc(ex_done.sem, 1)

            setup()
            for b in range(B):
                adjacency(b)
                ffn_in(b)
                ffn_up(b, 0)
                ffn_up(b, 1)
                ffn_down(b, 0)
                ffn_down(b, 1)
                attention_in(b)
                attention(b)
                experts(b)

        @block.vector
        def _(dve):
            def quantise(b, call, src, dst, mag, blocks, setup=False):
                q0 = q_step.at(b, 8 * call) if not setup else 8 * call
                h0 = hq_ready.at(b, call) if not setup else call
                blk = lambda ap: v3(ap, blocks)
                wide = lambda s: s[:, 0:blocks].unsqueeze(2).to_broadcast([P, blocks, BLK])
                nc.vector.tensor_reduce(amax[:, 0:blocks], blk(src), AX_X, ALU.max,
                                        apply_absolute_value=True).then_inc(q_step.sem, 1)
                dve.wait_ge(q_step.sem, q0 + 1)
                dve.wait_ge(hq_ready.sem, h0)
                nc.vector.tensor_scalar(qsc[:, 0:blocks], amax[:, 0:blocks], 1.0 / FP8_MAX, 1e-30,
                                        ALU.mult, ALU.max).then_inc(q_step.sem, 1)
                dve.wait_ge(q_step.sem, q0 + 2)
                nc.vector.reciprocal(qrs[:, 0:blocks], qsc[:, 0:blocks]).then_inc(q_step.sem, 1)
                dve.wait_ge(q_step.sem, q0 + 3)
                nc.vector.tensor_tensor(blk(dst), blk(src), wide(qrs), ALU.mult).then_inc(q_step.sem, 1)
                dve.wait_ge(q_step.sem, q0 + 4)
                nc.vector.tensor_scalar(mag.bitcast(U32), dst.bitcast(U32), EXP_BITS, None,
                                        ALU.bitwise_and).then_inc(q_step.sem, 1)
                dve.wait_ge(q_step.sem, q0 + 5)
                nc.vector.tensor_scalar(mag, mag, MIN_NORMAL, ROUND4, ALU.max, ALU.mult).then_inc(q_step.sem, 1)
                dve.wait_ge(q_step.sem, q0 + 6)
                nc.vector.tensor_tensor(dst, dst, mag, ALU.add).then_inc(q_step.sem, 1)
                dve.wait_ge(q_step.sem, q0 + 7)
                nc.vector.tensor_tensor(dst, dst, mag, ALU.subtract).then_inc(q_step.sem, 1)

            def stats(b, i, src):
                st, mv = ln_small(i)[:2]
                for t in range(T):
                    nc.vector.bn_stats(st[:, t, :], src[:, t * D:(t + 1) * D]).then_inc(ln_stats[i].sem, 1)
                for t in range(T):
                    dve.wait_ge(ln_stats[i].sem, ln_stats[i].at(b, t + 1))
                    nc.vector.bn_aggr(mv[:, t, :], st[:, t, :]).then_inc(ln_mv[i].sem, 1)

            def setup():
                dve.wait_ge(gam_t.sem, 1)
                nc.vector.tensor_scalar(gam[:, 2:3], gam[:, 1:2], -0.5, 0.5, ALU.mult, ALU.add).then_inc(gam_ready.sem, 1)
                nc.vector.tensor_scalar(gam[:, 3:4], gam[:, 1:2], 0.125, 0.125, ALU.mult, ALU.add).then_inc(gam_ready.sem, 1)
                dve.wait_ge(ld_moe.sem, 16)
                nc.vector.tensor_scalar(tern[:, :], tern[:, :], 2.0, ROUND_INT, ALU.mult, ALU.add).then_inc(tern_step.sem, 1)
                dve.wait_ge(tern_step.sem, 1)
                nc.vector.tensor_scalar(tern[:, :], tern[:, :], ROUND_INT, 1.0, ALU.subtract, ALU.min).then_inc(tern_step.sem, 1)
                dve.wait_ge(tern_step.sem, 2)
                nc.vector.tensor_scalar(tern[:, :], tern[:, :], -1.0, None, ALU.max).then_inc(tern_step.sem, 1)
                for m in range(3):
                    dve.wait_ge(ld_nat[m].sem, 16)
                    quantise(0, m, nat[m], wqy, wqm, 64, setup=True)

            def adjacency(b):
                dve.wait_ge(UAf.sem, UAf.at(b, 1))
                nc.vector.tensor_copy(sim[:, :], pUA[:, :]).then_inc(UAd.sem, 1)
                dve.wait_ge(ld_x.sem, ld_x.at(b, 16))
                stats(b, 0, xb)
                dve.wait_ge(UAd.sem, UAd.at(b, 1))
                n = 0
                for r in range(ROUNDS):
                    cur = sim if r == 0 else wk
                    for t in range(T):
                        if n >= T:
                            dve.wait_ge(topk_step.sem, topk_step.at(b, n - T + 1))
                        nc.vector.max(top[:, t * 8:(t + 1) * 8], cur[:, t * S:(t + 1) * S]).then_inc(topk_step.sem, 1)
                        n += 1
                    for t in range(T):
                        if r < ROUNDS - 1:
                            dve.wait_ge(topk_step.sem, topk_step.at(b, n - T + 1))
                            nc.vector.match_replace(wk[:, t * S:(t + 1) * S], top[:, t * 8:(t + 1) * 8],
                                                    cur[:, t * S:(t + 1) * S], -3.0e38).then_inc(topk_step.sem, 1)
                            n += 1
                dve.wait_ge(th1_ready.sem, th1_ready.at(b, 1))
                for t in range(T):
                    thr = top[:, t * 8 + (TOPK - 1) % 8:t * 8 + (TOPK - 1) % 8 + 1]
                    dve.wait_ge(topk_step.sem, topk_step.at(b, n - T + 1 + t))
                    nc.vector.scalar_tensor_tensor(am[:, t * S:(t + 1) * S], sim[:, t * S:(t + 1) * S], thr,
                                                   th[:, t * S:(t + 1) * S], ALU.is_ge, ALU.mult).then_inc(am_ready.sem, 1)

            def adjacency_out(b):
                dve.wait_ge(am_ready.sem, am_ready.at(b, T))
                dve.wait_ge(GAf.sem, GAf.at(b, 2))
                nc.vector.tensor_tensor(am[:, :], am[:, :], pGA[:, :], ALU.add).then_inc(GAd.sem, 1)
                dve.wait_ge(GAd.sem, GAd.at(b, 2))
                dve.wait_ge(y2_ready.sem, y2_ready.at(b, T))
                dve.wait_ge(gam_ready.sem, 2)
                nc.vector.scalar_tensor_tensor(x1[:, :], am[:, :], gam[:, 3:4], y2[:, :], ALU.mult, ALU.add).then_inc(x1_ready.sem, 1)
                dve.wait_ge(x1_ready.sem, x1_ready.at(b, 1))
                stats(b, 1, x1)

            def ffn_in(b):
                dve.wait_ge(xn_ready.sem, xn_ready.at(b, T))
                quantise(b, 0, xn, qy[:, 0:512], qm[:, 0:512], 16)

            def ffn_up(b, t):
                for half in range(2):
                    u = 2 * t + half
                    dve.wait_ge(thg_ready.sem, thg_ready.at(b, u + 1))
                    nc.vector.scalar_tensor_tensor(sg[:, :], sg[:, :], 1.0, pGA[:, :], ALU.add, ALU.mult).then_inc(GAd.sem, 1)
                    dve.wait_ge(GAd.sem, GAd.at(b, 3 + u))
                    dve.wait_ge(UAf.sem, UAf.at(b, 3 + u))
                    nc.vector.scalar_tensor_tensor(hid[:, half * 512:(half + 1) * 512], sg[:, :], 0.5, pUA[:, :],
                                                   ALU.mult, ALU.mult).then_inc(UAd.sem, 1)
                dve.wait_ge(UAd.sem, UAd.at(b, 4 + 2 * t))
                quantise(b, 1 + t, hid, qy, qm, 32)

            def ffn_down(b, t):
                dve.wait_ge(GAf.sem, GAf.at(b, 8 + 2 * t))
                if t == 0:
                    dve.wait_ge(xr_ready.sem, xr_ready.at(b, 0))
                    dve.wait_ge(xn3_ready.sem, xn3_ready.at(b, 0))
                nc.vector.tensor_tensor(x2[:, t * D:(t + 1) * D], x1[:, t * D:(t + 1) * D], pGA[:, 0:D], ALU.add).then_inc(GAd.sem, 1)

            def attention_in(b):
                dve.wait_ge(GAd.sem, GAd.at(b, 10))
                stats(b, 2, x2)

            def rotate(b, p):
                if p == 0:
                    dve.wait_ge(ld_tab.sem, 112)
                dve.wait_ge(QBf.sem, QBf.at(b, p + 1))
                dve.wait_ge(QCf.sem, QCf.at(b, max(p - 1, 0)))
                for g, tab in enumerate((cosq, sinq)):
                    nc.vector.tensor_tensor(qcs[p % 2][:, g * J * S:(g + 1) * J * S], pQB[:, 0:J * S], tab[:, :],
                                            ALU.mult).then_inc((qc_ready if g == 0 else QBd).sem, 1)

            def row_max(b, p):
                dve.wait_ge(SCf.sem, SCf.at(b, p + 1))
                nc.vector.tensor_reduce(nmax[:, 4 * (p % 2):4 * (p % 2) + 4], v3(pSC[:, :], 4), AX_X, ALU.max,
                                        negate=True).then_inc(nmax_ready.sem, 1)

            def row_sum(b, p):
                dve.wait_ge(SCd.sem, SCd.at(b, p + 1))
                nc.vector.reciprocal(rsum[:, 4 * (p % 2):4 * (p % 2) + 4], ssum[:, 4 * (p % 2):4 * (p % 2) + 4]).then_inc(rsum_ready.sem, 1)

            def attention(b):
                rotate(b, 0)
                for p in range(PAIRS):
                    if p + 1 < PAIRS:
                        rotate(b, p + 1)
                    row_max(b, p)
                    row_sum(b, p)
                dve.wait_ge(QCf.sem, QCf.at(b, 9))
                dve.wait_ge(xr_ready.sem, xr_ready.at(b, 1))
                dve.wait_ge(o_ready.sem, o_ready.at(b, 0))
                nc.vector.tensor_tensor(x3, xr, pQC[:, :], ALU.add).then_inc(QCd.sem, 1)
                dve.wait_ge(QCd.sem, QCd.at(b, 9))
                stats(b, 3, x3)

            def experts(b):
                mx, es, wt, rm = (small[:, 96 + 2 * i:98 + 2 * i] for i in range(4))
                ex, df, rk = route[:, 64:128], route[:, 128:192], route[:, 192:256]
                wide = lambda s: s.unsqueeze(2).to_broadcast([P, T, E])
                dve.wait_ge(xhi_ready.sem, xhi_ready.at(b, 1))
                nc.vector.tensor_tensor(xlo[:, :], xT, xhi[:, :], ALU.subtract).then_inc(xlo_ready.sem, 1)
                dve.wait_ge(QCf.sem, QCf.at(b, 10))
                nc.vector.tensor_reduce(mx, v3(pQC[:, 0:T * E], T), AX_X, ALU.max).then_inc(rt_step.sem, 1)
                dve.wait_ge(rt_step.sem, rt_step.at(b, 1))
                nc.vector.tensor_tensor(v3(df, T), v3(pQC[:, 0:T * E], T), wide(mx), ALU.subtract).then_inc(rt_step.sem, 1)
                dve.wait_ge(rt_step.sem, rt_step.at(b, 2))
                nc.vector.scalar_tensor_tensor(rk, df, 0.0, rnk[:, :], ALU.is_equal, ALU.mult).then_inc(rt_step.sem, 1)
                dve.wait_ge(rt_step.sem, rt_step.at(b, 3))
                nc.vector.tensor_reduce(rm, v3(rk, T), AX_X, ALU.max).then_inc(QCd.sem, 1)
                dve.wait_ge(QCd.sem, QCd.at(b, 10))
                nc.vector.tensor_tensor(v3(rk, T), v3(rk, T), wide(rm), ALU.is_equal).then_inc(rt_step.sem, 1)
                dve.wait_ge(ex_done.sem, ex_done.at(b, 1))
                nc.vector.tensor_reduce(es, v3(ex, T), AX_X, ALU.add).then_inc(rt_step.sem, 1)
                dve.wait_ge(rt_step.sem, rt_step.at(b, 5))
                nc.vector.reciprocal(wt, es).then_inc(rt_step.sem, 1)
                dve.wait_ge(rt_step.sem, rt_step.at(b, 6))
                nc.vector.tensor_tensor(selw, v3(rk, T), wide(wt), ALU.mult).then_inc(rt_step.sem, 1)
                dve.wait_ge(rt_step.sem, rt_step.at(b, 7))
                for f in range(16):
                    t, q = divmod(f, E // EF)
                    bank, full, free = qb_fill(f)
                    dve.wait_ge(full.sem, full.at(b, 9 + f // 2))
                    if q > 0:
                        _, _, before = qb_fill(f - 1)
                        dve.wait_ge(before.sem, before.at(b, 9 + (f - 1) // 2))
                    for k in range(EF):
                        e = EF * q + k
                        src, w = bank[:, k * D:(k + 1) * D], selw[:, t, e:e + 1]
                        if q == 0:
                            ins = nc.vector.tensor_scalar(acc[t][k], src, w, None, ALU.mult)
                        else:
                            ins = nc.vector.scalar_tensor_tensor(acc[t][k], src, w, acc[t][k], ALU.mult, ALU.add)
                        ins.then_inc((acc_step if k < EF - 1 else free).sem, 1)
                dve.wait_ge(QBd.sem, QBd.at(b, 16))
                dve.wait_ge(SCd.sem, SCd.at(b, 16))
                a = [reg_acc[:, :, k * D:(k + 1) * D] for k in range(4)]
                nc.vector.tensor_tensor(a[0], a[0], a[1], ALU.add).then_inc(osum.sem, 1)
                nc.vector.tensor_tensor(a[2], a[2], a[3], ALU.add).then_inc(osum.sem, 1)
                dve.wait_ge(osum.sem, osum.at(b, 2))
                nc.vector.tensor_tensor(a[0], a[0], a[2], ALU.add).then_inc(osum.sem, 1)

            setup()
            for b in range(B):
                adjacency(b)
                adjacency_out(b)
                ffn_in(b)
                ffn_up(b, 0)
                ffn_up(b, 1)
                ffn_down(b, 0)
                ffn_down(b, 1)
                attention_in(b)
                attention(b)
                experts(b)

        @block.gpsimd
        def _(pool):
            def ts(dst, src, s1, s2, o1, o2=None):
                if o2 is None:
                    return nc.gpsimd.tensor_scalar(dst, src, s1, None, o1)
                return nc.gpsimd.tensor_scalar(dst, src, s1, s2, o1, o2)

            def dequant(b, call, src, dst, blocks, setup=False):
                q0 = (q_step.at(b, 8 * call) if not setup else 8 * call) + 8
                pool.wait_ge(q_step.sem, q0)
                wide = qsc[:, 0:blocks].unsqueeze(2).to_broadcast([P, blocks, BLK])
                nc.gpsimd.tensor_tensor(v3(dst, blocks), v3(src, blocks), wide, ALU.mult).then_inc(hq_ready.sem, 1)

            def rstd(b, i):
                _, mv, r, nb, a1, b1 = ln_small(i)
                step, ready = ln_step[i], ln_ready[i]
                pool.wait_ge(ln_mv[i].sem, ln_mv[i].at(b, T))
                ts(r, mv[:, :, 1], EPS, None, ALU.add).then_inc(step.sem, 1)
                ts(nb, mv[:, :, 0], -1.0, None, ALU.mult).then_inc(step.sem, 1)
                pool.wait_ge(step.sem, step.at(b, 2))
                nc.gpsimd.tensor_tensor(r, r, halfneg[:, :], ALU.pow).then_inc(step.sem, 1)
                pool.wait_ge(step.sem, step.at(b, 3))
                last = nc.gpsimd.tensor_tensor(nb, nb, r, ALU.mult)
                if i == 0:
                    last.then_inc(step.sem, 1)
                    pool.wait_ge(step.sem, step.at(b, 4))
                    ts(a1, r, gam[:, 2:3], 1.0, ALU.mult, ALU.add).then_inc(ready.sem, 1)
                    ts(b1, nb, gam[:, 2:3], None, ALU.mult).then_inc(ready.sem, 1)
                else:
                    last.then_inc(ready.sem, 1)

            def setup():
                nc.gpsimd.memset(halfneg[:, :], -0.5).then_inc(half_ready.sem, 1)
                pool.wait_ge(QBd.sem, 4)
                pool.wait_ge(SCd.sem, 4)
                nc.gpsimd.memset(wM[:, :], 0.0).then_inc(m_zero.sem, 1)
                for m in range(3):
                    dequant(0, m, wqy, nat[m], 64, setup=True)
                pool.wait_ge(tern_step.sem, 3)
                pool.wait_ge(QBd.sem, 6)
                pool.wait_ge(SCd.sem, 6)
                we = wE[:, :].rearrange("p (c e o) -> p c e o", c=C, e=E)
                for n in range(NEC):
                    pool.wait_ge(ld_mask[n % 2].sem, 16 * (n // 2 + 1))
                    src = masks[:, (n % 2) * 1024:(n % 2 + 1) * 1024].rearrange("p (c e o) -> p c e o", c=C, e=EC)
                    for c in range(C):
                        last = nc.gpsimd.tensor_tensor(we[:, c, n * EC:(n + 1) * EC, :], src[:, c],
                                                       tern[:, c * D:(c + 1) * D].unsqueeze(1).to_broadcast([P, EC, D]),
                                                       ALU.mult, saturate=False)
                    last.then_inc(mask_used.sem, 1)
                pool.wait_ge(half_ready.sem, 1)
                pool.wait_ge(gam_ready.sem, 2)

            def adjacency(b):
                pool.wait_ge(th_ready.sem, th_ready.at(b, 1))
                ts(th[:, :], th[:, :], 1.0, None, ALU.add).then_inc(th1_ready.sem, 1)
                rstd(b, 0)

            def ffn_in(b):
                rstd(b, 1)
                pool.wait_ge(UAf.sem, UAf.at(b, 0))
                dequant(b, 0, qy[:, 0:512], hq[:, 0:512], 16)

            def ffn_up(b, t):
                pool.wait_ge(UAf.sem, UAf.at(b, 2 if t == 0 else 7))
                dequant(b, 1 + t, qy, hq, 32)

            def keys(b):
                pool.wait_ge(ld_cxn.sem, ld_cxn.at(b, 16))
                pool.wait_ge(ld_tab.sem, 112)
                pool.wait_ge(CXf.sem, CXf.at(b, 0))
                hw = DC // 2
                a, r = v3(kvtmp[:, 0:T * DC], T), v3(kvtmp[:, T * DC:2 * T * DC], T)
                c3, cs, sn = v3(cxn, T), v3(cosk[:, :], T), v3(sink[:, :], T)
                nc.gpsimd.tensor_tensor(a, c3, cs, ALU.mult).then_inc(kv_step.sem, 1)
                nc.gpsimd.tensor_tensor(r[:, :, 0:hw], c3[:, :, hw:DC], sn[:, :, 0:hw], ALU.mult).then_inc(kv_step.sem, 1)
                nc.gpsimd.tensor_tensor(r[:, :, hw:DC], c3[:, :, 0:hw], sn[:, :, hw:DC], ALU.mult).then_inc(kv_step.sem, 1)
                pool.wait_ge(kv_step.sem, kv_step.at(b, 3))
                k4 = kvn.rearrange("p (t u d) -> p t u d", t=T, u=2)
                nc.gpsimd.tensor_tensor(k4[:, :, 0, :], a, r, ALU.add).then_inc(kv_step.sem, 1)
                nc.gpsimd.tensor_tensor(k4[:, :, 1, :], a, r, ALU.add).then_inc(kv_ready.sem, 1)

            def attention_in(b):
                rstd(b, 2)
                pool.wait_ge(QCd.sem, QCd.at(b, 0))
                pool.wait_ge(stored.sem, stored.at(b, 0))
                nc.gpsimd.tensor_copy(xr, x2[:, :]).then_inc(xr_ready.sem, 1)

            def attention(b):
                for p in range(PAIRS):
                    pool.wait_ge(rsum_ready.sem, rsum_ready.at(b, p + 1))
                    a = v3(attn[p % 2], 4)
                    nc.gpsimd.tensor_tensor(a, a, rsum[:, 4 * (p % 2):4 * (p % 2) + 4].unsqueeze(2).to_broadcast([P, 4, S]),
                                            ALU.mult).then_inc(attn_ready.sem, 1)

            def experts(b):
                rstd(b, 3)
                pool.wait_ge(osum.sem, osum.at(b, 3))
                pool.wait_ge(stored.sem, stored.at(b, 0))
                nc.gpsimd.tensor_tensor(v3(outb, T), reg_acc[:, :, 0:D], scl[:, :].unsqueeze(1).to_broadcast([P, T, D]),
                                        ALU.mult).then_inc(o_step.sem, 1)
                pool.wait_ge(o_step.sem, o_step.at(b, 1))
                nc.gpsimd.tensor_tensor(outb, outb, x3, ALU.add).then_inc(o_ready.sem, 1)
                pool.wait_ge(o_ready.sem, o_ready.at(b, 1))
                pool.dma_start(out[b].rearrange("(t p) d -> p t d", p=P), v3(outb, T)).then_inc(stored.sem, 16)

            setup()
            for b in range(B):
                adjacency(b)
                ffn_in(b)
                ffn_up(b, 0)
                ffn_up(b, 1)
                keys(b)
                attention_in(b)
                attention(b)
                experts(b)
            pool.wait_ge(stored.sem, 16 * B)


def tables():
    def rope(length, dim):
        inv = (1.0 / 10000.0 ** (np.arange(0, dim, 2, dtype=np.float32) / np.float32(dim))).astype(np.float32)
        f = np.arange(length, dtype=np.float32)[:, None] * inv[None, :]
        return np.repeat(np.sin(f), 2, axis=-1).astype(np.float32), np.repeat(np.cos(f), 2, axis=-1).astype(np.float32)

    sin, cos = rope(S, DQ)
    half = DQ // 2
    sin = np.concatenate([sin[:, half:], -sin[:, :half]], axis=1)
    q = np.arange(J * P) % DQ
    tile = lambda a: np.ascontiguousarray(a[:, q].T.reshape(J, P, S).transpose(1, 0, 2).reshape(P, J * S))
    sin_k, cos_k = rope(S, DC)
    sin_k = np.concatenate([-sin_k[:, :DC // 2], sin_k[:, DC // 2:]], axis=1)
    nat = lambda a: np.ascontiguousarray(a.reshape(T, P, DC).transpose(1, 0, 2).reshape(P, T * DC))
    rank = np.ascontiguousarray(np.broadcast_to((E - np.arange(E, dtype=np.float32)), (P, T, E)).reshape(P, T * E))
    return {"cos_q": tile(cos), "sin_q": tile(sin), "cos_k": nat(cos_k), "sin_k": nat(sin_k),
            "ident": np.eye(P, dtype=np.float32), "rank": rank}


def layout(i):
    def a(name):
        return np.asarray(i[name])
    rows = lambda w: w.reshape(-1, P, w.shape[1]).transpose(1, 0, 2).reshape(P, -1)
    qr = a("L1_xattn_W_qr")
    qr2 = np.stack([qr, np.roll(qr, DQ // 2, axis=1)])
    out = {
        "x": a("x"), "ctx_nat": a("ctx_512"), "ctx_t": a("ctx_512").transpose(0, 2, 1),
        "adj_wq": a("L0_xattn_Wq").T, "adj_wk": a("L0_xattn_Wk").T, "gamma": a("L0_xattn_gamma_raw").reshape(1),
        "gate_w": rows(a("L0_ffn_gate_w")), "up_w": rows(a("L0_ffn_up_w")), "down_w": rows(a("L0_ffn_down_w")),
        "att_wq": rows(a("L1_xattn_Wq")),
        "kc_q": a("L1_xattn_w_kc_q").transpose(1, 0, 2).reshape(HK, H * DQ),
        "kc_kv": a("L1_xattn_w_kc_kv").transpose(1, 0, 2).reshape(HK, H * DC),
        "qr_t": qr2.transpose(3, 0, 1, 2).reshape(R, 2 * H * DQ),
        "kr_t": a("L1_xattn_W_kr").transpose(2, 0, 1).reshape(R, H * DC),
        "wo_t": rows(a("L1_xattn_Wo").T),
        "moe_w": rows(a("L1_ffn_weight").T),
        "moe_scale": a("L1_ffn_scale"),
        "moe_masks": a("L1_ffn_expert_masks").reshape(NEC, EC, D, C, P).transpose(0, 4, 3, 1, 2).reshape(NEC, P, C * EC * D),
        "router": rows(a("L1_ffn_router_w").T),
    }
    out.update(tables())
    return {k: np.ascontiguousarray(v) for k, v in out.items()}


_INS = ["x", "ctx_nat", "ctx_t", "adj_wq", "adj_wk", "gamma", "gate_w", "up_w", "down_w", "att_wq", "kc_q", "kc_kv",
        "qr_t", "kr_t", "wo_t", "moe_w", "moe_scale", "moe_masks", "router", "cos_q", "sin_q", "cos_k", "sin_k",
        "ident", "rank"]


def kernel(**inputs):
    import concourse.bacc as _bacc
    from concourse.bass_utils import run_bass_kernel_spmd as _run

    nc = _bacc.Bacc("TRN2", target_bir_lowering=False, num_devices=1)
    laid = layout(inputs)
    arrays, args = {}, []
    for name in _INS:
        arrays[f"in_{name}"] = laid[name]
        args.append(nc.dram_tensor(f"in_{name}", laid[name].shape, mybir.dt.from_np(laid[name].dtype),
                                   kind="ExternalInput").ap())
    out = nc.dram_tensor("out_0", (B, S, D), F32, kind="ExternalOutput").ap()
    build(nc, *args, out)
    r = _run(nc, [arrays], core_ids=[0])
    return r.results[0]["out_0"]
```

```python
from contextlib import ExitStack

import numpy as np

import concourse.bass as bass
from concourse import mybir

P = 128
F32 = mybir.dt.float32
F16 = mybir.dt.float16
F8 = mybir.dt.float8e4
U32 = mybir.dt.uint32
ALU = mybir.AluOpType
ACT = mybir.ActivationFunctionType
AX_X = mybir.AxisListType.X

B, S, D = 4, 256, 256
T = S // P
C = D // P
DC = 64
TOPK = int(S * 0.3)
ROUNDS = (TOPK + 7) // 8
I = 1024
BLK = 32
H, HK, DQ, R = 16, 128, 192, 64
PAIRS = H // 2
J = 2 * DQ // P
E = 32
EC = 2
NEC = E // EC
EF = 4
EPS = 1e-5
FP8_MAX = 448.0
EXP_BITS = 0x7F800000
ROUND4 = 1.5 * 2.0 ** 20
MIN_NORMAL = 2.0 ** -6
ROUND_INT = 1.5 * 2.0 ** 23


class Count:

    def __init__(self, sem, per_batch, setup=0):
        self.sem, self.per_batch, self.setup = sem, per_batch, setup

    def at(self, b, k):
        return b * self.per_batch + self.setup + k


class Bank:

    def __init__(self, tensor, filled, drained):
        self.tensor, self.filled, self.drained, self.turn = tensor, filled, drained, {}

    def free(self, key):
        return self.turn[key]

    def done(self, key):
        return self.turn[key] + 1


def tensor_order():
    steps = [("adjacency", 0)]
    steps += [("fold_q", n) for n in range(H // 2)]
    steps += [("fold_k", n) for n in range(2 * J)]
    steps += [("fold_o", n) for n in range(4)]
    steps += [("adjacency_turn", 0)]
    steps += [("turn_w", m, n) for m in range(3) for n in range(4)]
    steps += [("ffn_in", 0)] + [("ffn_up", 0, u) for u in range(4)]
    for t in range(T):
        steps += [("hidden_turn", 0, t), ("ffn_down", 0, t)]
    for b in range(B):
        steps += [("keys_turn", b), ("x_turn", b), ("project", b, 0)]
        if b + 1 < B:
            steps += [("adjacency", b + 1)]
        steps += [("to_keys", b, 0)]
        if b >= 1:
            steps += [("att_out", b - 1)]
        for p in range(PAIRS):
            steps += [("scores", b, p)]
            if p >= 1:
                steps += [("attn_turn", b, p - 1, 0)]
            if p + 1 < PAIRS:
                steps += [("project", b, p + 1)]
            if p >= 1:
                steps += [("attn_turn", b, p - 1, 1)]
                if b >= 1:
                    steps += [("expert", b - 1, 2 * (p - 1))]
                steps += [("context", b, p - 1)]
            elif b >= 1:
                steps += [("moe_turn", b - 1)]
            if p + 1 < PAIRS:
                steps += [("to_keys", b, p + 1)]
            if p == 0 and b >= 1:
                steps += [("logits", b - 1)]
            first, second = BESIDE.get(p, ([], [])) if b + 1 < B else ([], [])
            steps += [(name, b + 1, *args) for name, *args in first]
            if p >= 1 and b >= 1:
                steps += [("expert", b - 1, 2 * (p - 1) + 1)]
            steps += [(name, b + 1, *args) for name, *args in second]
        steps += [("attn_turn", b, PAIRS - 1, 0), ("attn_turn", b, PAIRS - 1, 1)]
        if b >= 1:
            steps += [("expert", b - 1, FILLS - 2)]
        steps += [("context", b, PAIRS - 1)]
        if b >= 1:
            steps += [("expert", b - 1, FILLS - 1)]
    steps += [("att_out", B - 1), ("moe_turn", B - 1), ("logits", B - 1)]
    steps += [("expert", B - 1, f) for f in range(FILLS)]
    return steps


BESIDE = {
    2: ([("adjacency_turn",)], []),
    4: ([("ffn_in",)], [("ffn_up", 0)]),
    5: ([("ffn_up", 1)], [("ffn_up", 2)]),
    6: ([("ffn_up", 3)], [("hidden_turn", 0)]),
    7: ([("ffn_down", 0), ("hidden_turn", 1)], [("ffn_down", 1)]),
}
FILLS = T * E // EF


def banks_of(name, *args):
    if name in ("fold_q", "fold_o"):
        return [("QB", "SC")[args[0] % 2]]
    if name == "fold_k":
        return [("TP", "QC")[args[0] % 2]]
    if name == "turn_w":
        return [("GA", "UA")[args[1] % 2]]
    if name == "expert":
        return [("QB", "SC")[args[1] % 2] if args[0] == B - 1 else "SC"]
    return {
        "adjacency": ["GA", "UA"], "adjacency_turn": ["GA"], "ffn_in": ["UA"], "ffn_up": ["GA", "UA"],
        "hidden_turn": ["GA", "UA"], "ffn_down": ["GA"], "keys_turn": ["TP"], "x_turn": ["TP"],
        "project": ["QB"], "to_keys": ["QC"], "scores": ["SC"], "attn_turn": ["TP"], "context": ["QB"],
        "att_out": ["QC"], "moe_turn": ["TP"], "logits": ["QC"],
    }[name]


def build(nc, x, ctx_nat, ctx_t, adj_wq, adj_wk, gamma, gate_w, up_w, down_w, att_wq, kc_q, kc_kv,
          qr_t, kr_t, wo_t, moe_w, moe_scale, moe_masks, router, cos_q, sin_q, cos_k, sin_k, ident,
          rank, out):
    ctx = ExitStack()
    with ctx:
        def sb(name, cols, dt=F32, parts=P):
            return ctx.enter_context(nc.sbuf_tensor(name, [parts, cols], dt))

        def count(name, per_batch, setup=0):
            return Count(ctx.enter_context(nc.semaphore(name)), per_batch, setup)

        def bank(name, cols):
            return Bank(ctx.enter_context(nc.psum_tensor(name, [P, cols], F32)),
                        ctx.enter_context(nc.semaphore(name + "_filled")),
                        ctx.enter_context(nc.semaphore(name + "_drained")))

        def v3(ap, n):
            return ap.rearrange("p (a b) -> p a b", a=n)

        wA = sb("wA", C * H * DQ)
        wM = sb("wM", 2 * PAIRS * J * P)
        wF = sb("wF", PAIRS * D)
        wG = sb("wG", C * I)
        wU = sb("wU", C * I)
        wD = sb("wD", (I // P) * D)
        wE = sb("wE", C * E * D, F8)
        cosq = sb("cosq", J * S)
        sinq = sb("sinq", J * S)
        cosk = sb("cosk", T * DC)
        sink = sb("sink", T * DC)
        idn = sb("idn", P)
        scl = sb("scl", D)
        tern = sb("tern", C * D)
        rtr = sb("rtr", C * E)
        rnk = sb("rnk", T * E)
        awq = sb("awq", DC, parts=DC)
        awk = sb("awk", DC, parts=DC)
        gam = sb("gam", 4)
        halfneg = sb("halfneg", T)
        masks = sb("masks", 2 * C * EC * D)

        xb = sb("xb", T * D)
        cxt = sb("cxt", S, parts=DC)
        qk0 = sb("qk0", 2 * S, parts=DC)
        sim = sb("sim", T * S)
        wk = sb("wk", T * S)
        am = wk
        th = sb("th", T * S)
        y2 = sb("y2", T * D)
        x1 = y2
        x2 = [sb(f"x2_{i}", T * D) for i in range(2)]
        top = sb("top", T * 8)
        ffn = sb("ffn", 6144)
        hid, qy, qm, hq = (ffn[:, i * I:(i + 1) * I] for i in range(4))
        hqT = ffn[:, 4096:5120]
        xn = ffn[:, 5120:5632]
        xqT = ffn[:, 5632:6144]
        sg = sb("sg", 512)
        small = sb("small", 128)
        amax, qsc, qrs = (sb(n, 64) for n in ("amax", "qsc", "qrs"))

        reg = sb("reg", 11264)
        at = [0]

        def part(cols):
            at[0] += cols
            return reg[:, at[0] - cols:at[0]]
        cxn = part(T * DC)
        kvns = [part(T * 3 * DC) for _ in range(2)]
        kvt = part(2 * S)
        xT = part(C * S)
        qcs = part(2 * J * S)
        qkT = part(S)
        attn = [part(4 * S) for _ in range(2)]
        attT = part(4 * S)
        cT = part(PAIRS * S)
        x3 = part(T * D)
        xnat = part(C * S)
        kvtmp = part(T * DC * 2)
        xhi = sb("xhi", C * S, F16)
        xlo = sb("xlo", C * S, F16)
        acc = masks[:, 0:T * 2 * D].rearrange("p (t k d) -> p t k d", t=T, k=2)
        x4T = masks[:, T * 2 * D:T * 2 * D + C * S]
        nmax = sb("nmax", 8)
        ssum = sb("ssum", 8)
        rsum = sb("rsum", 8)
        route = sb("route", 4 * T * E)
        selw = v3(route[:, 0:T * E], T)
        ex, df, rk = (route[:, i * T * E:(i + 1) * T * E] for i in range(1, 4))

        raw_q = reg[:, 0:H * DQ]
        raw_qr = reg[:, 3072:3072 + H * DQ]
        raw_kv = reg[:, 6144:6144 + H * DC]
        raw_kr = reg[:, 7168:7168 + H * 2 * DC]
        raw_wq = wM[:, 0:H * D]
        raw_wo = wE[:, :].bitcast(F32)
        nat = [wU[:, :], wD[:, :], reg[:, 9216:11264]]
        wqy, wqm = ffn[:, 0:2048], ffn[:, 2048:4096]

        QB = bank("qb", 1024)
        SC = bank("sc", 1024)
        QC = bank("qc", 512)
        TP = bank("tp", 512)
        GA = bank("ga", 512)
        UA = bank("ua", 512)
        by_name = {"QB": QB, "SC": SC, "QC": QC, "TP": TP, "GA": GA, "UA": UA}
        order = tensor_order()
        for step in order:
            for name in banks_of(*step):
                turns = by_name[name].turn
                turns[step] = len(turns)

        def bank_of(*step):
            return by_name[banks_of(*step)[0]]

        ld_x, ld_cxt, ld_cxn = (count(n, 16) for n in ("ld_x", "ld_cxt", "ld_cxn"))
        ld_adj = count("ld_adj", 0, 16 * 4)
        ld_nat = [count(f"ld_nat{i}", 0, 16) for i in range(3)]
        ld_fold_q = count("ld_fold_q", 0, 16 * 2)
        ld_fold_k = count("ld_fold_k", 0, 16 * 3)
        ld_fold_o = count("ld_fold_o", 0, 16 * 2)
        ld_tab = count("ld_tab", 0, 16 * 7)
        ld_moe = count("ld_moe", 0, 16)
        ld_mask = [count(f"ld_mask{i}", 0) for i in range(2)]
        stored = count("stored", 16)
        half_ready = count("half_ready", 0, 1)
        kr_zero = count("kr_zero", 0, 1)
        m_zero = count("m_zero", 0, 1)
        kv_zero = count("kv_zero", 0, 1)
        gam_t = count("gam_t", 0, 1)
        gam_ready = count("gam_ready", 0, 2)
        tern_step = count("tern_step", 0, 3)
        mask_used = count("mask_used", 0, NEC)
        ln_stats = [count(f"ln{i}_stats", 2) for i in range(4)]
        ln_mv = [count(f"ln{i}_mv", 2) for i in range(4)]
        ln_step = [count(f"ln{i}_step", 4 if i == 0 else 3) for i in range(4)]
        ln_ready = [count(f"ln{i}_ready", 2 if i == 0 else 1) for i in range(4)]
        th_ready = count("th_ready", 1)
        th1_ready = count("th1_ready", 1)
        topk_step = count("topk_step", T * (2 * ROUNDS - 1))
        am_ready = count("am_ready", T)
        y2_ready = count("y2_ready", T)
        x1_ready = count("x1_ready", 1)
        xn_ready = count("xn_ready", T)
        q_step = count("q_step", 8 * 3, 8 * 3)
        hq_ready = count("hq_ready", 3, 3)
        thg_ready = count("thg_ready", 4)
        xn3_ready = count("xn3_ready", T)
        kv_step = count("kv_step", 4)
        kv_ready = count("kv_ready", 1)
        qc_ready = count("qc_ready", PAIRS)
        nmax_ready = count("nmax_ready", PAIRS)
        exp_done = count("exp_done", 3 * PAIRS)
        rsum_ready = count("rsum_ready", PAIRS)
        attn_ready = count("attn_ready", PAIRS)
        xn4_ready = count("xn4_ready", T)
        xhi_ready = count("xhi_ready", 1)
        xlo_ready = count("xlo_ready", 1)
        rt_step = count("rt_step", 7)
        ex_done = count("ex_done", 1)
        acc_step = count("acc_step", (EF - 1) * FILLS)
        osum = count("osum", 1)
        o_step = count("o_step", 1)
        o_ready = count("o_ready", 1)

        block = ctx.enter_context(nc.Block())

        def ln_small(i):
            o = 24 * i
            st = small[:, o:o + 12].rearrange("p (t s) -> p t s", t=T)
            mv = small[:, o + 12:o + 16].rearrange("p (t s) -> p t s", t=T)
            return st, mv, small[:, o + 16:o + 18], small[:, o + 18:o + 20], small[:, o + 20:o + 22], small[:, o + 22:o + 24]

        @block.sync
        def _(sp):
            def load_a(b):
                sp.wait_ge(y2_ready.sem, y2_ready.at(b, 0))
                sp.dma_start(v3(xb[:, :], T), x[b].rearrange("(t p) d -> p t d", p=P)).then_inc(ld_x.sem, 16)
                if b >= 1:
                    sp.wait_ge(GA.filled, GA.done(("adjacency", b - 1)))
                sp.dma_start(cxt[:, :], ctx_t[b]).then_inc(ld_cxt.sem, 16)

            def load_b(b):
                if b == 0:
                    sp.wait_ge(SC.filled, SC.done(("fold_q", H // 2 - 1)))
                else:
                    sp.wait_ge(kv_ready.sem, kv_ready.at(b, 0))
                sp.dma_start(v3(cxn, T), ctx_nat[b].rearrange("(t p) d -> p t d", p=P)).then_inc(ld_cxn.sem, 16)

            sp.dma_start(awq[:, :], adj_wq).then_inc(ld_adj.sem, 16)
            sp.dma_start(awk[:, :], adj_wk).then_inc(ld_adj.sem, 16)
            load_a(0)
            sp.dma_start(idn[:, :], ident).then_inc(ld_adj.sem, 16)
            sp.dma_start(gam[:, 0:1], gamma.partition_broadcast(P)).then_inc(ld_adj.sem, 16)
            sp.dma_start(nat[0], gate_w).then_inc(ld_nat[0].sem, 16)
            sp.dma_start(nat[1], up_w).then_inc(ld_nat[1].sem, 16)
            sp.dma_start(nat[2], down_w).then_inc(ld_nat[2].sem, 16)
            sp.dma_start(tern[:, :], moe_w).then_inc(ld_moe.sem, 16)
            for dst, src in ((cosq, cos_q), (sinq, sin_q), (cosk, cos_k), (sink, sin_k), (rtr, router), (rnk, rank)):
                sp.dma_start(dst[:, :], src).then_inc(ld_tab.sem, 16)
            sp.dma_start(scl[:, :], moe_scale.partition_broadcast(P)).then_inc(ld_tab.sem, 16)
            load_b(0)
            load_a(1)
            for n in range(NEC):
                if n == 2:
                    load_b(1)
                if n >= 2:
                    sp.wait_ge(mask_used.sem, n - 1)
                sp.dma_start(masks[:, (n % 2) * 1024:(n % 2 + 1) * 1024], moe_masks[n]).then_inc(ld_mask[n % 2].sem, 16)
            for b in range(2, B):
                load_a(b)
                load_b(b)

        @block.tensor
        def _(pe):
            def mm(dst, lhsT, rhs, start=True, stop=True, check=True):
                return nc.tensor.matmul(dst, lhsT, rhs, start=start, stop=stop, skip_group_check=not check)

            def turn(dst, src):
                return nc.tensor.transpose(dst, src, idn[:, :])

            def fold_q(n):
                k = bank_of("fold_q", n)
                if n == 0:
                    pe.wait_ge(ld_fold_q.sem, 32)
                pe.wait_ge(k.drained, k.free(("fold_q", n)))
                for c in range(C):
                    for hh in range(2):
                        h = 2 * n + hh
                        last = mm(k.tensor[:, c * 512 + hh * DQ:c * 512 + (hh + 1) * DQ],
                                  raw_wq[:, h * D + c * P:h * D + (c + 1) * P], raw_q[:, h * DQ:(h + 1) * DQ])
                last.then_inc(k.filled, 1)

            def fold_k(n):
                j, half = divmod(n, 2)
                k = bank_of("fold_k", n)
                if n == 0:
                    pe.wait_ge(ld_fold_k.sem, 48)
                pe.wait_ge(k.drained, k.free(("fold_k", n)))
                for a in range(4):
                    o = k.tensor[:, a * P:(a + 1) * P]
                    parts = {0: ((0, 0, 0, P),), 1: ((0, 0, P, 64), (1, 64, 0, 64)), 2: ((1, 0, DC, P),)}[j]
                    for hh, lo, q0, w in parts:
                        h = 2 * (4 * half + a) + hh
                        last = mm(o[lo:lo + w, :], raw_qr[:, h * DQ + q0:h * DQ + q0 + w], raw_kr[:, h * P:(h + 1) * P])
                last.then_inc(k.filled, 1)

            def fold_o(n):
                k = bank_of("fold_o", n)
                if n == 0:
                    pe.wait_ge(ld_fold_o.sem, 32)
                pe.wait_ge(k.drained, k.free(("fold_o", n)))
                for pp in range(2):
                    for hh in range(2):
                        h = 4 * n + 2 * pp + hh
                        last = mm(k.tensor[hh * 64:(hh + 1) * 64, pp * D:(pp + 1) * D],
                                  raw_kv[:, h * DC:(h + 1) * DC], raw_wo[:, h * D:(h + 1) * D])
                last.then_inc(k.filled, 1)

            def turn_w(m, n):
                k = bank_of("turn_w", m, n)
                pe.wait_ge(hq_ready.sem, m + 1)
                pe.wait_ge(k.drained, k.free(("turn_w", m, n)))
                for a in range(4):
                    if m < 2:
                        c, half = divmod(n, 2)
                        src = nat[m][:, (4 * half + a) * D + c * P:(4 * half + a) * D + (c + 1) * P]
                    else:
                        j, ot = 2 * n + a // 2, a % 2
                        src = nat[m][:, ot * I + j * P:ot * I + (j + 1) * P]
                    last = turn(k.tensor[:, a * P:(a + 1) * P], src)
                last.then_inc(k.filled, 1)

            def adjacency(b):
                key = ("adjacency", b)
                if b == 0:
                    pe.wait_ge(ld_adj.sem, 64)
                pe.wait_ge(ld_cxt.sem, ld_cxt.at(b, 16))
                pe.wait_ge(GA.drained, GA.free(key))
                mm(GA.tensor[0:DC, 0:S], awq[:, :], cxt[:, :])
                mm(GA.tensor[0:DC, S:2 * S], awk[:, :], cxt[:, :]).then_inc(GA.filled, 1)
                pe.wait_ge(GA.drained, GA.done(key))
                pe.wait_ge(UA.drained, UA.free(key))
                for t in range(T):
                    last = mm(UA.tensor[:, t * S:(t + 1) * S], qk0[:, t * P:(t + 1) * P], qk0[:, S:2 * S])
                last.then_inc(UA.filled, 1)

            def adjacency_turn(b):
                pe.wait_ge(am_ready.sem, am_ready.at(b, T))
                pe.wait_ge(GA.drained, GA.free(("adjacency_turn", b)))
                for r in range(T):
                    for c in range(T):
                        last = turn(GA.tensor[:, r * S + c * P:r * S + (c + 1) * P], am[:, c * S + r * P:c * S + (r + 1) * P])
                last.then_inc(GA.filled, 1)

            def ffn_in(b):
                pe.wait_ge(hq_ready.sem, hq_ready.at(b, 1))
                pe.wait_ge(UA.drained, UA.free(("ffn_in", b)))
                for c in range(C):
                    for t in range(T):
                        last = turn(UA.tensor[:, c * S + t * P:c * S + (t + 1) * P], hq[:, t * D + c * P:t * D + (c + 1) * P])
                last.then_inc(UA.filled, 1)

            def ffn_up(b, u):
                key = ("ffn_up", b, u)
                t, half = divmod(u, 2)
                if u == 0:
                    pe.wait_ge(UA.drained, UA.done(("ffn_in", b)))
                if b == 0 and u == 0:
                    pe.wait_ge(GA.drained, GA.done(("turn_w", 2, 2)))
                for k, w in ((GA, wG), (UA, wU)):
                    pe.wait_ge(k.drained, k.free(key))
                    for c in range(C):
                        last = mm(k.tensor[:, :], xqT[:, c * S + t * P:c * S + (t + 1) * P],
                                  w[:, c * I + half * 512:c * I + (half + 1) * 512], c == 0, c == C - 1)
                    last.then_inc(k.filled, 1)

            def hidden_turn(b, t):
                key = ("hidden_turn", b, t)
                pe.wait_ge(hq_ready.sem, hq_ready.at(b, 2 + t))
                for k, j0 in ((GA, 0), (UA, 4)):
                    pe.wait_ge(k.drained, k.free(key))
                    for j in range(4):
                        last = turn(k.tensor[:, j * P:(j + 1) * P], hq[:, (j0 + j) * P:(j0 + j + 1) * P])
                    last.then_inc(k.filled, 1)

            def ffn_down(b, t):
                pe.wait_ge(GA.drained, GA.free(("ffn_down", b, t)))
                pe.wait_ge(UA.drained, UA.done(("hidden_turn", b, t)))
                for j in range(I // P):
                    last = mm(GA.tensor[:, 0:D], hqT[:, j * P:(j + 1) * P], wD[:, j * D:(j + 1) * D], j == 0, j == I // P - 1)
                last.then_inc(GA.filled, 1)

            def keys_turn(b):
                kvn = kvns[b % 2]
                pe.wait_ge(kv_ready.sem, kv_ready.at(b, 1))
                pe.wait_ge(TP.drained, TP.free(("keys_turn", b)))
                for g in range(2):
                    for t in range(T):
                        o = t * 3 * DC + g * DC
                        last = turn(TP.tensor[:, g * S + t * P:g * S + (t + 1) * P], kvn[:, o:o + P])
                last.then_inc(TP.filled, 1)

            def turn_x(key, ready):
                b = key[1]
                pe.wait_ge(ready.sem, ready.at(b, T))
                pe.wait_ge(TP.drained, TP.free(key))
                for c in range(C):
                    for t in range(T):
                        last = turn(TP.tensor[:, c * S + t * P:c * S + (t + 1) * P], xnat[:, t * D + c * P:t * D + (c + 1) * P])
                last.then_inc(TP.filled, 1)

            def x_turn(b):
                turn_x(("x_turn", b), xn3_ready)

            def moe_turn(b):
                turn_x(("moe_turn", b), xn4_ready)

            def project(b, p):
                if p == 0:
                    pe.wait_ge(TP.drained, TP.done(("x_turn", b)))
                pe.wait_ge(QB.drained, QB.free(("project", b, p)))
                for j in range(J):
                    for c in range(C):
                        w = c * H * DQ + (J * p + j) * P
                        last = mm(QB.tensor[:, j * S:(j + 1) * S], wA[:, w:w + P], xT[:, c * S:(c + 1) * S], c == 0, c == C - 1)
                last.then_inc(QB.filled, 1)

            def to_keys(b, p):
                pe.wait_ge(QB.drained, QB.done(("project", b, p)))
                pe.wait_ge(QC.drained, QC.free(("to_keys", b, p)))
                o = QC.tensor
                def w(g, j):
                    m0 = ((g * PAIRS + p) * J + j) * P
                    return wM[:, m0:m0 + P]
                def q(g, j):
                    return qcs[:, (g * J + j) * S:(g * J + j + 1) * S]
                mm(o[:, 0:S], w(0, 1), q(0, 1), True, False, check=False)
                mm(o[:, 0:S], w(1, 1), q(1, 1), False, False, check=False)
                for g in range(2):
                    mm(o[0:DC, 0:S], w(g, 0)[:, 0:DC], q(g, 0), False, False, check=False)
                    last = mm(o[DC:P, 0:S], w(g, 2)[:, DC:P], q(g, 2), False, g == 1, check=False)
                last.then_inc(QC.filled, 1)

            def scores(b, p):
                pe.wait_ge(QC.drained, QC.done(("to_keys", b, p)))
                pe.wait_ge(SC.drained, SC.free(("scores", b, p)))
                for hh in range(2):
                    for t in range(T):
                        o = (2 * hh + t) * S
                        last = mm(SC.tensor[:, o:o + S], qkT[:, t * P:(t + 1) * P], kvt[:, hh * S:(hh + 1) * S])
                last.then_inc(SC.filled, 1)

            def attn_turn(b, p, hh):
                pe.wait_ge(attn_ready.sem, attn_ready.at(b, p + 1))
                pe.wait_ge(TP.drained, TP.free(("attn_turn", b, p, hh)))
                for c in range(T):
                    for t in range(T):
                        last = turn(TP.tensor[:, c * S + t * P:c * S + (t + 1) * P],
                                    attn[p % 2][:, (2 * hh + t) * S + c * P:(2 * hh + t) * S + (c + 1) * P])
                last.then_inc(TP.filled, 1)

            def context(b, p):
                kvn = kvns[b % 2]
                pe.wait_ge(TP.drained, TP.done(("attn_turn", b, p, 1)))
                pe.wait_ge(QB.drained, QB.free(("context", b, p)))
                for hh in range(2):
                    for c in range(T):
                        last = mm(QB.tensor[DC * hh:DC * (hh + 1), 0:S], kvn[:, c * 3 * DC:c * 3 * DC + DC],
                                  attT[:, (2 * hh + c) * S:(2 * hh + c + 1) * S], c == 0, c == T - 1)
                last.then_inc(QB.filled, 1)

            def att_out(b):
                pe.wait_ge(QB.drained, QB.done(("context", b, PAIRS - 1)))
                pe.wait_ge(QC.drained, QC.free(("att_out", b)))
                for t in range(T):
                    for p in range(PAIRS):
                        last = mm(QC.tensor[:, t * D:(t + 1) * D], cT[:, p * S + t * P:p * S + (t + 1) * P],
                                  wF[:, p * D:(p + 1) * D], p == 0, p == PAIRS - 1)
                last.then_inc(QC.filled, 1)

            def logits(b):
                pe.wait_ge(TP.drained, TP.done(("moe_turn", b)))
                pe.wait_ge(QC.drained, QC.free(("logits", b)))
                for t in range(T):
                    for c in range(C):
                        last = mm(QC.tensor[:, t * E:(t + 1) * E], x4T[:, c * S + t * P:c * S + (t + 1) * P],
                                  rtr[:, c * E:(c + 1) * E], c == 0, c == C - 1)
                last.then_inc(QC.filled, 1)

            def expert(b, f):
                q, t = divmod(f, T)
                k = bank_of("expert", b, f)
                if f == 0:
                    pe.wait_ge(mask_used.sem, NEC)
                    pe.wait_ge(xhi_ready.sem, xhi_ready.at(b, 1))
                    pe.wait_ge(xlo_ready.sem, xlo_ready.at(b, 1))
                pe.wait_ge(k.drained, k.free(("expert", b, f)))
                for half in range(2):
                    e = EF * q + 2 * half
                    for c in range(C):
                        for i, src in enumerate((xhi, xlo)):
                            last = mm(k.tensor[:, half * 512:(half + 1) * 512], src[:, c * S + t * P:c * S + (t + 1) * P],
                                      wE[:, (c * E + e) * D:(c * E + e + 2) * D], c == 0 and i == 0, c == C - 1 and i == 1)
                last.then_inc(k.filled, 1)

            steps = {f.__name__: f for f in (
                fold_q, fold_k, fold_o, turn_w, adjacency, adjacency_turn, ffn_in, ffn_up, hidden_turn, ffn_down,
                keys_turn, x_turn, project, to_keys, scores, attn_turn, context, att_out, moe_turn, logits, expert)}
            for name, *args in order:
                steps[name](*args)

        @block.scalar
        def _(act):
            def drain(bank, key, dst, src):
                act.wait_ge(bank.filled, bank.done(key))
                nc.scalar.copy(dst, src).then_inc(bank.drained, 1)

            def fold_q(n):
                k = bank_of("fold_q", n)
                drain(k, ("fold_q", n), v3(wA[:, :], C)[:, :, n * 384:(n + 1) * 384], v3(k.tensor[:, :], 2)[:, :, 0:384])

            def fold_k(n):
                j, half = divmod(n, 2)
                k = bank_of("fold_k", n)
                act.wait_ge(k.filled, k.done(("fold_k", n)))
                src = k.tensor[:, :].rearrange("p (a g d) -> p g a d", a=4, g=2)
                dst = wM[:, :].rearrange("p (g a j m) -> p g a j m", g=2, a=PAIRS, j=J)[:, :, 4 * half:4 * half + 4, j, :]
                for lo, hi, col in {0: ((0, P, 0),), 1: ((0, 64, 0), (64, P, DC)), 2: ((0, P, DC),)}[j]:
                    for g in range(2):
                        last = nc.scalar.copy(dst[lo:hi, g, :, col:col + DC], src[lo:hi, g])
                last.then_inc(k.drained, 1)

            def fold_o(n):
                k = bank_of("fold_o", n)
                drain(k, ("fold_o", n), wF[:, n * 512:(n + 1) * 512], k.tensor[:, 0:512])

            def turn_w(m, n):
                k = bank_of("turn_w", m, n)
                drain(k, ("turn_w", m, n), (wG, wU, wD)[m][:, n * 512:(n + 1) * 512], k.tensor[:, :])

            def norm(b, i, dst, src, ready):
                _, _, r, nb, a1, b1 = ln_small(i)
                scale, bias = (a1, b1) if i == 0 else (r, nb)
                act.wait_ge(ln_ready[i].sem, ln_ready[i].at(b, ln_ready[i].per_batch))
                for t in range(T):
                    nc.scalar.activation(dst[:, t * D:(t + 1) * D], src[:, t * D:(t + 1) * D], ACT.Identity,
                                         bias=bias[:, t:t + 1], scale=scale[:, t:t + 1]).then_inc(ready.sem, 1)

            def adjacency(b):
                drain(GA, ("adjacency", b), qk0[:, :], GA.tensor[0:DC, :])

            def adjacency_tanh(b):
                act.wait_ge(UA.drained, UA.done(("adjacency", b)))
                nc.scalar.activation(th[:, :], sim[:, :], ACT.Tanh, scale=1.0 / 32).then_inc(th_ready.sem, 1)

            def ffn_in(b):
                drain(UA, ("ffn_in", b), xqT, UA.tensor[:, :])

            def ffn_up(b, u):
                act.wait_ge(GA.filled, GA.done(("ffn_up", b, u)))
                act.wait_ge(UA.drained, UA.free(("ffn_up", b, u)))
                nc.scalar.activation(sg[:, :], GA.tensor[:, :], ACT.Tanh, scale=0.5).then_inc(thg_ready.sem, 1)

            def hidden_turn(b, t):
                drain(GA, ("hidden_turn", b, t), hqT[:, 0:512], GA.tensor[:, :])
                drain(UA, ("hidden_turn", b, t), hqT[:, 512:1024], UA.tensor[:, :])

            def keys_turn(b):
                drain(TP, ("keys_turn", b), kvt, TP.tensor[:, :])

            def x_turn(b):
                drain(TP, ("x_turn", b), xT, TP.tensor[:, :])

            def to_keys(b, p):
                drain(QC, ("to_keys", b, p), qkT, QC.tensor[:, 0:S])

            def attn_turn(b, p, hh):
                drain(TP, ("attn_turn", b, p, hh), attT[:, hh * 512:(hh + 1) * 512], TP.tensor[:, :])

            def softmax(b, p):
                act.wait_ge(nmax_ready.sem, nmax_ready.at(b, p + 1))
                for k in range(4):
                    o = 4 * (p % 2) + k
                    nc.scalar.activation(attn[p % 2][:, k * S:(k + 1) * S], SC.tensor[:, k * S:(k + 1) * S], ACT.Exp,
                                         bias=nmax[:, o:o + 1], accum_out=ssum[:, o:o + 1])\
                        .then_inc(exp_done.sem if k < 3 else SC.drained, 1)

            def context(b, p):
                if b >= 1:
                    act.wait_ge(QC.filled, QC.done(("att_out", b - 1)))
                drain(QB, ("context", b, p), cT[:, p * S:(p + 1) * S], QB.tensor[:, 0:S])

            def moe_turn(b):
                if b == 0:
                    act.wait_ge(mask_used.sem, NEC)
                drain(TP, ("moe_turn", b), x4T, TP.tensor[:, :])
                act.wait_ge(TP.drained, TP.done(("moe_turn", b)))
                nc.scalar.copy(xhi[:, :], x4T).then_inc(xhi_ready.sem, 1)

            def route_exp(b):
                act.wait_ge(rt_step.sem, rt_step.at(b, 2))
                nc.scalar.activation(ex, df, ACT.Exp).then_inc(ex_done.sem, 1)

            def moe_norm(b):
                act.wait_ge(QC.drained, QC.done(("att_out", b)))
                norm(b, 3, xnat, x3, xn4_ready)

            act.dma_start(raw_wq, att_wq).then_inc(ld_fold_q.sem, 16)
            act.dma_start(raw_q, kc_q).then_inc(ld_fold_q.sem, 16)
            act.dma_start(raw_qr, qr_t).then_inc(ld_fold_k.sem, 16)
            act.wait_ge(kr_zero.sem, 1)
            for g in range(2):
                act.dma_start(v3(raw_kr[g * R:(g + 1) * R, :], H)[:, :, g * DC:(g + 1) * DC], v3(kr_t, H))\
                    .then_inc(ld_fold_k.sem, 16)
            act.dma_start(raw_kv, kc_kv).then_inc(ld_fold_o.sem, 16)
            act.dma_start(raw_wo, wo_t).then_inc(ld_fold_o.sem, 16)
            act.wait_ge(ld_adj.sem, 64)
            nc.scalar.activation(gam[:, 1:2], gam[:, 0:1], ACT.Tanh, scale=0.5).then_inc(gam_t.sem, 1)
            adjacency(0)
            adjacency_tanh(0)
            for n in range(H // 2):
                fold_q(n)
            norm(0, 0, y2, xb, y2_ready)
            act.wait_ge(m_zero.sem, 1)
            for n in range(2 * J):
                fold_k(n)
            for n in range(4):
                fold_o(n)
            for n in range(4):
                turn_w(0, n)
            norm(0, 1, xn, x1, xn_ready)
            for m in range(1, 3):
                for n in range(4):
                    turn_w(m, n)
            ffn_in(0)
            for u in range(4):
                ffn_up(0, u)
            for t in range(T):
                hidden_turn(0, t)
            for b in range(B):
                more = b + 1 < B
                keys_turn(b)
                norm(b, 2, xnat, x2[b % 2], xn3_ready)
                x_turn(b)
                if more:
                    adjacency(b + 1)
                to_keys(b, 0)
                if more:
                    adjacency_tanh(b + 1)
                    norm(b + 1, 0, y2, xb, y2_ready)
                if b >= 1:
                    moe_norm(b - 1)
                for p in range(PAIRS):
                    if p >= 1:
                        attn_turn(b, p - 1, 0)
                    softmax(b, p)
                    if p >= 1:
                        attn_turn(b, p - 1, 1)
                        context(b, p - 1)
                    elif b >= 1:
                        moe_turn(b - 1)
                    if p + 1 < PAIRS:
                        to_keys(b, p + 1)
                    if p == 0 and b >= 1:
                        route_exp(b - 1)
                    if more:
                        if p == 3:
                            norm(b + 1, 1, xn, x1, xn_ready)
                        for name, *args in BESIDE.get(p, ([], []))[0] + BESIDE.get(p, ([], []))[1]:
                            if name in ("ffn_in", "ffn_up", "hidden_turn"):
                                {"ffn_in": ffn_in, "ffn_up": ffn_up, "hidden_turn": hidden_turn}[name](b + 1, *args)
                attn_turn(b, PAIRS - 1, 0)
                attn_turn(b, PAIRS - 1, 1)
                context(b, PAIRS - 1)
            moe_norm(B - 1)
            moe_turn(B - 1)
            route_exp(B - 1)

        @block.vector
        def _(dve):
            def quantise(q0, h0, src, dst, mag, blocks):
                def blk(ap):
                    return v3(ap, blocks)
                nc.vector.tensor_reduce(amax[:, 0:blocks], blk(src), AX_X, ALU.max,
                                        apply_absolute_value=True).then_inc(q_step.sem, 1)
                dve.wait_ge(q_step.sem, q0 + 1)
                dve.wait_ge(hq_ready.sem, h0)
                nc.vector.tensor_scalar(qsc[:, 0:blocks], amax[:, 0:blocks], 1.0 / FP8_MAX, 1e-30,
                                        ALU.mult, ALU.max).then_inc(q_step.sem, 1)
                dve.wait_ge(q_step.sem, q0 + 2)
                nc.vector.reciprocal(qrs[:, 0:blocks], qsc[:, 0:blocks]).then_inc(q_step.sem, 1)
                dve.wait_ge(q_step.sem, q0 + 3)
                nc.vector.tensor_tensor(blk(dst), blk(src), qrs[:, 0:blocks].unsqueeze(2).to_broadcast([P, blocks, BLK]),
                                        ALU.mult).then_inc(q_step.sem, 1)
                dve.wait_ge(q_step.sem, q0 + 4)
                nc.vector.tensor_scalar(mag.bitcast(U32), dst.bitcast(U32), EXP_BITS, None,
                                        ALU.bitwise_and).then_inc(q_step.sem, 1)
                dve.wait_ge(q_step.sem, q0 + 5)
                nc.vector.tensor_scalar(mag, mag, MIN_NORMAL, ROUND4, ALU.max, ALU.mult).then_inc(q_step.sem, 1)
                dve.wait_ge(q_step.sem, q0 + 6)
                nc.vector.tensor_tensor(dst, dst, mag, ALU.add).then_inc(q_step.sem, 1)
                dve.wait_ge(q_step.sem, q0 + 7)
                nc.vector.tensor_tensor(dst, dst, mag, ALU.subtract).then_inc(q_step.sem, 1)

            def stats(b, i, src):
                st, mv = ln_small(i)[:2]
                for t in range(T):
                    nc.vector.bn_stats(st[:, t, :], src[:, t * D:(t + 1) * D]).then_inc(ln_stats[i].sem, 1)
                for t in range(T):
                    dve.wait_ge(ln_stats[i].sem, ln_stats[i].at(b, t + 1))
                    nc.vector.bn_aggr(mv[:, t, :], st[:, t, :]).then_inc(ln_mv[i].sem, 1)

            def adjacency(b):
                dve.wait_ge(UA.filled, UA.done(("adjacency", b)))
                nc.vector.tensor_copy(sim[:, :], UA.tensor[:, :]).then_inc(UA.drained, 1)
                dve.wait_ge(ld_x.sem, ld_x.at(b, 16))
                stats(b, 0, xb)

            topk = [(r, what, t) for r in range(ROUNDS) for what in (["max", "strike"] if r < ROUNDS - 1 else ["max"])
                    for t in range(T)]

            def top_rounds(b, quarter):
                n0, n1 = (len(topk) * q // 4 for q in (quarter, quarter + 1))
                for n in range(n0, n1):
                    r, what, t = topk[n]
                    cur = (sim if r == 0 else wk)[:, t * S:(t + 1) * S]
                    best = top[:, t * 8:(t + 1) * 8]
                    if n < T:
                        dve.wait_ge(UA.drained, UA.done(("adjacency", b)))
                    else:
                        dve.wait_ge(topk_step.sem, topk_step.at(b, n - T + 1))
                    if what == "max":
                        nc.vector.max(best, cur).then_inc(topk_step.sem, 1)
                    else:
                        nc.vector.match_replace(wk[:, t * S:(t + 1) * S], best, cur, -3.0e38).then_inc(topk_step.sem, 1)

            def masked(b):
                dve.wait_ge(th1_ready.sem, th1_ready.at(b, 1))
                for t in range(T):
                    thr = top[:, t * 8 + (TOPK - 1) % 8:t * 8 + (TOPK - 1) % 8 + 1]
                    dve.wait_ge(topk_step.sem, topk_step.at(b, len(topk) - T + 1 + t))
                    nc.vector.scalar_tensor_tensor(am[:, t * S:(t + 1) * S], sim[:, t * S:(t + 1) * S], thr,
                                                   th[:, t * S:(t + 1) * S], ALU.is_ge, ALU.mult).then_inc(am_ready.sem, 1)

            def adjacency_out(b):
                key = ("adjacency_turn", b)
                dve.wait_ge(am_ready.sem, am_ready.at(b, T))
                dve.wait_ge(GA.filled, GA.done(key))
                nc.vector.tensor_tensor(am[:, :], am[:, :], GA.tensor[:, :], ALU.add).then_inc(GA.drained, 1)
                dve.wait_ge(GA.drained, GA.done(key))
                dve.wait_ge(y2_ready.sem, y2_ready.at(b, T))
                dve.wait_ge(gam_ready.sem, 2)
                nc.vector.scalar_tensor_tensor(x1[:, :], am[:, :], gam[:, 3:4], y2[:, :], ALU.mult, ALU.add).then_inc(x1_ready.sem, 1)
                dve.wait_ge(x1_ready.sem, x1_ready.at(b, 1))
                stats(b, 1, x1)

            def ffn_in(b):
                dve.wait_ge(xn_ready.sem, xn_ready.at(b, T))
                quantise(q_step.at(b, 0), hq_ready.at(b, 0), xn, qy[:, 0:512], qm[:, 0:512], 16)

            def ffn_up(b, u):
                key = ("ffn_up", b, u)
                t, half = divmod(u, 2)
                dve.wait_ge(thg_ready.sem, thg_ready.at(b, u + 1))
                nc.vector.scalar_tensor_tensor(sg[:, :], sg[:, :], 1.0, GA.tensor[:, :], ALU.add, ALU.mult).then_inc(GA.drained, 1)
                dve.wait_ge(GA.drained, GA.done(key))
                dve.wait_ge(UA.filled, UA.done(key))
                nc.vector.scalar_tensor_tensor(hid[:, half * 512:(half + 1) * 512], sg[:, :], 0.5, UA.tensor[:, :],
                                               ALU.mult, ALU.mult).then_inc(UA.drained, 1)
                if half == 1:
                    dve.wait_ge(UA.drained, UA.done(key))
                    quantise(q_step.at(b, 8 * (1 + t)), hq_ready.at(b, 1 + t), hid, qy, qm, 32)

            def ffn_down(b, t):
                dve.wait_ge(GA.filled, GA.done(("ffn_down", b, t)))
                if b >= 2:
                    dve.wait_ge(QC.drained, QC.done(("att_out", b - 2)))
                nc.vector.tensor_tensor(x2[b % 2][:, t * D:(t + 1) * D], x1[:, t * D:(t + 1) * D], GA.tensor[:, 0:D],
                                        ALU.add).then_inc(GA.drained, 1)
                if t == T - 1:
                    dve.wait_ge(GA.drained, GA.done(("ffn_down", b, t)))
                    stats(b, 2, x2[b % 2])

            def rotate(b, p):
                key = ("project", b, p)
                if p == 0:
                    dve.wait_ge(ld_tab.sem, 112)
                dve.wait_ge(QB.filled, QB.done(key))
                if p >= 1:
                    dve.wait_ge(QC.filled, QC.done(("to_keys", b, p - 1)))
                for g, tab in enumerate((cosq, sinq)):
                    nc.vector.tensor_tensor(qcs[:, g * J * S:(g + 1) * J * S], QB.tensor[:, 0:J * S], tab[:, :],
                                            ALU.mult).then_inc(qc_ready.sem if g == 0 else QB.drained, 1)

            def row_max(b, p):
                dve.wait_ge(SC.filled, SC.done(("scores", b, p)))
                nc.vector.tensor_reduce(nmax[:, 4 * (p % 2):4 * (p % 2) + 4], v3(SC.tensor[:, :], 4), AX_X, ALU.max,
                                        negate=True).then_inc(nmax_ready.sem, 1)

            def row_sum(b, p):
                o = 4 * (p % 2)
                dve.wait_ge(SC.drained, SC.done(("scores", b, p)))
                nc.vector.reciprocal(rsum[:, o:o + 4], ssum[:, o:o + 4]).then_inc(rsum_ready.sem, 1)

            def att_out(b):
                dve.wait_ge(QC.filled, QC.done(("att_out", b)))
                dve.wait_ge(o_ready.sem, o_ready.at(b, 0))
                nc.vector.tensor_tensor(x3, x2[b % 2][:, :], QC.tensor[:, :], ALU.add).then_inc(QC.drained, 1)
                dve.wait_ge(QC.drained, QC.done(("att_out", b)))
                stats(b, 3, x3)

            def routing(b):
                mx, es, wt, rm = (small[:, 96 + 2 * i:98 + 2 * i] for i in range(4))
                key = ("logits", b)

                def wide(s):
                    return s.unsqueeze(2).to_broadcast([P, T, E])
                dve.wait_ge(xhi_ready.sem, xhi_ready.at(b, 1))
                nc.vector.tensor_tensor(xlo[:, :], x4T, xhi[:, :], ALU.subtract).then_inc(xlo_ready.sem, 1)
                dve.wait_ge(QC.filled, QC.done(key))
                lg = v3(QC.tensor[:, 0:T * E], T)
                nc.vector.tensor_reduce(mx, lg, AX_X, ALU.max).then_inc(rt_step.sem, 1)
                dve.wait_ge(rt_step.sem, rt_step.at(b, 1))
                nc.vector.tensor_tensor(v3(df, T), lg, wide(mx), ALU.subtract).then_inc(rt_step.sem, 1)
                dve.wait_ge(rt_step.sem, rt_step.at(b, 2))
                nc.vector.scalar_tensor_tensor(rk, df, 0.0, rnk[:, :], ALU.is_equal, ALU.mult).then_inc(rt_step.sem, 1)
                dve.wait_ge(rt_step.sem, rt_step.at(b, 3))
                nc.vector.tensor_reduce(rm, v3(rk, T), AX_X, ALU.max).then_inc(QC.drained, 1)
                dve.wait_ge(QC.drained, QC.done(key))
                nc.vector.tensor_tensor(v3(rk, T), v3(rk, T), wide(rm), ALU.is_equal).then_inc(rt_step.sem, 1)
                dve.wait_ge(ex_done.sem, ex_done.at(b, 1))
                nc.vector.tensor_reduce(es, v3(ex, T), AX_X, ALU.add).then_inc(rt_step.sem, 1)
                dve.wait_ge(rt_step.sem, rt_step.at(b, 5))
                nc.vector.reciprocal(wt, es).then_inc(rt_step.sem, 1)
                dve.wait_ge(rt_step.sem, rt_step.at(b, 6))
                nc.vector.tensor_tensor(selw, v3(rk, T), wide(wt), ALU.mult).then_inc(rt_step.sem, 1)

            def expert(b, f):
                q, t = divmod(f, T)
                k = bank_of("expert", b, f)
                if f == 0:
                    dve.wait_ge(rt_step.sem, rt_step.at(b, 7))
                    dve.wait_ge(stored.sem, stored.at(b, 0))
                dve.wait_ge(k.filled, k.done(("expert", b, f)))
                for i in range(EF):
                    e, chain = EF * q + i, i % 2
                    src, w = k.tensor[:, i * D:(i + 1) * D], selw[:, t, e:e + 1]
                    if i >= 2:
                        dve.wait_ge(acc_step.sem, acc_step.at(b, 3 * f + i - 1))
                    elif q > 0 and i == 0:
                        dve.wait_ge(acc_step.sem, acc_step.at(b, 3 * (f - T) + 3))
                    elif q > 0:
                        before = bank_of("expert", b, f - T)
                        dve.wait_ge(before.drained, before.done(("expert", b, f - T)))
                    if q == 0 and i < 2:
                        ins = nc.vector.tensor_scalar(acc[:, t, chain], src, w, None, ALU.mult)
                    else:
                        ins = nc.vector.scalar_tensor_tensor(acc[:, t, chain], src, w, acc[:, t, chain], ALU.mult, ALU.add)
                    ins.then_inc(acc_step.sem if i < EF - 1 else k.drained, 1)
                if f == FILLS - 1:
                    dve.wait_ge(k.drained, k.done(("expert", b, f)))
                    nc.vector.tensor_tensor(acc[:, :, 0], acc[:, :, 0], acc[:, :, 1], ALU.add).then_inc(osum.sem, 1)

            dve.wait_ge(gam_t.sem, 1)
            nc.vector.tensor_scalar(gam[:, 2:3], gam[:, 1:2], -0.5, 0.5, ALU.mult, ALU.add).then_inc(gam_ready.sem, 1)
            nc.vector.tensor_scalar(gam[:, 3:4], gam[:, 1:2], 0.125, 0.125, ALU.mult, ALU.add).then_inc(gam_ready.sem, 1)
            adjacency(0)
            for quarter in range(4):
                top_rounds(0, quarter)
            masked(0)
            for m in range(3):
                dve.wait_ge(ld_nat[m].sem, 16)
                quantise(8 * m, m, nat[m], wqy, wqm, 64)
                if m == 0:
                    adjacency_out(0)
            ffn_in(0)
            dve.wait_ge(ld_moe.sem, 16)
            nc.vector.tensor_scalar(tern[:, :], tern[:, :], 2.0, ROUND_INT, ALU.mult, ALU.add).then_inc(tern_step.sem, 1)
            dve.wait_ge(tern_step.sem, 1)
            nc.vector.tensor_scalar(tern[:, :], tern[:, :], ROUND_INT, 1.0, ALU.subtract, ALU.min).then_inc(tern_step.sem, 1)
            dve.wait_ge(tern_step.sem, 2)
            nc.vector.tensor_scalar(tern[:, :], tern[:, :], -1.0, None, ALU.max).then_inc(tern_step.sem, 1)
            for u in range(4):
                ffn_up(0, u)
            for t in range(T):
                ffn_down(0, t)
            for b in range(B):
                more = b + 1 < B
                rotate(b, 0)
                if more:
                    adjacency(b + 1)
                if b >= 1:
                    att_out(b - 1)
                for p in range(PAIRS):
                    row_max(b, p)
                    if p + 1 < PAIRS:
                        rotate(b, p + 1)
                    row_sum(b, p)
                    if p >= 1 and b >= 1:
                        expert(b - 1, 2 * (p - 1))
                    if p == 0 and b >= 1:
                        routing(b - 1)
                    if more:
                        if p < 2:
                            top_rounds(b + 1, 2 * p)
                        for name, *args in BESIDE.get(p, ([], []))[0]:
                            if name in ("ffn_up", "ffn_down"):
                                {"ffn_up": ffn_up, "ffn_down": ffn_down}[name](b + 1, *args)
                    if p >= 1 and b >= 1:
                        expert(b - 1, 2 * (p - 1) + 1)
                    if more:
                        if p < 2:
                            top_rounds(b + 1, 2 * p + 1)
                        if p == 1:
                            masked(b + 1)
                        if p == 2:
                            adjacency_out(b + 1)
                        if p == 3:
                            ffn_in(b + 1)
                        for name, *args in BESIDE.get(p, ([], []))[1]:
                            if name == "ffn_up":
                                ffn_up(b + 1, *args)
                if b >= 1:
                    expert(b - 1, FILLS - 2)
                if more:
                    ffn_down(b + 1, 1)
                if b >= 1:
                    expert(b - 1, FILLS - 1)
            att_out(B - 1)
            routing(B - 1)
            for f in range(FILLS):
                expert(B - 1, f)

        @block.gpsimd
        def _(pool):
            def ts(dst, src, s1, s2, o1, o2=None):
                if o2 is None:
                    return nc.gpsimd.tensor_scalar(dst, src, s1, None, o1)
                return nc.gpsimd.tensor_scalar(dst, src, s1, s2, o1, o2)

            def dequant(q0, src, dst, blocks):
                pool.wait_ge(q_step.sem, q0 + 8)
                nc.gpsimd.tensor_tensor(v3(dst, blocks), v3(src, blocks),
                                        qsc[:, 0:blocks].unsqueeze(2).to_broadcast([P, blocks, BLK]),
                                        ALU.mult).then_inc(hq_ready.sem, 1)

            def rstd(b, i):
                _, mv, r, nb, a1, b1 = ln_small(i)
                step, ready = ln_step[i], ln_ready[i]
                pool.wait_ge(ln_mv[i].sem, ln_mv[i].at(b, T))
                ts(r, mv[:, :, 1], EPS, None, ALU.add).then_inc(step.sem, 1)
                ts(nb, mv[:, :, 0], -1.0, None, ALU.mult).then_inc(step.sem, 1)
                pool.wait_ge(step.sem, step.at(b, 2))
                nc.gpsimd.tensor_tensor(r, r, halfneg[:, :], ALU.pow).then_inc(step.sem, 1)
                pool.wait_ge(step.sem, step.at(b, 3))
                last = nc.gpsimd.tensor_tensor(nb, nb, r, ALU.mult)
                if i == 0:
                    last.then_inc(step.sem, 1)
                    pool.wait_ge(step.sem, step.at(b, 4))
                    ts(a1, r, gam[:, 2:3], 1.0, ALU.mult, ALU.add).then_inc(ready.sem, 1)
                    ts(b1, nb, gam[:, 2:3], None, ALU.mult).then_inc(ready.sem, 1)
                else:
                    last.then_inc(ready.sem, 1)

            def adjacency(b):
                pool.wait_ge(th_ready.sem, th_ready.at(b, 1))
                ts(th[:, :], th[:, :], 1.0, None, ALU.add).then_inc(th1_ready.sem, 1)
                rstd(b, 0)

            def ffn_in(b):
                if b >= 1:
                    pool.wait_ge(UA.filled, UA.done(("hidden_turn", b - 1, 1)))
                dequant(q_step.at(b, 0), qy[:, 0:512], hq[:, 0:512], 16)

            def ffn_up(b, t):
                pool.wait_ge(UA.filled, UA.done(("ffn_in", b) if t == 0 else ("hidden_turn", b, 0)))
                dequant(q_step.at(b, 8 * (1 + t)), qy, hq, 32)

            def keys(b):
                pool.wait_ge(ld_cxn.sem, ld_cxn.at(b, 16))
                pool.wait_ge(ld_tab.sem, 112)
                if b == 0:
                    pool.wait_ge(UA.filled, UA.done(("turn_w", 2, 3)))
                hw = DC // 2
                a, r = v3(kvtmp[:, 0:T * DC], T), v3(kvtmp[:, T * DC:2 * T * DC], T)
                c3, cs, sn = v3(cxn, T), v3(cosk[:, :], T), v3(sink[:, :], T)
                nc.gpsimd.tensor_tensor(a, c3, cs, ALU.mult).then_inc(kv_step.sem, 1)
                nc.gpsimd.tensor_tensor(r[:, :, 0:hw], c3[:, :, hw:DC], sn[:, :, 0:hw], ALU.mult).then_inc(kv_step.sem, 1)
                nc.gpsimd.tensor_tensor(r[:, :, hw:DC], c3[:, :, 0:hw], sn[:, :, hw:DC], ALU.mult).then_inc(kv_step.sem, 1)
                pool.wait_ge(kv_step.sem, kv_step.at(b, 3))
                if b >= 2:
                    pool.wait_ge(QB.filled, QB.done(("context", b - 2, PAIRS - 1)))
                k4 = kvns[b % 2].rearrange("p (t u d) -> p t u d", t=T, u=3)
                nc.gpsimd.tensor_tensor(k4[:, :, 0, :], a, r, ALU.add).then_inc(kv_step.sem, 1)
                nc.gpsimd.tensor_tensor(k4[:, :, 2, :], a, r, ALU.add).then_inc(kv_ready.sem, 1)

            def attention(b, p):
                o = 4 * (p % 2)
                pool.wait_ge(rsum_ready.sem, rsum_ready.at(b, p + 1))
                a = v3(attn[p % 2], 4)
                nc.gpsimd.tensor_tensor(a, a, rsum[:, o:o + 4].unsqueeze(2).to_broadcast([P, 4, S]),
                                        ALU.mult).then_inc(attn_ready.sem, 1)

            def result(b):
                o, o3 = v3(acc_rows, T)[:, :, 0:D], v3(x3, T)
                pool.wait_ge(osum.sem, osum.at(b, 1))
                nc.gpsimd.tensor_tensor(o, o, scl[:, :].unsqueeze(1).to_broadcast([P, T, D]), ALU.mult).then_inc(o_step.sem, 1)
                pool.wait_ge(o_step.sem, o_step.at(b, 1))
                nc.gpsimd.tensor_tensor(o, o, o3, ALU.add).then_inc(o_ready.sem, 1)
                pool.wait_ge(o_ready.sem, o_ready.at(b, 1))
                pool.dma_start(out[b].rearrange("(t p) d -> p t d", p=P), o).then_inc(stored.sem, 16)

            def expert_weights(n):
                we = wE[:, :].rearrange("p (c e o) -> p c e o", c=C, e=E)
                src = masks[:, (n % 2) * 1024:(n % 2 + 1) * 1024].rearrange("p (c e o) -> p c e o", c=C, e=EC)
                if n == 0:
                    pool.wait_ge(tern_step.sem, 3)
                    pool.wait_ge(SC.filled, SC.done(("fold_o", 3)))
                pool.wait_ge(ld_mask[n % 2].sem, 16 * (n // 2 + 1))
                for c in range(C):
                    last = nc.gpsimd.tensor_tensor(we[:, c, n * EC:(n + 1) * EC, :], src[:, c],
                                                   tern[:, c * D:(c + 1) * D].unsqueeze(1).to_broadcast([P, EC, D]),
                                                   ALU.mult, saturate=False)
                last.then_inc(mask_used.sem, 1)

            acc_rows = masks[:, 0:T * 2 * D]
            nc.gpsimd.memset(halfneg[:, :], -0.5).then_inc(half_ready.sem, 1)
            nc.gpsimd.memset(raw_kr, 0.0).then_inc(kr_zero.sem, 1)
            pool.wait_ge(half_ready.sem, 1)
            pool.wait_ge(gam_ready.sem, 2)
            adjacency(0)
            pool.wait_ge(SC.filled, SC.done(("fold_q", H // 2 - 1)))
            nc.gpsimd.memset(wM[:, :], 0.0).then_inc(m_zero.sem, 1)
            for m in range(3):
                dequant(8 * m, wqy, nat[m], 64)
                if m == 0:
                    rstd(0, 1)
            for i in range(2):
                last = nc.gpsimd.memset(kvns[i].rearrange("p (t u d) -> p t u d", t=T, u=3)[:, :, 1, :], 0.0)
            last.then_inc(kv_zero.sem, 1)
            pool.wait_ge(kv_zero.sem, 1)
            ffn_in(0)
            keys(0)
            for t in range(T):
                ffn_up(0, t)
            rstd(0, 2)
            for b in range(B):
                more = b + 1 < B
                if more:
                    adjacency(b + 1)
                if b >= 1:
                    rstd(b - 1, 3)
                for p in range(PAIRS):
                    if more and p == 3:
                        rstd(b + 1, 1)
                    attention(b, p)
                    if b == 0:
                        expert_weights(2 * p)
                        expert_weights(2 * p + 1)
                    if more and p == 1:
                        keys(b + 1)
                    if more and p == 3:
                        ffn_in(b + 1)
                    if more and p == 5:
                        ffn_up(b + 1, 0)
                    if more and p == 6:
                        ffn_up(b + 1, 1)
                if more:
                    rstd(b + 1, 2)
                if b >= 1:
                    result(b - 1)
            rstd(B - 1, 3)
            result(B - 1)
            pool.wait_ge(stored.sem, 16 * B)


def tables():
    def rope(length, dim):
        inv = (1.0 / 10000.0 ** (np.arange(0, dim, 2, dtype=np.float32) / np.float32(dim))).astype(np.float32)
        f = np.arange(length, dtype=np.float32)[:, None] * inv[None, :]
        return np.repeat(np.sin(f), 2, axis=-1).astype(np.float32), np.repeat(np.cos(f), 2, axis=-1).astype(np.float32)

    sin, cos = rope(S, DQ)
    half = DQ // 2
    sin = np.concatenate([sin[:, half:], -sin[:, :half]], axis=1)
    q = np.arange(J * P) % DQ
    tile = lambda a: np.ascontiguousarray(a[:, q].T.reshape(J, P, S).transpose(1, 0, 2).reshape(P, J * S))
    sin_k, cos_k = rope(S, DC)
    sin_k = np.concatenate([-sin_k[:, :DC // 2], sin_k[:, DC // 2:]], axis=1)
    nat = lambda a: np.ascontiguousarray(a.reshape(T, P, DC).transpose(1, 0, 2).reshape(P, T * DC))
    rank = np.ascontiguousarray(np.broadcast_to((E - np.arange(E, dtype=np.float32)), (P, T, E)).reshape(P, T * E))
    return {"cos_q": tile(cos), "sin_q": tile(sin), "cos_k": nat(cos_k), "sin_k": nat(sin_k),
            "ident": np.eye(P, dtype=np.float32), "rank": rank}


def layout(i):
    def a(name):
        return np.asarray(i[name])
    rows = lambda w: w.reshape(-1, P, w.shape[1]).transpose(1, 0, 2).reshape(P, -1)
    qr = a("L1_xattn_W_qr")
    qr2 = np.stack([qr, np.roll(qr, DQ // 2, axis=1)])
    out = {
        "x": a("x"), "ctx_nat": a("ctx_512"), "ctx_t": a("ctx_512").transpose(0, 2, 1),
        "adj_wq": a("L0_xattn_Wq").T, "adj_wk": a("L0_xattn_Wk").T, "gamma": a("L0_xattn_gamma_raw").reshape(1),
        "gate_w": rows(a("L0_ffn_gate_w")), "up_w": rows(a("L0_ffn_up_w")), "down_w": rows(a("L0_ffn_down_w")),
        "att_wq": rows(a("L1_xattn_Wq")),
        "kc_q": a("L1_xattn_w_kc_q").transpose(1, 0, 2).reshape(HK, H * DQ),
        "kc_kv": a("L1_xattn_w_kc_kv").transpose(1, 0, 2).reshape(HK, H * DC),
        "qr_t": qr2.transpose(0, 3, 1, 2).reshape(2 * R, H * DQ),
        "kr_t": a("L1_xattn_W_kr").transpose(2, 0, 1).reshape(R, H * DC),
        "wo_t": rows(a("L1_xattn_Wo").T),
        "moe_w": rows(a("L1_ffn_weight").T),
        "moe_scale": a("L1_ffn_scale"),
        "moe_masks": a("L1_ffn_expert_masks").reshape(NEC, EC, D, C, P).transpose(0, 4, 3, 1, 2).reshape(NEC, P, C * EC * D),
        "router": rows(a("L1_ffn_router_w").T),
    }
    out.update(tables())
    return {k: np.ascontiguousarray(v) for k, v in out.items()}


_INS = ["x", "ctx_nat", "ctx_t", "adj_wq", "adj_wk", "gamma", "gate_w", "up_w", "down_w", "att_wq", "kc_q", "kc_kv",
        "qr_t", "kr_t", "wo_t", "moe_w", "moe_scale", "moe_masks", "router", "cos_q", "sin_q", "cos_k", "sin_k",
        "ident", "rank"]


def kernel(**inputs):
    import concourse.bacc as _bacc
    from concourse.bass_utils import run_bass_kernel_spmd as _run

    nc = _bacc.Bacc("TRN2", target_bir_lowering=False, num_devices=1)
    laid = layout(inputs)
    arrays, args = {}, []
    for name in _INS:
        arrays[f"in_{name}"] = laid[name]
        args.append(nc.dram_tensor(f"in_{name}", laid[name].shape, mybir.dt.from_np(laid[name].dtype),
                                   kind="ExternalInput").ap())
    out = nc.dram_tensor("out_0", (B, S, D), F32, kind="ExternalOutput").ap()
    build(nc, *args, out)
    r = _run(nc, [arrays], core_ids=[0])
    return r.results[0]["out_0"]
```

```python
from contextlib import ExitStack

import numpy as np

import concourse.bass as bass
from concourse import mybir

P = 128
F32 = mybir.dt.float32
F16 = mybir.dt.float16
F8 = mybir.dt.float8e4
U32 = mybir.dt.uint32
ALU = mybir.AluOpType
ACT = mybir.ActivationFunctionType
AX_X = mybir.AxisListType.X

B, S, D = 4, 256, 256
T = S // P
C = D // P
DC = 64
TOPK = int(S * 0.3)
ROUNDS = (TOPK + 7) // 8
I = 1024
BLK = 32
H, HK, DQ, R = 16, 128, 192, 64
PAIRS = H // 2
J = 2 * DQ // P
E = 32
EC = 2
NEC = E // EC
EF = 4
EPS = 1e-5
FP8_MAX = 448.0
EXP_BITS = 0x7F800000
ROUND4 = 1.5 * 2.0 ** 20
MIN_NORMAL = 2.0 ** -6
ROUND_INT = 1.5 * 2.0 ** 23


class Count:

    def __init__(self, sem, per_batch, setup=0):
        self.sem, self.per_batch, self.setup = sem, per_batch, setup

    def at(self, b, k):
        return b * self.per_batch + self.setup + k


class Bank:

    def __init__(self, tensor, filled, drained):
        self.tensor, self.filled, self.drained, self.turn = tensor, filled, drained, {}

    def free(self, key):
        return self.turn[key]

    def done(self, key):
        return self.turn[key] + 1


def tensor_order():
    steps = [("adjacency", 0)]
    steps += [("fold_q", n) for n in range(H // 2)]
    steps += [("adjacency_turn", 0)]
    steps += [("fold_k", n) for n in range(2 * J)]
    steps += [("fold_o", n) for n in range(4)]
    steps += [("turn_w", m, n) for m in range(2) for n in range(4)]
    steps += [("ffn_in", 0)] + [("ffn_up", 0, u) for u in range(4)]
    steps += [("turn_w", 2, n) for n in range(4)]
    for t in range(T):
        steps += [("hidden_turn", 0, t), ("ffn_down", 0, t)]
    for b in range(B):
        more = b + 1 < B
        experts = experts_beside(b)
        steps += [("keys_turn", b), ("x_turn", b)]
        if b >= 2:
            steps += [("expert", b - 2, FILLS - 1)]
        steps += [("project_first", b, 0), ("project", b, 0)]
        if more:
            steps += [("adjacency", b + 1)]
        steps += [("to_keys", b, 0), ("project_first", b, 1), ("project", b, 1)]
        if b >= 1:
            steps += [("att_out", b - 1)]
        for p in range(PAIRS):
            first, second = BESIDE[min(b, 1)][p] if more else ([], [])
            steps += [("scores", b, p)]
            if p >= 1:
                steps += [("context", b, p - 1)]
            if p + 1 < PAIRS:
                steps += [("to_keys", b, p + 1)]
            if p + 2 < PAIRS:
                steps += [("project_first", b, p + 2)]
            steps += [("expert", b - 1, f) for f in experts[p][0]]
            if p + 2 < PAIRS:
                steps += [("project", b, p + 2)]
            if p == 0 and b >= 1:
                steps += [("moe_turn", b - 1)]
            steps += [(name, b + 1, *args) for name, *args in first]
            steps += [("expert", b - 1, f) for f in experts[p][1]]
            steps += [("attn_turn", b, p, 0)]
            if p == 0 and b >= 1:
                steps += [("logits", b - 1)]
            steps += [("expert", b - 1, f) for f in experts[p][2]]
            steps += [(name, b + 1, *args) for name, *args in second]
            steps += [("expert", b - 1, f) for f in experts[p][3]]
            steps += [("attn_turn", b, p, 1)]
        if b >= 1:
            steps += [("expert", b - 1, FILLS - 2)]
        steps += [("context", b, PAIRS - 1)]
    steps += [("expert", B - 2, FILLS - 1), ("att_out", B - 1), ("moe_turn", B - 1), ("logits", B - 1)]
    steps += [("expert", B - 1, f) for f in range(FILLS)]
    return steps


BESIDE = [{
    0: ([], []),
    1: ([], []),
    2: ([], [('adjacency_turn',)]),
    3: ([], []),
    4: ([('ffn_in',)], [('ffn_up', 0), ('ffn_up', 1)]),
    5: ([('ffn_up', 2)], [('ffn_up', 3)]),
    6: ([('hidden_turn', 0)], []),
    7: ([('ffn_down', 0), ('hidden_turn', 1)], [('ffn_down', 1)]),
}, {
    0: ([], []),
    1: ([], []),
    2: ([('adjacency_turn',)], []),
    3: ([], []),
    4: ([('ffn_in',)], [('ffn_up', 0), ('ffn_up', 1)]),
    5: ([('ffn_up', 2)], [('ffn_up', 3)]),
    6: ([('hidden_turn', 0)], [('ffn_down', 0)]),
    7: ([('hidden_turn', 1)], [('ffn_down', 1)]),
}]
VECTOR_BESIDE = [{
    0: ([], [], [('top', 0), ('top', 1)], [('top', 2)], [('top', 3)]),
    1: ([], [], [('top', 4)], [('top', 5)], []),
    2: ([('top', 6)], [('top', 7)], [('masked',), ('adjacency_out',)], [], []),
    3: ([], [], [], [('ffn_in',)], []),
    4: ([], [], [('ffn_up', 0)], [], [('ffn_up', 1), ('round', 0, 0)]),
    5: ([], [('round', 0, 1), ('ffn_up', 2)], [], [], [('ffn_up', 3)]),
    6: ([], [('round', 1, 0)], [('round', 1, 1)], [], []),
    7: ([], [], [], [('ffn_down', 0)], [('ffn_down', 1)]),
}, {
    0: ([('top', 0), ('top', 1)], [], [], [], [('top', 2)]),
    1: ([('top', 3)], [('top', 4)], [('top', 5)], [], [('top', 6)]),
    2: ([('top', 7)], [('masked',)], [], [], []),
    3: ([('adjacency_out',)], [], [], [('ffn_in',)], []),
    4: ([], [], [('ffn_up', 0)], [('ffn_up', 1)], [('round', 0, 0)]),
    5: ([], [('round', 0, 1), ('ffn_up', 2)], [], [], []),
    6: ([('ffn_up', 3)], [('round', 1, 0)], [('round', 1, 1)], [], [('ffn_down', 0)]),
    7: ([], [], [], [], [('ffn_down', 1)]),
}]
POOL_BESIDE = [{
    0: ([], [('expert_weights', 0), ('expert_weights', 1)]),
    1: ([('expert_weights', 2), ('expert_weights', 3)], [('expert_weights', 4)]),
    2: ([('keys',)], [('expert_weights', 5), ('expert_weights', 6), ('rstd', 1)]),
    3: ([('expert_weights', 7)], [('ffn_in',)]),
    4: ([('expert_weights', 8)], []),
    5: ([('expert_weights', 9), ('expert_weights', 10), ('expert_weights', 11)], [('ffn_up', 0)]),
    6: ([('expert_weights', 12)], [('expert_weights', 13), ('ffn_up', 1)]),
    7: ([], [('expert_weights', 14), ('expert_weights', 15)]),
}, {
    0: ([], []),
    1: ([], []),
    2: ([], [('keys',), ('rstd', 1)]),
    3: ([], [('ffn_in',)]),
    4: ([], []),
    5: ([('ffn_up', 0)], []),
    6: ([('ffn_up', 1)], []),
    7: ([], []),
}]
NORM_STEP = [3, 3]
EXPERTS_LAST = [
    ([], [0], [1], []),
    ([], [], [2], [3]),
    ([4], [], [], [5]),
    ([], [6], [], [7]),
    ([], [8], [9], []),
    ([10], [], [11], []),
    ([12], [13], [], []),
]
EXPERTS = [
    ([], [], [0], []),
    ([], [], [], [1]),
    ([], [2], [3], [4]),
    ([], [5], [], []),
    ([], [6], [7], [8]),
    ([9], [], [], [10]),
    ([], [11, 12], [], [13]),
]


def experts_beside(b):
    none = ([], [], [], [])
    if b == 0:
        return [none] * PAIRS
    return [none] + (EXPERTS_LAST if b == B - 1 else EXPERTS)


FILLS = T * E // EF


def banks_of(name, *args):
    if name == "fold_q":
        return [("S0", "S1"), ("GA", "UA")][args[0] % 2]
    if name == "fold_o":
        return [("QC", "S0")[args[0] % 2]]
    if name == "fold_k":
        return [("TP", "QC")[args[0] % 2]]
    if name == "attn_turn" and args[2] == 1 and args[1] < 4 and args[0] < B - 1:
        return ["UA"]
    if name == "project_first":
        return []
    if name == "turn_w":
        return [("GA", "UA")[args[1] % 2]]
    if name == "expert":
        return ("GA", "UA") if args[0] >= B - 2 and args[1] % T == 0 else ("S0", "S1")
    return {
        "adjacency": ["GA", "UA"], "adjacency_turn": ["GA"], "ffn_in": ["UA"], "ffn_up": ["GA", "UA"],
        "hidden_turn": ["GA", "UA"], "ffn_down": ["GA"], "keys_turn": ["TP"], "x_turn": ["TP"],
        "project": ["QB"], "to_keys": ["QC"], "scores": ["S0", "S1"], "attn_turn": ["TP"], "context": ["QB"],
        "att_out": ["QC"], "moe_turn": ["TP"], "logits": ["QC"],
    }[name]


def build(nc, x, ctx_nat, ctx_t, adj_wq, adj_wk, gamma, gate_w, up_w, down_w, att_wq, kc_q, kc_kv,
          qr_t, kr_t, wo_t, moe_w, moe_scale, moe_masks, router, cos_q, sin_q, cos_k, sin_k, ident,
          rank, out):
    ctx = ExitStack()
    with ctx:
        def sb(name, cols, dt=F32, parts=P):
            return ctx.enter_context(nc.sbuf_tensor(name, [parts, cols], dt))

        def count(name, per_batch, setup=0):
            return Count(ctx.enter_context(nc.semaphore(name)), per_batch, setup)

        def bank(name, cols):
            return Bank(ctx.enter_context(nc.psum_tensor(name, [P, cols], F32)),
                        ctx.enter_context(nc.semaphore(name + "_filled")),
                        ctx.enter_context(nc.semaphore(name + "_drained")))

        def v3(ap, n):
            return ap.rearrange("p (a b) -> p a b", a=n)

        wA_hi, wA_lo = (sb(n, C * H * DQ, F16) for n in ("wA_hi", "wA_lo"))
        wM = sb("wM", 2 * PAIRS * J * P)
        wF = sb("wF", PAIRS * D)
        wG = sb("wG", C * I)
        wU = sb("wU", C * I)
        wD = sb("wD", (I // P) * D)
        wE = sb("wE", C * E * D, F8)
        cosq = sb("cosq", J * S)
        sinq = sb("sinq", J * S)
        cosk = sb("cosk", T * DC)
        sink = sb("sink", T * DC)
        idn = sb("idn", P)
        scl = sb("scl", D)
        tern = sb("tern", C * D)
        rtr = sb("rtr", C * E)
        rnk = sb("rnk", T * E)
        awq = sb("awq", DC, parts=DC)
        awk = sb("awk", DC, parts=DC)
        gam = sb("gam", 4)
        halfneg = sb("halfneg", T)
        masks = sb("masks", 2 * C * EC * D)

        xb = sb("xb", T * D)
        cxt = sb("cxt", S, parts=DC)
        qk0 = sb("qk0", 2 * S, parts=DC)
        sim = sb("sim", T * S)
        wk = sb("wk", T * S)
        am = wk
        th = sb("th", T * S)
        y2 = sb("y2", T * D)
        x1 = y2
        x2 = [sb(f"x2_{i}", T * D) for i in range(2)]
        top = sb("top", T * 8)
        ffn = sb("ffn", 6144)
        hid, qy, qm, hq = (ffn[:, i * I:(i + 1) * I] for i in range(4))
        hqT = ffn[:, 4096:5120]
        xn = ffn[:, 5120:5632]
        xqT = ffn[:, 5632:6144]
        sg = sb("sg", 512)
        small = sb("small", 128)
        amax, qsc, qrs = (sb(n, 64) for n in ("amax", "qsc", "qrs"))
        wsc = sb("wsc", 128)

        reg = sb("reg", 11264)
        at = [0]

        def part(cols):
            at[0] += cols
            return reg[:, at[0] - cols:at[0]]
        cxn = part(T * DC)
        kvns = [part(T * 2 * DC) for _ in range(2)]
        key_hi, key_lo = (part(S // 2).bitcast(F16) for _ in range(2))
        xT_hi, xT_lo = (part(C * S // 2).bitcast(F16) for _ in range(2))
        qk = part(S).bitcast(F16)
        qcs = part(2 * J * S)
        attn = [part(4 * S) for _ in range(2)]
        attT = part(4 * S)
        cT = part(PAIRS * S)
        x3 = part(T * D)
        xnat = part(C * S)
        kvtmp = part(T * DC * 2)
        xhi = sb("xhi", C * S, F16)
        xlo = sb("xlo", C * S, F16)
        scaled = [masks[:, 3 * T * D:4 * T * D], tern[:, :]]
        acc = masks[:, 0:T * 2 * D].rearrange("p (t k d) -> p t k d", t=T, k=2)
        x4T = masks[:, T * 2 * D:T * 2 * D + C * S]
        nmax = sb("nmax", 8)
        ssum = sb("ssum", 8)
        rsum = sb("rsum", 8)
        route = sb("route", 4 * T * E)
        selw = v3(route[:, 0:T * E], T)
        ex, df, rk = (route[:, i * T * E:(i + 1) * T * E] for i in range(1, 4))

        raw_q = reg[:, 0:H * DQ]
        raw_qr = reg[:, 3072:3072 + H * DQ]
        raw_kv = reg[:, 6144:6144 + H * DC]
        raw_kr = reg[:, 7168:7168 + H * 2 * DC]
        raw_wq = wM[:, 0:H * D]
        raw_wo = wE[:, :].bitcast(F32)
        nat = [wU[:, :], wD[:, :], reg[:, 9216:11264]]
        wmag = [ffn[:, 0:2048], masks[:, :], reg[:, 3072:5120]]
        wA_full = [ffn[:, 2048:2816], ffn[:, 2816:3584]]
        wscale = [wsc[:, 0:64], wsc[:, 64:128]]

        QB = bank("qb", 1024)
        S0 = bank("s0", 512)
        S1 = bank("s1", 512)
        QC = bank("qc", 512)
        TP = bank("tp", 512)
        GA = bank("ga", 512)
        UA = bank("ua", 512)
        by_name = {"QB": QB, "S0": S0, "S1": S1, "QC": QC, "TP": TP, "GA": GA, "UA": UA}
        order = tensor_order()
        for step in order:
            for name in banks_of(*step):
                turns = by_name[name].turn
                turns[step] = len(turns)

        def bank_of(*step):
            return by_name[banks_of(*step)[0]]

        def both_banks(*step):
            return [by_name[name] for name in banks_of(*step)]

        ld_x, ld_cxt, ld_cxn = (count(n, 16) for n in ("ld_x", "ld_cxt", "ld_cxn"))
        ld_adj = count("ld_adj", 0, 16 * 4)
        ld_nat = [count(f"ld_nat{i}", 0, 16) for i in range(3)]
        ld_fold_q = count("ld_fold_q", 0, 16 * 2)
        ld_fold_k = count("ld_fold_k", 0, 16 * 3)
        ld_fold_o = count("ld_fold_o", 0, 16 * 2)
        ld_tab = count("ld_tab", 0, 16 * 7)
        ld_moe = count("ld_moe", 0, 16)
        ld_mask = [count(f"ld_mask{i}", 0) for i in range(2)]
        stored = count("stored", 16)
        half_ready = count("half_ready", 0, 1)
        kr_zero = count("kr_zero", 0, 1)
        m_zero = count("m_zero", 0, 2)
        wA_copy = count("wA_copy", 0, C * H // 2)
        wA_ready = count("wA_ready", 0, H // 2)
        gam_t = count("gam_t", 0, 1)
        gam_ready = count("gam_ready", 0, 2)
        w0 = [0, 7, 15, 22]
        w_step = count("w_step", 0, w0[-1])
        w_rounded = count("w_rounded", 0, 2)
        w_ready = count("w_ready", 0, 3)
        tern_step = count("tern_step", 0, 3)
        mask_used = count("mask_used", 0, NEC)
        ln_stats = [count(f"ln{i}_stats", 2) for i in range(4)]
        ln_mv = [count(f"ln{i}_mv", 2) for i in range(4)]
        ln_step = [count(f"ln{i}_step", 4 if i == 0 else 3) for i in range(4)]
        ln_ready = [count(f"ln{i}_ready", 2 if i == 0 else 1) for i in range(4)]
        th_ready = count("th_ready", 1)
        th1_ready = count("th1_ready", 1)
        topk_step = count("topk_step", T * (2 * ROUNDS - 1))
        am_ready = count("am_ready", T)
        y2_ready = count("y2_ready", T)
        x1_ready = count("x1_ready", 1)
        xn_ready = count("xn_ready", T)
        q_step = count("q_step", 8 * 3)
        hq_ready = count("hq_ready", 3)
        thg_ready = count("thg_ready", 4)
        xn3_ready = count("xn3_ready", T)
        kv_step = count("kv_step", 4)
        kv_ready = count("kv_ready", 1)
        key_hi_ready = count("key_hi_ready", 1)
        xT_hi_ready = count("xT_hi_ready", 1)
        qk_hi_ready = count("qk_hi_ready", 2 * PAIRS)
        qk_lo_ready = count("qk_lo_ready", PAIRS)
        qc_ready = count("qc_ready", PAIRS)
        nmax_ready = count("nmax_ready", 2 * PAIRS)
        exp_done = count("exp_done", 2 * PAIRS)
        rsum_ready = count("rsum_ready", PAIRS)
        attn_ready = count("attn_ready", 2 * PAIRS)
        xn4_ready = count("xn4_ready", T)
        xhi_ready = count("xhi_ready", 1)
        xlo_ready = count("xlo_ready", 1)
        rt_step = count("rt_step", 7)
        ex_done = count("ex_done", 1)
        acc_step = count("acc_step", 2 * FILLS // T)
        summed = count("summed", FILLS - 1)
        osum = count("osum", 1)
        o_step = count("o_step", 1)
        o_ready = count("o_ready", 1)
        last_step = count("last_step", 0, 3)
        stored_last = count("stored_last", 0, 32)

        block = ctx.enter_context(nc.Block())

        def ln_small(i):
            o = 24 * i
            st = small[:, o:o + 12].rearrange("p (t s) -> p t s", t=T)
            mv = small[:, o + 12:o + 16].rearrange("p (t s) -> p t s", t=T)
            return st, mv, small[:, o + 16:o + 18], small[:, o + 18:o + 20], small[:, o + 20:o + 22], small[:, o + 22:o + 24]

        @block.sync
        def _(sp):
            def load_a(b):
                sp.wait_ge(y2_ready.sem, y2_ready.at(b, 0))
                sp.dma_start(v3(xb[:, :], T), x[b].rearrange("(t p) d -> p t d", p=P)).then_inc(ld_x.sem, 16)
                if b >= 1:
                    sp.wait_ge(GA.filled, GA.done(("adjacency", b - 1)))
                sp.dma_start(cxt[:, :], ctx_t[b]).then_inc(ld_cxt.sem, 16)

            def load_b(b):
                if b == 0:
                    sp.wait_ge(UA.filled, UA.done(("fold_q", H // 2 - 1)))
                else:
                    sp.wait_ge(kv_ready.sem, kv_ready.at(b, 0))
                sp.dma_start(v3(cxn, T), ctx_nat[b].rearrange("(t p) d -> p t d", p=P)).then_inc(ld_cxn.sem, 16)

            sp.dma_start(awq[:, :], adj_wq).then_inc(ld_adj.sem, 16)
            sp.dma_start(awk[:, :], adj_wk).then_inc(ld_adj.sem, 16)
            load_a(0)
            sp.dma_start(gam[:, 0:1], gamma.partition_broadcast(P)).then_inc(ld_adj.sem, 16)
            sp.dma_start(idn[:, :], ident).then_inc(ld_adj.sem, 16)
            sp.dma_start(raw_wq, att_wq).then_inc(ld_fold_q.sem, 16)
            sp.dma_start(raw_q, kc_q).then_inc(ld_fold_q.sem, 16)
            sp.dma_start(nat[0], gate_w).then_inc(ld_nat[0].sem, 16)
            sp.dma_start(nat[1], up_w).then_inc(ld_nat[1].sem, 16)
            sp.dma_start(raw_qr, qr_t).then_inc(ld_fold_k.sem, 16)
            sp.wait_ge(kr_zero.sem, 1)
            for g in range(2):
                sp.dma_start(v3(raw_kr[g * R:(g + 1) * R, :], H)[:, :, g * DC:(g + 1) * DC], v3(kr_t, H))\
                    .then_inc(ld_fold_k.sem, 16)
            sp.dma_start(nat[2], down_w).then_inc(ld_nat[2].sem, 16)
            sp.dma_start(raw_kv, kc_kv).then_inc(ld_fold_o.sem, 16)
            sp.dma_start(raw_wo, wo_t).then_inc(ld_fold_o.sem, 16)
            sp.dma_start(tern[:, :], moe_w).then_inc(ld_moe.sem, 16)
            for dst, src in ((cosq, cos_q), (sinq, sin_q), (cosk, cos_k), (sink, sin_k), (rtr, router), (rnk, rank)):
                sp.dma_start(dst[:, :], src).then_inc(ld_tab.sem, 16)
            sp.dma_start(scl[:, :], moe_scale.partition_broadcast(P)).then_inc(ld_tab.sem, 16)
            load_b(0)
            load_a(1)
            sp.wait_ge(w_ready.sem, 2)
            for n in range(NEC):
                if n == 2:
                    load_b(1)
                if n >= 2:
                    sp.wait_ge(mask_used.sem, n - 1)
                sp.dma_start(masks[:, (n % 2) * 1024:(n % 2 + 1) * 1024], moe_masks[n]).then_inc(ld_mask[n % 2].sem, 16)
            for b in range(2, B):
                load_a(b)
                load_b(b)
            sp.wait_ge(o_ready.sem, o_ready.at(B - 1, 1))
            sp.dma_start(out[B - 1, 0:P], acc[:, 0, 0]).then_inc(stored_last.sem, 16)
            sp.wait_ge(last_step.sem, 3)
            sp.dma_start(out[B - 1, P:S], acc[:, 1, 0]).then_inc(stored_last.sem, 16)
            sp.wait_ge(stored.sem, 16 * (B - 1))
            sp.wait_ge(stored_last.sem, 32)

        @block.tensor
        def _(pe):
            def mm(dst, lhsT, rhs, start=True, stop=True, check=True):
                return nc.tensor.matmul(dst, lhsT, rhs, start=start, stop=stop, skip_group_check=not check)

            def turn(dst, src):
                return nc.tensor.transpose(dst, src, idn[:, :])

            def fold_q(n):
                if n == 0:
                    pe.wait_ge(ld_fold_q.sem, 32)
                for c, k in enumerate(both_banks("fold_q", n)):
                    pe.wait_ge(k.drained, k.free(("fold_q", n)))
                    for hh in range(2):
                        h = 2 * n + hh
                        last = mm(k.tensor[:, hh * DQ:(hh + 1) * DQ],
                                  raw_wq[:, h * D + c * P:h * D + (c + 1) * P], raw_q[:, h * DQ:(h + 1) * DQ])
                    last.then_inc(k.filled, 1)

            def fold_k(n):
                j, half = divmod(n, 2)
                k = bank_of("fold_k", n)
                if n == 0:
                    pe.wait_ge(ld_fold_k.sem, 48)
                pe.wait_ge(k.drained, k.free(("fold_k", n)))
                for a in range(4):
                    o = k.tensor[:, a * P:(a + 1) * P]
                    parts = {0: ((0, 0, 0, P),), 1: ((0, 0, P, 64), (1, 64, 0, 64)), 2: ((1, 0, DC, P),)}[j]
                    for hh, lo, q0, w in parts:
                        h = 2 * (4 * half + a) + hh
                        last = mm(o[lo:lo + w, :], raw_qr[:, h * DQ + q0:h * DQ + q0 + w], raw_kr[:, h * P:(h + 1) * P])
                last.then_inc(k.filled, 1)

            def fold_o(n):
                k = bank_of("fold_o", n)
                if n == 0:
                    pe.wait_ge(ld_fold_o.sem, 32)
                pe.wait_ge(k.drained, k.free(("fold_o", n)))
                for pp in range(2):
                    for hh in range(2):
                        h = 4 * n + 2 * pp + hh
                        last = mm(k.tensor[hh * 64:(hh + 1) * 64, pp * D:(pp + 1) * D],
                                  raw_kv[:, h * DC:(h + 1) * DC], raw_wo[:, h * D:(h + 1) * D])
                last.then_inc(k.filled, 1)

            def turn_w(m, n):
                k = bank_of("turn_w", m, n)
                pe.wait_ge(w_ready.sem, m + 1)
                pe.wait_ge(k.drained, k.free(("turn_w", m, n)))
                for a in range(4):
                    if m < 2:
                        c, half = divmod(n, 2)
                        src = nat[m][:, (4 * half + a) * D + c * P:(4 * half + a) * D + (c + 1) * P]
                    else:
                        j, ot = 2 * n + a // 2, a % 2
                        src = nat[m][:, ot * I + j * P:ot * I + (j + 1) * P]
                    last = turn(k.tensor[:, a * P:(a + 1) * P], src)
                last.then_inc(k.filled, 1)

            def adjacency(b):
                key = ("adjacency", b)
                if b == 0:
                    pe.wait_ge(ld_adj.sem, 64)
                pe.wait_ge(ld_cxt.sem, ld_cxt.at(b, 16))
                pe.wait_ge(GA.drained, GA.free(key))
                mm(GA.tensor[0:DC, 0:S], awq[:, :], cxt[:, :])
                mm(GA.tensor[0:DC, S:2 * S], awk[:, :], cxt[:, :]).then_inc(GA.filled, 1)
                pe.wait_ge(GA.drained, GA.done(key))
                pe.wait_ge(UA.drained, UA.free(key))
                for t in range(T):
                    last = mm(UA.tensor[:, t * S:(t + 1) * S], qk0[:, t * P:(t + 1) * P], qk0[:, S:2 * S])
                last.then_inc(UA.filled, 1)

            def adjacency_turn(b):
                pe.wait_ge(am_ready.sem, am_ready.at(b, T))
                pe.wait_ge(GA.drained, GA.free(("adjacency_turn", b)))
                for r in range(T):
                    for c in range(T):
                        last = turn(GA.tensor[:, r * S + c * P:r * S + (c + 1) * P], am[:, c * S + r * P:c * S + (r + 1) * P])
                last.then_inc(GA.filled, 1)

            def ffn_in(b):
                pe.wait_ge(hq_ready.sem, hq_ready.at(b, 1))
                pe.wait_ge(UA.drained, UA.free(("ffn_in", b)))
                for c in range(C):
                    for t in range(T):
                        last = turn(UA.tensor[:, c * S + t * P:c * S + (t + 1) * P], hq[:, t * D + c * P:t * D + (c + 1) * P])
                last.then_inc(UA.filled, 1)

            def ffn_up(b, u):
                key = ("ffn_up", b, u)
                t, half = divmod(u, 2)
                if u == 0:
                    pe.wait_ge(UA.drained, UA.done(("ffn_in", b)))
                if b == 0 and u == 0:
                    pe.wait_ge(GA.drained, GA.done(("turn_w", 1, 2)))
                for k, w in ((GA, wG), (UA, wU)):
                    pe.wait_ge(k.drained, k.free(key))
                    for c in range(C):
                        last = mm(k.tensor[:, :], xqT[:, c * S + t * P:c * S + (t + 1) * P],
                                  w[:, c * I + half * 512:c * I + (half + 1) * 512], c == 0, c == C - 1)
                    last.then_inc(k.filled, 1)

            def hidden_turn(b, t):
                key = ("hidden_turn", b, t)
                pe.wait_ge(hq_ready.sem, hq_ready.at(b, 2 + t))
                for k, j0 in ((GA, 0), (UA, 4)):
                    pe.wait_ge(k.drained, k.free(key))
                    for j in range(4):
                        last = turn(k.tensor[:, j * P:(j + 1) * P], hq[:, (j0 + j) * P:(j0 + j + 1) * P])
                    last.then_inc(k.filled, 1)

            def ffn_down(b, t):
                pe.wait_ge(GA.drained, GA.free(("ffn_down", b, t)))
                if b == 0 and t == 0:
                    pe.wait_ge(UA.drained, UA.done(("turn_w", 2, 3)))
                pe.wait_ge(UA.drained, UA.done(("hidden_turn", b, t)))
                for j in range(I // P):
                    last = mm(GA.tensor[:, 0:D], hqT[:, j * P:(j + 1) * P], wD[:, j * D:(j + 1) * D], j == 0, j == I // P - 1)
                last.then_inc(GA.filled, 1)

            def keys_turn(b):
                kvn = kvns[b % 2]
                pe.wait_ge(kv_ready.sem, kv_ready.at(b, 1))
                pe.wait_ge(TP.drained, TP.free(("keys_turn", b)))
                for t in range(T):
                    last = turn(TP.tensor[:, t * P:(t + 1) * P], kvn[:, t * P:(t + 1) * P])
                last.then_inc(TP.filled, 1)

            def turn_x(key, ready):
                b = key[1]
                pe.wait_ge(ready.sem, ready.at(b, T))
                pe.wait_ge(TP.drained, TP.free(key))
                for c in range(C):
                    for t in range(T):
                        last = turn(TP.tensor[:, c * S + t * P:c * S + (t + 1) * P], xnat[:, t * D + c * P:t * D + (c + 1) * P])
                last.then_inc(TP.filled, 1)

            def x_turn(b):
                turn_x(("x_turn", b), xn3_ready)

            def moe_turn(b):
                turn_x(("moe_turn", b), xn4_ready)

            def project_tile(p, j, x_turned=None):
                parts = [(wx, xx, c) for wx, xx in ((wA_hi, xT_hi), (wA_lo, xT_hi), (wA_hi, xT_lo)) for c in range(C)]
                for i, (wx, xx, c) in enumerate(parts):
                    if x_turned is not None and i == 2 * C:
                        pe.wait_ge(TP.drained, TP.done(x_turned))
                    o = c * H * DQ + (J * p + j) * P
                    last = mm(QB.tensor[:, j * S:(j + 1) * S], wx[:, o:o + P], xx[:, c * S:(c + 1) * S],
                              i == 0, i == len(parts) - 1)
                return last

            def project_first(b, p):
                if p == 0:
                    pe.wait_ge(xT_hi_ready.sem, xT_hi_ready.at(b, 1))
                    if b == 0:
                        pe.wait_ge(wA_ready.sem, H // 2)
                pe.wait_ge(QB.drained, QB.free(("project", b, p)))
                project_tile(p, 0, ("x_turn", b) if p == 0 else None)

            def project(b, p):
                for j in range(1, J):
                    last = project_tile(p, j)
                last.then_inc(QB.filled, 1)

            def to_keys(b, p):
                pe.wait_ge(QB.drained, QB.done(("project", b, p)))
                pe.wait_ge(QC.drained, QC.free(("to_keys", b, p)))
                o = QC.tensor
                def w(g, j):
                    m0 = ((g * PAIRS + p) * J + j) * P
                    return wM[:, m0:m0 + P]
                def q(g, j):
                    return qcs[:, (g * J + j) * S:(g * J + j + 1) * S]
                mm(o[:, 0:S], w(0, 1), q(0, 1), True, False, check=False)
                mm(o[:, 0:S], w(1, 1), q(1, 1), False, False, check=False)
                for g in range(2):
                    mm(o[0:DC, 0:S], w(g, 0)[:, 0:DC], q(g, 0), False, False, check=False)
                    last = mm(o[DC:P, 0:S], w(g, 2)[:, DC:P], q(g, 2), False, g == 1, check=False)
                last.then_inc(QC.filled, 1)

            def scores(b, p):
                pe.wait_ge(QC.drained, QC.done(("to_keys", b, p)))
                for hh, k in enumerate((S0, S1)):
                    pe.wait_ge(k.drained, k.free(("scores", b, p)))
                    for t in range(T):
                        o = t * S
                        q = qk[:, hh * S + t * P:hh * S + (t + 1) * P]
                        mm(k.tensor[:, o:o + S], q, key_hi[:, :], True, False)
                        last = mm(k.tensor[:, o:o + S], q, key_lo[:, :], False, True)
                    last.then_inc(k.filled, 1)

            def attn_turn(b, p, hh):
                pe.wait_ge(attn_ready.sem, attn_ready.at(b, 2 * p + hh + 1))
                k = bank_of("attn_turn", b, p, hh)
                pe.wait_ge(k.drained, k.free(("attn_turn", b, p, hh)))
                for c in range(T):
                    for t in range(T):
                        last = turn(k.tensor[:, c * S + t * P:c * S + (t + 1) * P],
                                    attn[p % 2][:, (2 * hh + t) * S + c * P:(2 * hh + t) * S + (c + 1) * P])
                last.then_inc(k.filled, 1)

            def context(b, p):
                kvn = kvns[b % 2]
                for hh in range(2):
                    k = bank_of("attn_turn", b, p, hh)
                    pe.wait_ge(k.drained, k.done(("attn_turn", b, p, hh)))
                pe.wait_ge(QB.drained, QB.free(("context", b, p)))
                for hh in range(2):
                    for c in range(T):
                        last = mm(QB.tensor[DC * hh:DC * (hh + 1), 0:S], kvn[:, c * 2 * DC:c * 2 * DC + DC],
                                  attT[:, (2 * hh + c) * S:(2 * hh + c + 1) * S], c == 0, c == T - 1)
                last.then_inc(QB.filled, 1)

            def att_out(b):
                pe.wait_ge(QB.drained, QB.done(("context", b, PAIRS - 1)))
                pe.wait_ge(QC.drained, QC.free(("att_out", b)))
                for t in range(T):
                    for p in range(PAIRS):
                        last = mm(QC.tensor[:, t * D:(t + 1) * D], cT[:, p * S + t * P:p * S + (t + 1) * P],
                                  wF[:, p * D:(p + 1) * D], p == 0, p == PAIRS - 1)
                last.then_inc(QC.filled, 1)

            def logits(b):
                pe.wait_ge(TP.drained, TP.done(("moe_turn", b)))
                pe.wait_ge(QC.drained, QC.free(("logits", b)))
                for t in range(T):
                    for c in range(C):
                        last = mm(QC.tensor[:, t * E:(t + 1) * E], x4T[:, c * S + t * P:c * S + (t + 1) * P],
                                  rtr[:, c * E:(c + 1) * E], c == 0, c == C - 1)
                last.then_inc(QC.filled, 1)

            def expert(b, f):
                q, t = divmod(f, T)
                if f == 0:
                    pe.wait_ge(mask_used.sem, NEC)
                    pe.wait_ge(xhi_ready.sem, xhi_ready.at(b, 1))
                    pe.wait_ge(xlo_ready.sem, xlo_ready.at(b, 1))
                for half, k in enumerate(both_banks("expert", b, f)):
                    e = EF * q + 2 * half
                    pe.wait_ge(k.drained, k.free(("expert", b, f)))
                    for c in range(C):
                        for i, src in enumerate((xhi, xlo)):
                            last = mm(k.tensor[:, :], src[:, c * S + t * P:c * S + (t + 1) * P],
                                      wE[:, (c * E + e) * D:(c * E + e + 2) * D], c == 0 and i == 0, c == C - 1 and i == 1)
                    last.then_inc(k.filled, 1)

            steps = {f.__name__: f for f in (
                fold_q, fold_k, fold_o, turn_w, adjacency, adjacency_turn, ffn_in, ffn_up, hidden_turn, ffn_down,
                keys_turn, x_turn, project_first, project, to_keys, scores, attn_turn, context, att_out, moe_turn, logits, expert)}
            for name, *args in order:
                steps[name](*args)

        @block.scalar
        def _(act):
            def drain(bank, key, dst, src):
                act.wait_ge(bank.filled, bank.done(key))
                nc.scalar.copy(dst, src).then_inc(bank.drained, 1)

            def fold_q(n):
                w = 2 * DQ
                if n >= 2:
                    act.wait_ge(wA_ready.sem, n - 1)
                for c, k in enumerate(both_banks("fold_q", n)):
                    act.wait_ge(k.filled, k.done(("fold_q", n)))
                    nc.scalar.copy(wA_full[n % 2][:, c * w:(c + 1) * w], k.tensor[:, 0:w]).then_inc(wA_copy.sem, 1)
                    nc.scalar.copy(v3(wA_hi[:, :], C)[:, c, n * w:(n + 1) * w], k.tensor[:, 0:w]).then_inc(k.drained, 1)

            def fold_k(n):
                j, half = divmod(n, 2)
                k = bank_of("fold_k", n)
                act.wait_ge(k.filled, k.done(("fold_k", n)))
                src = k.tensor[:, :].rearrange("p (a g d) -> p g a d", a=4, g=2)
                dst = wM[:, :].rearrange("p (g a j m) -> p g a j m", g=2, a=PAIRS, j=J)[:, :, 4 * half:4 * half + 4, j, :]
                for lo, hi, col in {0: ((0, P, 0),), 1: ((0, 64, 0), (64, P, DC)), 2: ((0, P, DC),)}[j]:
                    for g in range(2):
                        last = nc.scalar.copy(dst[lo:hi, g, :, col:col + DC], src[lo:hi, g])
                last.then_inc(k.drained, 1)

            def fold_o(n):
                k = bank_of("fold_o", n)
                drain(k, ("fold_o", n), wF[:, n * 512:(n + 1) * 512], k.tensor[:, 0:512])

            def turn_w(m, n):
                k = bank_of("turn_w", m, n)
                drain(k, ("turn_w", m, n), (wG, wU, wD)[m][:, n * 512:(n + 1) * 512], k.tensor[:, :])

            def norm(b, i, dst, src, ready):
                _, _, r, nb, a1, b1 = ln_small(i)
                scale, bias = (a1, b1) if i == 0 else (r, nb)
                act.wait_ge(ln_ready[i].sem, ln_ready[i].at(b, ln_ready[i].per_batch))
                for t in range(T):
                    nc.scalar.activation(dst[:, t * D:(t + 1) * D], src[:, t * D:(t + 1) * D], ACT.Identity,
                                         bias=bias[:, t:t + 1], scale=scale[:, t:t + 1]).then_inc(ready.sem, 1)

            def adjacency(b):
                drain(GA, ("adjacency", b), qk0[:, :], GA.tensor[0:DC, :])

            def adjacency_tanh(b):
                act.wait_ge(UA.drained, UA.done(("adjacency", b)))
                nc.scalar.activation(th[:, :], sim[:, :], ACT.Tanh, scale=1.0 / 32).then_inc(th_ready.sem, 1)

            def ffn_in(b):
                drain(UA, ("ffn_in", b), xqT, UA.tensor[:, :])

            def ffn_up(b, u):
                act.wait_ge(GA.filled, GA.done(("ffn_up", b, u)))
                act.wait_ge(UA.drained, UA.free(("ffn_up", b, u)))
                nc.scalar.activation(sg[:, :], GA.tensor[:, :], ACT.Tanh, scale=0.5).then_inc(thg_ready.sem, 1)

            def hidden_turn(b, t):
                drain(GA, ("hidden_turn", b, t), hqT[:, 0:512], GA.tensor[:, :])
                drain(UA, ("hidden_turn", b, t), hqT[:, 512:1024], UA.tensor[:, :])

            def keys_turn(b):
                act.wait_ge(TP.filled, TP.done(("keys_turn", b)))
                nc.scalar.copy(key_hi, TP.tensor[:, 0:S]).then_inc(key_hi_ready.sem, 1)

            def x_turn(b):
                act.wait_ge(TP.filled, TP.done(("x_turn", b)))
                nc.scalar.copy(xT_hi, TP.tensor[:, :]).then_inc(xT_hi_ready.sem, 1)

            def to_keys(b, p):
                act.wait_ge(QC.filled, QC.done(("to_keys", b, p)))
                for hh in range(2):
                    r = slice(hh * DC, (hh + 1) * DC)
                    nc.scalar.copy(qk[r, hh * S:(hh + 1) * S], QC.tensor[r, 0:S]).then_inc(qk_hi_ready.sem, 1)

            def attn_turn(b, p, hh):
                k = bank_of("attn_turn", b, p, hh)
                drain(k, ("attn_turn", b, p, hh), attT[:, hh * 512:(hh + 1) * 512], k.tensor[:, :])

            def softmax(b, p):
                for k in range(4):
                    s = (S0, S1)[k // 2]
                    if k % 2 == 0:
                        act.wait_ge(nmax_ready.sem, nmax_ready.at(b, 2 * p + k // 2 + 1))
                    o = 4 * (p % 2) + k
                    nc.scalar.activation(attn[p % 2][:, k * S:(k + 1) * S], s.tensor[:, (k % 2) * S:(k % 2 + 1) * S], ACT.Exp,
                                         bias=nmax[:, o:o + 1], accum_out=ssum[:, o:o + 1])\
                        .then_inc(exp_done.sem if k % 2 == 0 else s.drained, 1)

            def context(b, p):
                if b >= 1:
                    act.wait_ge(QC.filled, QC.done(("att_out", b - 1)))
                drain(QB, ("context", b, p), cT[:, p * S:(p + 1) * S], QB.tensor[:, 0:S])

            def moe_turn(b):
                if b == 0:
                    act.wait_ge(mask_used.sem, NEC)
                drain(TP, ("moe_turn", b), x4T, TP.tensor[:, :])
                act.wait_ge(TP.drained, TP.done(("moe_turn", b)))
                nc.scalar.copy(xhi[:, :], x4T).then_inc(xhi_ready.sem, 1)

            def route_exp(b):
                act.wait_ge(rt_step.sem, rt_step.at(b, 2))
                nc.scalar.activation(ex, df, ACT.Exp).then_inc(ex_done.sem, 1)

            def expert(b, m):
                key = ("expert", b, T * m)
                if m == 0:
                    act.wait_ge(rt_step.sem, rt_step.at(b, 7))
                    if b >= 1:
                        act.wait_ge(stored.sem, stored.at(b, 0))
                for half, k in enumerate(both_banks(*key)):
                    n = 2 * m + half
                    act.wait_ge(k.filled, k.done(key))
                    if n > 0 and summed.at(b, max(n - 2, 0)) > 0:
                        act.wait_ge(summed.sem, summed.at(b, max(n - 2, 0)))
                    for i in range(2):
                        e = EF * m + 2 * half + i
                        dst = acc[:, 0, i] if n == 0 else scaled[half][:, i * D:(i + 1) * D]
                        ins = nc.scalar.activation(dst, k.tensor[:, i * D:(i + 1) * D], ACT.Copy, scale=selw[:, 0, e:e + 1])
                    ins.then_inc(k.drained, 1)

            def moe_norm(b):
                act.wait_ge(QC.drained, QC.done(("att_out", b)))
                norm(b, 3, xnat, x3, xn4_ready)

            act.wait_ge(ld_adj.sem, 64)
            nc.scalar.activation(gam[:, 1:2], gam[:, 0:1], ACT.Tanh, scale=0.5).then_inc(gam_t.sem, 1)
            adjacency(0)
            adjacency_tanh(0)
            for n in range(H // 2):
                fold_q(n)
            norm(0, 0, y2, xb, y2_ready)
            act.wait_ge(m_zero.sem, 2)
            for n in range(2 * J):
                fold_k(n)
            for n in range(4):
                fold_o(n)
            for n in range(4):
                turn_w(0, n)
            norm(0, 1, xn, x1, xn_ready)
            for n in range(4):
                turn_w(1, n)
            ffn_in(0)
            for u in range(4):
                ffn_up(0, u)
            for n in range(4):
                turn_w(2, n)
            for t in range(T):
                hidden_turn(0, t)
            for b in range(B):
                more = b + 1 < B
                keys_turn(b)
                norm(b, 2, xnat, x2[b % 2], xn3_ready)
                if b >= 2:
                    expert(b - 2, FILLS // T - 1)
                x_turn(b)
                if more:
                    adjacency(b + 1)
                to_keys(b, 0)
                if more:
                    adjacency_tanh(b + 1)
                    norm(b + 1, 0, y2, xb, y2_ready)
                experts = experts_beside(b)

                def experts_of(fills):
                    for f in fills:
                        if f % T == 0:
                            expert(b - 1, f // T)
                beside = {"ffn_in": ffn_in, "ffn_up": ffn_up, "hidden_turn": hidden_turn}
                for p in range(PAIRS):
                    first, second = BESIDE[min(b, 1)][p] if more else ([], [])
                    if p >= 1:
                        context(b, p - 1)
                    softmax(b, p)
                    if p == 0 and b >= 1:
                        moe_norm(b - 1)
                    if p + 1 < PAIRS:
                        to_keys(b, p + 1)
                    if p == NORM_STEP[min(b, 1)] and more:
                        norm(b + 1, 1, xn, x1, xn_ready)
                    if p == 0 and b >= 1:
                        moe_turn(b - 1)
                    experts_of(experts[p][0])
                    for name, *args in first:
                        if name in beside:
                            beside[name](b + 1, *args)
                    experts_of(experts[p][1])
                    attn_turn(b, p, 0)
                    experts_of(experts[p][2])
                    for name, *args in second:
                        if name in beside:
                            beside[name](b + 1, *args)
                    experts_of(experts[p][3])
                    attn_turn(b, p, 1)
                    if p == 0 and b >= 1:
                        route_exp(b - 1)
                context(b, PAIRS - 1)
            expert(B - 2, FILLS // T - 1)
            moe_norm(B - 1)
            moe_turn(B - 1)
            route_exp(B - 1)
            for m in range(FILLS // T):
                expert(B - 1, m)

        @block.vector
        def _(dve):
            def quantise(step, q0, free, f0, src, dst, mag, scale, blocks, part=None):
                def blk(ap):
                    return v3(ap, blocks)
                if part != 1:
                    nc.vector.tensor_reduce(amax[:, 0:blocks], blk(src), AX_X, ALU.max,
                                            apply_absolute_value=True).then_inc(step.sem, 1)
                    dve.wait_ge(step.sem, q0 + 1)
                    if f0 > 0:
                        dve.wait_ge(free.sem, f0)
                    nc.vector.tensor_scalar(scale, amax[:, 0:blocks], 1.0 / FP8_MAX, 1e-30,
                                            ALU.mult, ALU.max).then_inc(step.sem, 1)
                    dve.wait_ge(step.sem, q0 + 2)
                    nc.vector.reciprocal(qrs[:, 0:blocks], scale).then_inc(step.sem, 1)
                    dve.wait_ge(step.sem, q0 + 3)
                    nc.vector.tensor_tensor(blk(dst), blk(src), qrs[:, 0:blocks].unsqueeze(2).to_broadcast([P, blocks, BLK]),
                                            ALU.mult).then_inc(step.sem, 1)
                if part != 0:
                    dve.wait_ge(step.sem, q0 + 4)
                    nc.vector.tensor_scalar(mag.bitcast(U32), dst.bitcast(U32), EXP_BITS, None,
                                            ALU.bitwise_and).then_inc(step.sem, 1)
                    dve.wait_ge(step.sem, q0 + 5)
                    nc.vector.tensor_scalar(mag, mag, MIN_NORMAL, ROUND4, ALU.max, ALU.mult).then_inc(step.sem, 1)
                    dve.wait_ge(step.sem, q0 + 6)
                    nc.vector.tensor_tensor(dst, dst, mag, ALU.add).then_inc(step.sem, 1)

            def round_off(b, n, dst, mag):
                dve.wait_ge(q_step.sem, q_step.at(b, 8 * n + 7))
                nc.vector.tensor_tensor(dst, dst, mag, ALU.subtract).then_inc(q_step.sem, 1)

            def quantise_w(m):
                if m == 2:
                    dve.wait_ge(QC.filled, QC.done(("fold_k", 2 * J - 1)))
                quantise(w_step, w0[m], w_ready, m - 1, nat[m], nat[m], wmag[m], wscale[m % 2], 64)
                if m == 1:
                    dve.wait_ge(w_step.sem, w0[m] + 7)
                    nc.vector.tensor_tensor(nat[m], nat[m], wmag[m], ALU.subtract).then_inc(w_step.sem, 1)

            def quantise_in(b):
                quantise(q_step, q_step.at(b, 0), hq_ready, hq_ready.at(b, 0), xn, qy[:, 0:512], qm[:, 0:512], qsc[:, 0:16], 16)
                round_off(b, 0, qy[:, 0:512], qm[:, 0:512])

            def quantise_hidden(b, t, part=None):
                n = 1 + t
                quantise(q_step, q_step.at(b, 8 * n), hq_ready, hq_ready.at(b, n), hid, qy, qm, qsc[:, 0:32], 32, part)
                if part != 0:
                    round_off(b, n, qy, qm)

            def stats(b, i, src):
                st, mv = ln_small(i)[:2]
                for t in range(T):
                    nc.vector.bn_stats(st[:, t, :], src[:, t * D:(t + 1) * D]).then_inc(ln_stats[i].sem, 1)
                for t in range(T):
                    dve.wait_ge(ln_stats[i].sem, ln_stats[i].at(b, t + 1))
                    nc.vector.bn_aggr(mv[:, t, :], st[:, t, :]).then_inc(ln_mv[i].sem, 1)

            def adjacency(b):
                dve.wait_ge(UA.filled, UA.done(("adjacency", b)))
                nc.vector.tensor_copy(sim[:, :], UA.tensor[:, :]).then_inc(UA.drained, 1)
                dve.wait_ge(ld_x.sem, ld_x.at(b, 16))
                stats(b, 0, xb)

            topk = [(r, what, t) for r in range(ROUNDS) for what in (["max", "strike"] if r < ROUNDS - 1 else ["max"])
                    for t in range(T)]

            def top_rounds(b, eighth):
                n0, n1 = (len(topk) * q // 8 for q in (eighth, eighth + 1))
                for n in range(n0, n1):
                    r, what, t = topk[n]
                    cur = (sim if r == 0 else wk)[:, t * S:(t + 1) * S]
                    best = top[:, t * 8:(t + 1) * 8]
                    if n < T:
                        dve.wait_ge(UA.drained, UA.done(("adjacency", b)))
                    else:
                        dve.wait_ge(topk_step.sem, topk_step.at(b, n - T + 1))
                    if what == "max":
                        nc.vector.max(best, cur).then_inc(topk_step.sem, 1)
                    else:
                        nc.vector.match_replace(wk[:, t * S:(t + 1) * S], best, cur, -3.0e38).then_inc(topk_step.sem, 1)

            def masked(b):
                dve.wait_ge(th1_ready.sem, th1_ready.at(b, 1))
                for t in range(T):
                    thr = top[:, t * 8 + (TOPK - 1) % 8:t * 8 + (TOPK - 1) % 8 + 1]
                    dve.wait_ge(topk_step.sem, topk_step.at(b, len(topk) - T + 1 + t))
                    nc.vector.scalar_tensor_tensor(am[:, t * S:(t + 1) * S], sim[:, t * S:(t + 1) * S], thr,
                                                   th[:, t * S:(t + 1) * S], ALU.is_ge, ALU.mult).then_inc(am_ready.sem, 1)

            def adjacency_out(b):
                key = ("adjacency_turn", b)
                dve.wait_ge(am_ready.sem, am_ready.at(b, T))
                dve.wait_ge(GA.filled, GA.done(key))
                nc.vector.tensor_tensor(am[:, :], am[:, :], GA.tensor[:, :], ALU.add).then_inc(GA.drained, 1)
                dve.wait_ge(GA.drained, GA.done(key))
                dve.wait_ge(y2_ready.sem, y2_ready.at(b, T))
                dve.wait_ge(gam_ready.sem, 2)
                nc.vector.scalar_tensor_tensor(x1[:, :], am[:, :], gam[:, 3:4], y2[:, :], ALU.mult, ALU.add).then_inc(x1_ready.sem, 1)
                dve.wait_ge(x1_ready.sem, x1_ready.at(b, 1))
                stats(b, 1, x1)

            def ffn_in(b):
                dve.wait_ge(xn_ready.sem, xn_ready.at(b, T))
                if b == 0:
                    dve.wait_ge(w_ready.sem, 1)
                quantise_in(b)

            def ffn_up(b, u):
                key = ("ffn_up", b, u)
                t, half = divmod(u, 2)
                dve.wait_ge(thg_ready.sem, thg_ready.at(b, u + 1))
                nc.vector.scalar_tensor_tensor(sg[:, :], sg[:, :], 1.0, GA.tensor[:, :], ALU.add, ALU.mult).then_inc(GA.drained, 1)
                dve.wait_ge(GA.drained, GA.done(key))
                dve.wait_ge(UA.filled, UA.done(key))
                nc.vector.scalar_tensor_tensor(hid[:, half * 512:(half + 1) * 512], sg[:, :], 0.5, UA.tensor[:, :],
                                               ALU.mult, ALU.mult).then_inc(UA.drained, 1)
                if half == 1:
                    dve.wait_ge(UA.drained, UA.done(key))
                    if b == 0:
                        quantise_hidden(b, t, 0)

            def ffn_down(b, t):
                dve.wait_ge(GA.filled, GA.done(("ffn_down", b, t)))
                if b >= 2:
                    dve.wait_ge(QC.drained, QC.done(("att_out", b - 2)))
                nc.vector.tensor_tensor(x2[b % 2][:, t * D:(t + 1) * D], x1[:, t * D:(t + 1) * D], GA.tensor[:, 0:D],
                                        ALU.add).then_inc(GA.drained, 1)
                if t == T - 1:
                    dve.wait_ge(GA.drained, GA.done(("ffn_down", b, t)))
                    stats(b, 2, x2[b % 2])

            def low(dst, src, hi):
                return nc.vector.tensor_tensor(dst, src, hi, ALU.subtract)

            def keys_turn(b):
                dve.wait_ge(key_hi_ready.sem, key_hi_ready.at(b, 1))
                low(key_lo, TP.tensor[:, 0:S], key_hi).then_inc(TP.drained, 1)

            def x_turn(b):
                dve.wait_ge(xT_hi_ready.sem, xT_hi_ready.at(b, 1))
                low(xT_lo, TP.tensor[:, :], xT_hi).then_inc(TP.drained, 1)

            def to_keys(b, p):
                dve.wait_ge(qk_hi_ready.sem, qk_hi_ready.at(b, 2 * (p + 1)))
                for hh in range(2):
                    r, other = slice(hh * DC, (hh + 1) * DC), slice((1 - hh) * DC, (2 - hh) * DC)
                    low(qk[other, hh * S:(hh + 1) * S], QC.tensor[r, 0:S], qk[r, hh * S:(hh + 1) * S])\
                        .then_inc(qk_lo_ready.sem if hh == 0 else QC.drained, 1)

            def rotate(b, p):
                key = ("project", b, p)
                if p == 0:
                    dve.wait_ge(ld_tab.sem, 112)
                dve.wait_ge(QB.filled, QB.done(key))
                if p >= 1:
                    dve.wait_ge(QC.filled, QC.done(("to_keys", b, p - 1)))
                for g, tab in enumerate((cosq, sinq)):
                    nc.vector.tensor_tensor(qcs[:, g * J * S:(g + 1) * J * S], QB.tensor[:, 0:J * S], tab[:, :],
                                            ALU.mult).then_inc(qc_ready.sem if g == 0 else QB.drained, 1)

            def row_max(b, p):
                for hh, k in enumerate((S0, S1)):
                    o = 4 * (p % 2) + 2 * hh
                    dve.wait_ge(k.filled, k.done(("scores", b, p)))
                    nc.vector.tensor_reduce(nmax[:, o:o + 2], v3(k.tensor[:, :], T), AX_X, ALU.max,
                                            negate=True).then_inc(nmax_ready.sem, 1)

            def row_sum(b, p):
                o = 4 * (p % 2)
                dve.wait_ge(S0.drained, S0.done(("scores", b, p)))
                dve.wait_ge(S1.drained, S1.done(("scores", b, p)))
                nc.vector.reciprocal(rsum[:, o:o + 4], ssum[:, o:o + 4]).then_inc(rsum_ready.sem, 1)

            def att_out(b):
                dve.wait_ge(QC.filled, QC.done(("att_out", b)))
                dve.wait_ge(o_ready.sem, o_ready.at(b, 0))
                nc.vector.tensor_tensor(x3, x2[b % 2][:, :], QC.tensor[:, :], ALU.add).then_inc(QC.drained, 1)
                dve.wait_ge(QC.drained, QC.done(("att_out", b)))
                stats(b, 3, x3)

            def routing(b):
                mx, es, wt, rm = (small[:, 96 + 2 * i:98 + 2 * i] for i in range(4))
                key = ("logits", b)

                def wide(s):
                    return s.unsqueeze(2).to_broadcast([P, T, E])
                dve.wait_ge(xhi_ready.sem, xhi_ready.at(b, 1))
                nc.vector.tensor_tensor(xlo[:, :], x4T, xhi[:, :], ALU.subtract).then_inc(xlo_ready.sem, 1)
                dve.wait_ge(QC.filled, QC.done(key))
                lg = v3(QC.tensor[:, 0:T * E], T)
                nc.vector.tensor_reduce(mx, lg, AX_X, ALU.max).then_inc(rt_step.sem, 1)
                dve.wait_ge(rt_step.sem, rt_step.at(b, 1))
                nc.vector.tensor_tensor(v3(df, T), lg, wide(mx), ALU.subtract).then_inc(rt_step.sem, 1)
                dve.wait_ge(rt_step.sem, rt_step.at(b, 2))
                nc.vector.scalar_tensor_tensor(rk, df, 0.0, rnk[:, :], ALU.is_equal, ALU.mult).then_inc(rt_step.sem, 1)
                dve.wait_ge(rt_step.sem, rt_step.at(b, 3))
                nc.vector.tensor_reduce(rm, v3(rk, T), AX_X, ALU.max).then_inc(QC.drained, 1)
                dve.wait_ge(QC.drained, QC.done(key))
                nc.vector.tensor_tensor(v3(rk, T), v3(rk, T), wide(rm), ALU.is_equal).then_inc(rt_step.sem, 1)
                dve.wait_ge(ex_done.sem, ex_done.at(b, 1))
                nc.vector.tensor_reduce(es, v3(ex, T), AX_X, ALU.add).then_inc(rt_step.sem, 1)
                dve.wait_ge(rt_step.sem, rt_step.at(b, 5))
                nc.vector.reciprocal(wt, es).then_inc(rt_step.sem, 1)
                dve.wait_ge(rt_step.sem, rt_step.at(b, 6))
                if b >= 1:
                    dve.wait_ge(summed.sem, summed.at(b, 0))
                nc.vector.tensor_tensor(selw, v3(rk, T), wide(wt), ALU.mult).then_inc(rt_step.sem, 1)

            def expert(b, m):
                t = T - 1
                key = ("expert", b, T * m + t)
                if m == 0:
                    dve.wait_ge(rt_step.sem, rt_step.at(b, 7))
                    dve.wait_ge(stored.sem, stored.at(b, 0))
                banks = both_banks(*key)
                for i in range(EF):
                    e, chain, k = EF * m + i, i % 2, banks[i // 2]
                    src, w = k.tensor[:, chain * D:(chain + 1) * D], selw[:, t, e:e + 1]
                    if chain == 0:
                        dve.wait_ge(k.filled, k.done(key))
                    if i == 2:
                        dve.wait_ge(acc_step.sem, acc_step.at(b, 2 * m + 1))
                    elif i == 3:
                        dve.wait_ge(banks[0].drained, banks[0].done(key))
                    elif m > 0 and i == 0:
                        dve.wait_ge(acc_step.sem, acc_step.at(b, 2 * m))
                    elif m > 0:
                        before = ("expert", b, T * (m - 1) + t)
                        dve.wait_ge(banks[1].drained, banks[1].done(before))
                    if m == 0 and i < 2:
                        ins = nc.vector.tensor_scalar(acc[:, t, chain], src, w, None, ALU.mult)
                    else:
                        ins = nc.vector.scalar_tensor_tensor(acc[:, t, chain], src, w, acc[:, t, chain], ALU.mult, ALU.add)
                    ins.then_inc(acc_step.sem if chain == 0 else k.drained, 1)

            dve.wait_ge(gam_t.sem, 1)
            nc.vector.tensor_scalar(gam[:, 2:3], gam[:, 1:2], -0.5, 0.5, ALU.mult, ALU.add).then_inc(gam_ready.sem, 1)
            nc.vector.tensor_scalar(gam[:, 3:4], gam[:, 1:2], 0.125, 0.125, ALU.mult, ALU.add).then_inc(gam_ready.sem, 1)
            adjacency(0)
            for eighth in range(8):
                top_rounds(0, eighth)
            masked(0)
            for m in range(3):
                dve.wait_ge(ld_nat[m].sem, 16)
                quantise_w(m)
                if m == 0:
                    adjacency_out(0)
                if m == 1:
                    ffn_in(0)
            for u in range(4):
                ffn_up(0, u)
                if u >= 2:
                    quantise_hidden(0, u - 2, 1)
            for t in range(T):
                ffn_down(0, t)
            dve.wait_ge(ld_moe.sem, 16)
            nc.vector.tensor_scalar(tern[:, :], tern[:, :], 2.0, ROUND_INT, ALU.mult, ALU.add).then_inc(tern_step.sem, 1)
            dve.wait_ge(tern_step.sem, 1)
            nc.vector.tensor_scalar(tern[:, :], tern[:, :], ROUND_INT, 1.0, ALU.subtract, ALU.min).then_inc(tern_step.sem, 1)
            dve.wait_ge(tern_step.sem, 2)
            nc.vector.tensor_scalar(tern[:, :], tern[:, :], -1.0, None, ALU.max).then_inc(tern_step.sem, 1)
            for b in range(B):
                more = b + 1 < B
                keys_turn(b)
                x_turn(b)
                if b >= 2:
                    expert(b - 2, FILLS // T - 1)
                rotate(b, 0)
                if more:
                    adjacency(b + 1)
                to_keys(b, 0)
                rotate(b, 1)
                if b >= 1:
                    att_out(b - 1)
                experts = experts_beside(b)

                def experts_of(fills):
                    for f in fills:
                        if f % T == 1:
                            expert(b - 1, f // T)
                steps = {"top": top_rounds, "masked": masked, "adjacency_out": adjacency_out, "ffn_in": ffn_in,
                         "ffn_up": ffn_up, "round": quantise_hidden, "ffn_down": ffn_down}
                for p in range(PAIRS):
                    def first_stream(gap):
                        for name, *args in VECTOR_BESIDE[min(b, 1)][p][gap] if more else []:
                            steps[name](b + 1, *args)
                    row_max(b, p)
                    first_stream(0)
                    row_sum(b, p)
                    first_stream(1)
                    if p + 1 < PAIRS:
                        to_keys(b, p + 1)
                    experts_of(experts[p][0])
                    if p + 2 < PAIRS:
                        rotate(b, p + 2)
                    if p == 0 and b >= 1:
                        routing(b - 1)
                    first_stream(2)
                    experts_of(experts[p][1] + experts[p][2])
                    first_stream(3)
                    experts_of(experts[p][3])
                    first_stream(4)
            expert(B - 2, FILLS // T - 1)
            att_out(B - 1)
            routing(B - 1)
            for m in range(FILLS // T):
                expert(B - 1, m)
            o, last = acc[:, 1, 0], ("expert", B - 1, FILLS - 1)
            k = both_banks(*last)[1]
            dve.wait_ge(k.drained, k.done(last))
            dve.wait_ge(acc_step.sem, acc_step.at(B - 1, acc_step.per_batch))
            nc.vector.tensor_tensor(o, o, acc[:, 1, 1], ALU.add).then_inc(last_step.sem, 1)
            dve.wait_ge(last_step.sem, 1)
            nc.vector.tensor_tensor(o, o, scl[:, :], ALU.mult).then_inc(last_step.sem, 1)
            dve.wait_ge(last_step.sem, 2)
            nc.vector.tensor_tensor(o, o, x3[:, D:2 * D], ALU.add).then_inc(last_step.sem, 1)

        @block.gpsimd
        def _(pool):
            def ts(dst, src, s1, s2, o1, o2=None):
                if o2 is None:
                    return nc.gpsimd.tensor_scalar(dst, src, s1, None, o1)
                return nc.gpsimd.tensor_scalar(dst, src, s1, s2, o1, o2)

            def dequant(ready, src, dst, scale, blocks):
                nc.gpsimd.tensor_tensor(v3(dst, blocks), v3(src, blocks),
                                        scale.unsqueeze(2).to_broadcast([P, blocks, BLK]), ALU.mult).then_inc(ready.sem, 1)

            def dequant_w(m):
                pool.wait_ge(w_step.sem, w0[m + 1])
                if m != 1:
                    nc.gpsimd.tensor_tensor(nat[m], nat[m], wmag[m], ALU.subtract).then_inc(w_rounded.sem, 1)
                    pool.wait_ge(w_rounded.sem, 1 + m // 2)
                dequant(w_ready, nat[m], nat[m], wscale[m % 2], 64)

            def rstd(b, i):
                _, mv, r, nb, a1, b1 = ln_small(i)
                step, ready = ln_step[i], ln_ready[i]
                pool.wait_ge(ln_mv[i].sem, ln_mv[i].at(b, T))
                ts(r, mv[:, :, 1], EPS, None, ALU.add).then_inc(step.sem, 1)
                ts(nb, mv[:, :, 0], -1.0, None, ALU.mult).then_inc(step.sem, 1)
                pool.wait_ge(step.sem, step.at(b, 2))
                nc.gpsimd.tensor_tensor(r, r, halfneg[:, :], ALU.pow).then_inc(step.sem, 1)
                pool.wait_ge(step.sem, step.at(b, 3))
                last = nc.gpsimd.tensor_tensor(nb, nb, r, ALU.mult)
                if i == 0:
                    last.then_inc(step.sem, 1)
                    pool.wait_ge(step.sem, step.at(b, 4))
                    ts(a1, r, gam[:, 2:3], 1.0, ALU.mult, ALU.add).then_inc(ready.sem, 1)
                    ts(b1, nb, gam[:, 2:3], None, ALU.mult).then_inc(ready.sem, 1)
                else:
                    last.then_inc(ready.sem, 1)

            def adjacency(b):
                pool.wait_ge(th_ready.sem, th_ready.at(b, 1))
                ts(th[:, :], th[:, :], 1.0, None, ALU.add).then_inc(th1_ready.sem, 1)
                rstd(b, 0)

            def ffn_in(b):
                if b >= 1:
                    pool.wait_ge(UA.filled, UA.done(("hidden_turn", b - 1, 1)))
                pool.wait_ge(q_step.sem, q_step.at(b, 8))
                dequant(hq_ready, qy[:, 0:512], hq[:, 0:512], qsc[:, 0:16], 16)

            def ffn_up(b, t):
                pool.wait_ge(UA.filled, UA.done(("ffn_in", b) if t == 0 else ("hidden_turn", b, 0)))
                pool.wait_ge(q_step.sem, q_step.at(b, 8 * (2 + t)))
                dequant(hq_ready, qy, hq, qsc[:, 0:32], 32)

            def keys(b):
                pool.wait_ge(ld_cxn.sem, ld_cxn.at(b, 16))
                pool.wait_ge(ld_tab.sem, 112)
                if b == 0:
                    pool.wait_ge(UA.filled, UA.done(("turn_w", 2, 3)))
                hw = DC // 2
                a, r = v3(kvtmp[:, 0:T * DC], T), v3(kvtmp[:, T * DC:2 * T * DC], T)
                c3, cs, sn = v3(cxn, T), v3(cosk[:, :], T), v3(sink[:, :], T)
                nc.gpsimd.tensor_tensor(a, c3, cs, ALU.mult).then_inc(kv_step.sem, 1)
                nc.gpsimd.tensor_tensor(r[:, :, 0:hw], c3[:, :, hw:DC], sn[:, :, 0:hw], ALU.mult).then_inc(kv_step.sem, 1)
                nc.gpsimd.tensor_tensor(r[:, :, hw:DC], c3[:, :, 0:hw], sn[:, :, hw:DC], ALU.mult).then_inc(kv_step.sem, 1)
                pool.wait_ge(kv_step.sem, kv_step.at(b, 3))
                if b >= 2:
                    pool.wait_ge(QB.filled, QB.done(("context", b - 2, PAIRS - 1)))
                k4 = kvns[b % 2].rearrange("p (t u d) -> p t u d", t=T, u=2)
                nc.gpsimd.tensor_tensor(k4[:, :, 0, :], a, r, ALU.add).then_inc(kv_step.sem, 1)
                nc.gpsimd.tensor_tensor(k4[:, :, 1, :], a, r, ALU.add).then_inc(kv_ready.sem, 1)

            def attention(b, p):
                o = 4 * (p % 2)
                pool.wait_ge(rsum_ready.sem, rsum_ready.at(b, p + 1))
                for hh in range(2):
                    a = v3(attn[p % 2], 4)[:, 2 * hh:2 * hh + 2]
                    nc.gpsimd.tensor_tensor(a, a, rsum[:, o + 2 * hh:o + 2 * hh + 2].unsqueeze(2).to_broadcast([P, 2, S]),
                                            ALU.mult).then_inc(attn_ready.sem, 1)

            def result(b):
                tiles = T if b < B - 1 else 1
                o, o3 = acc[:, 0:tiles, 0], v3(x3, T)[:, 0:tiles]
                last = ("expert", b, FILLS - 1 if b < B - 1 else FILLS - T)
                k = both_banks(*last)[1]
                pool.wait_ge(k.drained, k.done(last))
                pool.wait_ge(summed.sem, summed.at(b, FILLS - 1))
                nc.gpsimd.tensor_tensor(o, o, acc[:, 0:tiles, 1], ALU.add).then_inc(osum.sem, 1)
                pool.wait_ge(osum.sem, osum.at(b, 1))
                nc.gpsimd.tensor_tensor(o, o, scl[:, :].unsqueeze(1).to_broadcast([P, tiles, D]), ALU.mult).then_inc(o_step.sem, 1)
                pool.wait_ge(o_step.sem, o_step.at(b, 1))
                nc.gpsimd.tensor_tensor(o, o, o3, ALU.add).then_inc(o_ready.sem, 1)
                if b < B - 1:
                    pool.wait_ge(o_ready.sem, o_ready.at(b, 1))
                    pool.dma_start(out[b].rearrange("(t p) d -> p t d", p=P), o).then_inc(stored.sem, 16)

            def expert(b, m):
                key = ("expert", b, T * m)
                for half, k in enumerate(both_banks(*key)):
                    n = 2 * m + half
                    pool.wait_ge(k.drained, k.done(key))
                    if n > 1:
                        pool.wait_ge(summed.sem, summed.at(b, n - 1))
                    if n > 0:
                        nc.gpsimd.tensor_tensor(acc_rows[:, 0:2 * D], acc_rows[:, 0:2 * D], scaled[half], ALU.add)\
                            .then_inc(summed.sem, 1)

            def experts_of(b, fills):
                for f in fills:
                    if f % T == 0:
                        expert(b - 1, f // T)

            def expert_weights(n):
                we = wE[:, :].rearrange("p (c e o) -> p c e o", c=C, e=E)
                src = masks[:, (n % 2) * 1024:(n % 2 + 1) * 1024].rearrange("p (c e o) -> p c e o", c=C, e=EC)
                if n == 0:
                    pool.wait_ge(tern_step.sem, 3)
                    pool.wait_ge(S0.filled, S0.done(("fold_o", 3)))
                pool.wait_ge(ld_mask[n % 2].sem, 16 * (n // 2 + 1))
                for c in range(C):
                    last = nc.gpsimd.tensor_tensor(we[:, c, n * EC:(n + 1) * EC, :], src[:, c],
                                                   tern[:, c * D:(c + 1) * D].unsqueeze(1).to_broadcast([P, EC, D]),
                                                   ALU.mult, saturate=False)
                last.then_inc(mask_used.sem, 1)

            acc_rows = masks[:, 0:T * 2 * D]
            nc.gpsimd.memset(halfneg[:, :], -0.5).then_inc(half_ready.sem, 1)
            nc.gpsimd.memset(raw_kr, 0.0).then_inc(kr_zero.sem, 1)
            pool.wait_ge(half_ready.sem, 1)
            pool.wait_ge(gam_ready.sem, 2)
            adjacency(0)
            for n in range(H // 2):
                pool.wait_ge(wA_copy.sem, C * (n + 1))
                for k in both_banks("fold_q", n):
                    pool.wait_ge(k.drained, k.done(("fold_q", n)))
                o = slice(n * 384, (n + 1) * 384)
                nc.gpsimd.tensor_tensor(v3(wA_lo[:, :], C)[:, :, o], v3(wA_full[n % 2], C), v3(wA_hi[:, :], C)[:, :, o],
                                        ALU.subtract).then_inc(wA_ready.sem, 1)
            pool.wait_ge(UA.filled, UA.done(("fold_q", H // 2 - 1)))
            shared = wM[:, :].rearrange("p (g j m) -> p g j m", j=J, m=P)[:, :, 1, :]
            pool.wait_ge(wA_ready.sem, H // 2)
            for lo in range(2):
                if lo == 1:
                    pool.wait_ge(m_zero.sem, 1)
                nc.gpsimd.memset(shared[lo * DC:(lo + 1) * DC, :, (1 - lo) * DC:(2 - lo) * DC], 0.0).then_inc(m_zero.sem, 1)
            pool.wait_ge(m_zero.sem, 2)
            for m in range(2):
                dequant_w(m)
                if m == 0:
                    rstd(0, 1)
            ffn_in(0)
            dequant_w(2)
            for t in range(T):
                ffn_up(0, t)
                if t == 0:
                    keys(0)
            rstd(0, 2)
            steps = {"keys": keys, "rstd": rstd, "ffn_in": ffn_in, "ffn_up": ffn_up,
                     "expert_weights": lambda b, n: expert_weights(n)}
            for b in range(B):
                more = b + 1 < B
                if more:
                    adjacency(b + 1)
                if b >= 1:
                    rstd(b - 1, 3)
                for p in range(PAIRS):
                    attention(b, p)
                    before, after = POOL_BESIDE[min(b, 1)][p] if more else ([], [])
                    for name, *args in before:
                        steps[name](b + 1, *args)
                    for fills in experts_beside(b)[p]:
                        experts_of(b, fills)
                    for name, *args in after:
                        steps[name](b + 1, *args)
                if more:
                    rstd(b + 1, 2)
                if b >= 1:
                    expert(b - 1, FILLS // T - 1)
                    result(b - 1)
            rstd(B - 1, 3)
            for m in range(FILLS // T):
                expert(B - 1, m)
            result(B - 1)


def tables():
    def rope(length, dim):
        inv = (1.0 / 10000.0 ** (np.arange(0, dim, 2, dtype=np.float32) / np.float32(dim))).astype(np.float32)
        f = np.arange(length, dtype=np.float32)[:, None] * inv[None, :]
        return np.repeat(np.sin(f), 2, axis=-1).astype(np.float32), np.repeat(np.cos(f), 2, axis=-1).astype(np.float32)

    sin, cos = rope(S, DQ)
    half = DQ // 2
    sin = np.concatenate([sin[:, half:], -sin[:, :half]], axis=1)
    q = np.arange(J * P) % DQ
    tile = lambda a: np.ascontiguousarray(a[:, q].T.reshape(J, P, S).transpose(1, 0, 2).reshape(P, J * S))
    sin_k, cos_k = rope(S, DC)
    sin_k = np.concatenate([-sin_k[:, :DC // 2], sin_k[:, DC // 2:]], axis=1)
    nat = lambda a: np.ascontiguousarray(a.reshape(T, P, DC).transpose(1, 0, 2).reshape(P, T * DC))
    rank = np.ascontiguousarray(np.broadcast_to((E - np.arange(E, dtype=np.float32)), (P, T, E)).reshape(P, T * E))
    return {"cos_q": tile(cos), "sin_q": tile(sin), "cos_k": nat(cos_k), "sin_k": nat(sin_k),
            "ident": np.eye(P, dtype=np.float32), "rank": rank}


def layout(i):
    def a(name):
        return np.asarray(i[name])
    rows = lambda w: w.reshape(-1, P, w.shape[1]).transpose(1, 0, 2).reshape(P, -1)
    qr = a("L1_xattn_W_qr")
    qr2 = np.stack([qr, np.roll(qr, DQ // 2, axis=1)])
    out = {
        "x": a("x"), "ctx_nat": a("ctx_512"), "ctx_t": a("ctx_512").transpose(0, 2, 1),
        "adj_wq": a("L0_xattn_Wq").T, "adj_wk": a("L0_xattn_Wk").T, "gamma": a("L0_xattn_gamma_raw").reshape(1),
        "gate_w": rows(a("L0_ffn_gate_w")), "up_w": rows(a("L0_ffn_up_w")), "down_w": rows(a("L0_ffn_down_w")),
        "att_wq": rows(a("L1_xattn_Wq")),
        "kc_q": a("L1_xattn_w_kc_q").transpose(1, 0, 2).reshape(HK, H * DQ),
        "kc_kv": a("L1_xattn_w_kc_kv").transpose(1, 0, 2).reshape(HK, H * DC),
        "qr_t": qr2.transpose(0, 3, 1, 2).reshape(2 * R, H * DQ),
        "kr_t": a("L1_xattn_W_kr").transpose(2, 0, 1).reshape(R, H * DC),
        "wo_t": rows(a("L1_xattn_Wo").T),
        "moe_w": rows(a("L1_ffn_weight").T),
        "moe_scale": a("L1_ffn_scale"),
        "moe_masks": a("L1_ffn_expert_masks").reshape(NEC, EC, D, C, P).transpose(0, 4, 3, 1, 2).reshape(NEC, P, C * EC * D),
        "router": rows(a("L1_ffn_router_w").T),
    }
    out.update(tables())
    return {k: np.ascontiguousarray(v) for k, v in out.items()}


_INS = ["x", "ctx_nat", "ctx_t", "adj_wq", "adj_wk", "gamma", "gate_w", "up_w", "down_w", "att_wq", "kc_q", "kc_kv",
        "qr_t", "kr_t", "wo_t", "moe_w", "moe_scale", "moe_masks", "router", "cos_q", "sin_q", "cos_k", "sin_k",
        "ident", "rank"]


def kernel(**inputs):
    import concourse.bacc as _bacc
    from concourse.bass_utils import run_bass_kernel_spmd as _run

    nc = _bacc.Bacc("TRN2", target_bir_lowering=False, num_devices=1)
    laid = layout(inputs)
    arrays, args = {}, []
    for name in _INS:
        arrays[f"in_{name}"] = laid[name]
        args.append(nc.dram_tensor(f"in_{name}", laid[name].shape, mybir.dt.from_np(laid[name].dtype),
                                   kind="ExternalInput").ap())
    out = nc.dram_tensor("out_0", (B, S, D), F32, kind="ExternalOutput").ap()
    build(nc, *args, out)
    r = _run(nc, [arrays], core_ids=[0])
    return r.results[0]["out_0"]
```
